# Optimizing a Trainium2 kernel written in Bass

```python
import numpy as np
import jax
import jax.numpy as jnp

def _softmax(x, axis=-1):
    return jax.nn.softmax(x, axis=axis)

def _gelu(x):
    return jax.nn.gelu(x, approximate=True)

def _silu(x):
    return jax.nn.silu(x)

def _sigmoid(x):
    return jax.nn.sigmoid(x)

def _layernorm(x, axis=-1, eps=1e-05):
    m = jnp.mean(x, axis=axis, keepdims=True)
    v = jnp.var(x, axis=axis, keepdims=True)
    return (x - m) / jnp.sqrt(v + eps)

def _scatter_add(tgt, idx, src, axis=0):
    return tgt.at[idx].add(src)

def _segment_sum(src, seg, n):
    return jax.ops.segment_sum(src, seg, n)
kernel_name = 'mk_gnn_ffn_d4_gnn_r32_0047be'

def setup_inputs(seed: int=0):
    np.random.seed(seed)
    _w = jnp.asarray

    def _rec_inputs():
        import jax
        import jax.numpy as jnp
        _gk = jax.random.key(seed)
        x = -0.0003713 + 1 * jax.random.normal(jax.random.fold_in(_gk, 1), (3125, 256), jnp.float32)
        src = jax.random.randint(jax.random.fold_in(_gk, 2), (50000,), 0, 3125, jnp.int32)
        dst = jax.random.randint(jax.random.fold_in(_gk, 3), (50000,), 0, 3125, jnp.int32)
        _o = jnp.argsort(dst, stable=True)
        src = src[_o]
        dst = dst[_o]
        edge_attr_64 = 0.000279952 + 1.00013 * jax.random.normal(jax.random.fold_in(_gk, 11), (50000, 64), jnp.float32)
        edge_weight = jax.random.uniform(jax.random.fold_in(_gk, 13), (50000,), jnp.float32, 0.0, 0.999998)
        return (x, src, dst, edge_attr_64, edge_weight)
    x, src, dst, edge_attr_64, edge_weight = _rec_inputs()

    def _L0_gnn_setup():
        import jax, jax.numpy as jnp
        import numpy as np
        N, D, H = (50000, 256, 8)
        C = D // H
        E = 50000
        NEG_SLOPE = 0.2
        EPS = 1e-05

        def _gat_block(x, src, dst, W, att_src, att_dst, bias, ln_w, ln_b):
            n = x.shape[0]
            h = (x @ W).reshape(n, H, C)
            a_src = jnp.einsum('nhc,hc->nh', h, att_src)
            a_dst = jnp.einsum('nhc,hc->nh', h, att_dst)
            e = a_src[src] + a_dst[dst]
            e = jnp.where(e > 0, e, NEG_SLOPE * e)
            m = jax.ops.segment_max(e, dst, num_segments=n)
            m = jnp.where(jnp.isfinite(m), m, 0.0)
            ex = jnp.exp(e - m[dst])
            denom = jax.ops.segment_sum(ex, dst, num_segments=n)
            alpha = ex / denom[dst]
            msg = h[src] * alpha[..., None]
            out = jax.ops.segment_sum(msg, dst, num_segments=n).reshape(n, H * C) + bias
            y = out + x
            mu = y.mean(axis=-1, keepdims=True)
            var = y.var(axis=-1, keepdims=True)
            return (y - mu) / jnp.sqrt(var + EPS) * ln_w + ln_b
        key = jax.random.key(seed)
        ks = jax.random.split(key, 8)
        x = jax.random.normal(ks[0], (N, D), dtype=jnp.float32)
        edge_index = jax.random.randint(ks[1], (2, E), 0, N, dtype=jnp.int32)
        scale = 1.0 / np.sqrt(D)
        W = jax.random.normal(ks[2], (D, H * C), dtype=jnp.float32) * scale
        att_src = jax.random.normal(ks[3], (H, C), dtype=jnp.float32) * scale
        att_dst = jax.random.normal(ks[4], (H, C), dtype=jnp.float32) * scale
        bias = jnp.zeros((H * C,), dtype=jnp.float32)
        ln_w = jnp.ones((D,), dtype=jnp.float32)
        ln_b = jnp.zeros((D,), dtype=jnp.float32)
        return {'x': x, 'edge_index': edge_index, 'W': W, 'att_src': att_src, 'att_dst': att_dst, 'bias': bias, 'ln_w': ln_w, 'ln_b': ln_b}
    _L0_gnn_all = _L0_gnn_setup()
    _L0_gnn_in = {k: v for k, v in _L0_gnn_all.items() if k in ('W', 'att_src', 'att_dst', 'bias', 'ln_w', 'ln_b')}
    del _L0_gnn_all

    def _L0_ffn_setup():
        import jax, jax.numpy as jnp
        import numpy as np
        NUM_EXPERTS = 8
        TOP_K = 2
        B, S, D = (8, 256, 256)

        def _moe(tokens, router_w, w1, b1, w2, b2):
            N = tokens.shape[0]
            E = router_w.shape[0]
            logits = tokens.astype(jnp.float32) @ router_w.astype(jnp.float32).T
            probs = jax.nn.softmax(logits, axis=-1)
            rw, re = jax.lax.top_k(probs, TOP_K)
            if TOP_K > 1:
                rw = rw / jnp.maximum(rw.sum(-1, keepdims=True), 1e-12)
            rw = rw.astype(tokens.dtype)
            combine = jnp.zeros((N, E), tokens.dtype).at[jnp.arange(N)[:, None], re].set(rw)
            out = tokens
            for e in range(E):
                h = jax.nn.gelu(tokens @ w1[e] + b1[e], approximate=False)
                y = h @ w2[e] + b2[e]
                out = out + combine[:, e:e + 1] * y
            return out
        key = jax.random.key(seed)
        ks = jax.random.split(key, 4)
        scale = 1.0 / np.sqrt(D).astype(np.float32)
        return {'input_embeddings': jax.random.normal(ks[0], (B, S, D), jnp.float32), 'router_w': jax.random.normal(ks[1], (NUM_EXPERTS, D), jnp.float32) * scale, 'w1': jax.random.normal(ks[2], (NUM_EXPERTS, D, D), jnp.float32) * scale, 'b1': jnp.zeros((NUM_EXPERTS, D), jnp.float32), 'w2': jax.random.normal(ks[3], (NUM_EXPERTS, D, D), jnp.float32) * scale, 'b2': jnp.zeros((NUM_EXPERTS, D), jnp.float32)}
    _L0_ffn_all = _L0_ffn_setup()
    _L0_ffn_in = {k: v for k, v in _L0_ffn_all.items() if k in ('router_w', 'w1', 'b1', 'w2', 'b2')}
    del _L0_ffn_all

    def _L1_gnn_setup():
        import jax, jax.numpy as jnp
        import numpy as np
        N, E, H, ED = (625, 10000, 256, 64)
        key = jax.random.key(seed)
        ks = jax.random.split(key, 12)

        def init_w(k, shape, fan_in):
            return (jax.random.normal(k, shape, jnp.float32) / np.sqrt(fan_in)).astype(jnp.float32)
        h = jax.random.normal(ks[0], (N, H), jnp.float32)
        edge_indices = jax.random.randint(ks[1], (2, E), 0, N, jnp.int32)
        edge_attr = jax.random.normal(ks[2], (E, ED), jnp.float32)
        din = 2 * H + ED
        W1 = init_w(ks[3], (H, din), din)
        b1 = jnp.zeros((H,), jnp.float32)
        W2 = init_w(ks[4], (H, H), H)
        b2 = jnp.zeros((H,), jnp.float32)
        W_ih = init_w(ks[5], (3 * H, H), H)
        b_ih = jnp.zeros((3 * H,), jnp.float32)
        W_hh = init_w(ks[6], (3 * H, H), H)
        b_hh = jnp.zeros((3 * H,), jnp.float32)
        return {'h': h, 'edge_indices': edge_indices, 'edge_attr': edge_attr, 'W1': W1, 'b1': b1, 'W2': W2, 'b2': b2, 'W_ih': W_ih, 'b_ih': b_ih, 'W_hh': W_hh, 'b_hh': b_hh}
    _L1_gnn_all = _L1_gnn_setup()
    _L1_gnn_in = {k: v for k, v in _L1_gnn_all.items() if k in ('W1', 'b1', 'W2', 'b2', 'W_ih', 'b_ih', 'W_hh', 'b_hh')}
    del _L1_gnn_all

    def _L1_ffn_setup():
        import jax, jax.numpy as jnp
        import numpy as np
        B, K, D = (512, 16, 256)
        E = 32
        H = int(D * 0.25)
        key = jax.random.key(seed)
        ks = jax.random.split(key, 7)
        d_rs = D ** (-0.5)
        h_rs = H ** (-0.5)
        x = jax.random.normal(ks[0], (B, K, D), dtype=jnp.float32)
        router_w = jax.random.uniform(ks[1], (E, D), jnp.float32, -d_rs, d_rs)
        router_b = jax.random.uniform(ks[2], (E,), jnp.float32, -d_rs, d_rs)
        W1 = jax.random.uniform(ks[3], (E, D, H), jnp.float32, -h_rs, h_rs)
        b1 = jax.random.uniform(ks[4], (E, H), jnp.float32, -h_rs, h_rs)
        W2 = jax.random.uniform(ks[5], (E, H, D), jnp.float32, -d_rs, d_rs)
        b2 = jax.random.uniform(ks[6], (E, D), jnp.float32, -d_rs, d_rs)
        return {'x': x, 'router_w': router_w, 'router_b': router_b, 'W1': W1, 'b1': b1, 'W2': W2, 'b2': b2}
    _L1_ffn_all = _L1_ffn_setup()
    _L1_ffn_in = {k: v for k, v in _L1_ffn_all.items() if k in ('router_w', 'router_b', 'W1', 'b1', 'W2', 'b2')}
    del _L1_ffn_all

    def _L2_gnn_setup():
        import jax, jax.numpy as jnp
        import numpy as np
        MIN_NORM = 1e-15
        BALL_EPS = 1e-05
        C = 1.0
        N_NODES, N_EDGES, D_IN, D_OUT = (1250, 10000, 256, 256)

        def _sqnorm(x):
            return jnp.sum(x * x, axis=-1, keepdims=True)

        def _norm(x):
            return jnp.maximum(jnp.sqrt(_sqnorm(x)), MIN_NORM)

        def _artanh(x):
            return jnp.arctanh(jnp.clip(x, -1.0 + 1e-07, 1.0 - 1e-07))

        def _lam(x, c):
            return jnp.maximum(2.0 / jnp.maximum(1.0 - c * _sqnorm(x), MIN_NORM), MIN_NORM)

        def mobius_add(x, y, c):
            x2, y2 = (_sqnorm(x), _sqnorm(y))
            xy = jnp.sum(x * y, axis=-1, keepdims=True)
            num = (1.0 + 2.0 * c * xy + c * y2) * x + (1.0 - c * x2) * y
            den = 1.0 + 2.0 * c * xy + c * c * x2 * y2
            return num / jnp.maximum(den, MIN_NORM)

        def expmap0(u, c):
            sc = jnp.sqrt(c)
            un = _norm(u)
            return jnp.tanh(sc * un) * u / (sc * un)

        def logmap0(p, c):
            sc = jnp.sqrt(c)
            pn = _norm(p)
            return _artanh(sc * pn) * p / (sc * pn)

        def expmap(u, base, c):
            sc = jnp.sqrt(c)
            un = _norm(u)
            second = jnp.tanh(sc * _lam(base, c) * un / 2.0) * u / (sc * un)
            return mobius_add(base, second, c)

        def logmap(p, base, c):
            sub = mobius_add(-base, p, c)
            sn = _norm(sub)
            sc = jnp.sqrt(c)
            return 2.0 / (sc * _lam(base, c)) * _artanh(sc * sn) * sub / sn

        def mobius_matvec(W, x, c):
            sc = jnp.sqrt(c)
            xn = _norm(x)
            mx = x @ W.T
            mxn = _norm(mx)
            res = jnp.tanh(mxn / xn * _artanh(sc * xn)) * mx / (mxn * sc)
            is_zero = jnp.all(mx == 0.0, axis=-1, keepdims=True)
            return jnp.where(is_zero, jnp.zeros_like(res), res)

        def project(x, c):
            n = _norm(x)
            maxn = (1.0 - BALL_EPS) / jnp.sqrt(c)
            return jnp.where(n > maxn, x / n * maxn, x)
        key = jax.random.key(seed)
        k1, k2, k3, k4, k5 = jax.random.split(key, 5)
        x_tan = 0.2 * jax.random.normal(k1, (N_NODES, D_IN), jnp.float32)
        x = project(expmap0(x_tan, C), C)
        bound = 0.05 * float(np.sqrt(6.0 / (D_IN + D_OUT)))
        weight = jax.random.uniform(k2, (D_OUT, D_IN), jnp.float32, -bound, bound)
        bias = 0.01 * jax.random.normal(k3, (D_OUT,), jnp.float32)
        edge_index = jax.random.randint(k4, (2, N_EDGES), 0, N_NODES, dtype=jnp.int32)
        edge_weight = jax.random.uniform(k5, (N_EDGES,), jnp.float32)
        return {'x': x, 'weight': weight, 'bias': bias, 'edge_index': edge_index, 'edge_weight': edge_weight}
    _L2_gnn_all = _L2_gnn_setup()
    _L2_gnn_in = {k: v for k, v in _L2_gnn_all.items() if k in ('weight', 'bias')}
    del _L2_gnn_all

    def _L2_ffn_setup():
        import jax, jax.numpy as jnp
        import numpy as np
        BN_EPS = 0.001

        def _bn(h, g, b, m, v):
            return g * (h - m) * jax.lax.rsqrt(v + BN_EPS) + b
        key = jax.random.key(seed)
        ks = jax.random.split(key, 8)
        B, F, Df = (256, 64, 256)
        E, H, D = (8, 256, 256)
        s1 = 1.0 / np.sqrt(Df)
        s2 = 1.0 / np.sqrt(H)
        return {'x': jax.random.normal(ks[0], (B, F, Df), jnp.float32), 'Wr': jax.random.normal(ks[1], (Df, E), jnp.float32) * s1, 'br': jnp.zeros((E,), jnp.float32), 'W1': jax.random.normal(ks[2], (E, Df, H), jnp.float32) * s1, 'b1': jnp.zeros((E, H), jnp.float32), 'g1': jnp.ones((E, H), jnp.float32), 'be1': jnp.zeros((E, H), jnp.float32), 'm1': jnp.zeros((E, H), jnp.float32), 'v1': jnp.ones((E, H), jnp.float32), 'W2': jax.random.normal(ks[3], (E, H, H), jnp.float32) * s2, 'b2': jnp.zeros((E, H), jnp.float32), 'g2': jnp.ones((E, H), jnp.float32), 'be2': jnp.zeros((E, H), jnp.float32), 'm2': jnp.zeros((E, H), jnp.float32), 'v2': jnp.ones((E, H), jnp.float32), 'Wo': jax.random.normal(ks[4], (E, H, D), jnp.float32) * s2, 'bo': jnp.zeros((E, D), jnp.float32)}
    _L2_ffn_all = _L2_ffn_setup()
    _L2_ffn_in = {k: v for k, v in _L2_ffn_all.items() if k in ('Wr', 'br', 'W1', 'b1', 'g1', 'be1', 'm1', 'v1', 'W2', 'b2', 'g2', 'be2', 'm2', 'v2', 'Wo', 'bo')}
    del _L2_ffn_all

    def _L3_gnn_setup():
        import jax, jax.numpy as jnp
        import numpy as np
        EPS = 1e-05

        def _bn(x, gamma, beta):
            m = jnp.mean(x, axis=0)
            v = jnp.mean((x - m) ** 2, axis=0)
            return gamma * (x - m) * jax.lax.rsqrt(v + EPS) + beta

        def _hconv(x, src, dst, ew, w1, b1, w2, b2, g, b):
            h = jax.nn.relu(x @ w1 + b1)
            msg = ew[:, None] * h[src]
            agg = jax.ops.segment_sum(msg, dst, num_segments=x.shape[0])
            h = agg @ w2 + b2
            return jax.nn.relu(_bn(h, g, b))
        N, C, E = (50000, 256, 9375)
        key = jax.random.key(seed)
        ks = jax.random.split(key, 16)
        s = 1.0 / np.sqrt(C)
        inp = {'x': jax.random.normal(ks[0], (N, C), dtype=jnp.float32), 'hyperedge_index': jax.random.randint(ks[1], (2, E), 0, N, dtype=jnp.int32), 'hyperedge_weight': jax.random.uniform(ks[2], (E,), dtype=jnp.float32), 'c1_w1': jax.random.normal(ks[3], (C, C), dtype=jnp.float32) * s, 'c1_b1': jnp.zeros((C,), jnp.float32), 'c1_w2': jax.random.normal(ks[4], (C, C), dtype=jnp.float32) * s, 'c1_b2': jnp.zeros((C,), jnp.float32), 'c1_g': jnp.ones((C,), jnp.float32), 'c1_b': jnp.zeros((C,), jnp.float32), 'bn1_g': jnp.ones((C,), jnp.float32), 'bn1_b': jnp.zeros((C,), jnp.float32), 'c2_w1': jax.random.normal(ks[5], (C, C), dtype=jnp.float32) * s, 'c2_b1': jnp.zeros((C,), jnp.float32), 'c2_w2': jax.random.normal(ks[6], (C, C), dtype=jnp.float32) * s, 'c2_b2': jnp.zeros((C,), jnp.float32), 'c2_g': jnp.ones((C,), jnp.float32), 'c2_b': jnp.zeros((C,), jnp.float32), 'bn2_g': jnp.ones((C,), jnp.float32), 'bn2_b': jnp.zeros((C,), jnp.float32)}
        return inp
    _L3_gnn_all = _L3_gnn_setup()
    _L3_gnn_in = {k: v for k, v in _L3_gnn_all.items() if k in ('c1_w1', 'c1_b1', 'c1_w2', 'c1_b2', 'c1_g', 'c1_b', 'bn1_g', 'bn1_b', 'c2_w1', 'c2_b1', 'c2_w2', 'c2_b2', 'c2_g', 'c2_b', 'bn2_g', 'bn2_b')}
    del _L3_gnn_all

    def _L3_ffn_setup():
        import jax, jax.numpy as jnp
        import numpy as np
        B, S, H, F, E, K = (8, 128, 256, 512, 16, 2)
        EPS = 1e-05
        key = jax.random.key(seed)
        ks = jax.random.split(key, 9)
        sc = 0.02
        return {'x': jax.random.normal(ks[0], (B, S, H), dtype=jnp.float32), 'gate_w': jax.random.normal(ks[1], (H, E), dtype=jnp.float32) * sc, 'gate_b': jnp.zeros((E,), dtype=jnp.float32), 'w1': jax.random.normal(ks[2], (E, H, F), dtype=jnp.float32) * sc, 'b1': jnp.zeros((E, F), dtype=jnp.float32), 'w2': jax.random.normal(ks[3], (E, F, H), dtype=jnp.float32) * sc, 'b2': jnp.zeros((E, H), dtype=jnp.float32), 'gamma': jnp.ones((H,), dtype=jnp.float32), 'beta': jnp.zeros((H,), dtype=jnp.float32)}
    _L3_ffn_all = _L3_ffn_setup()
    _L3_ffn_in = {k: v for k, v in _L3_ffn_all.items() if k in ('gate_w', 'gate_b', 'w1', 'b1', 'w2', 'b2', 'gamma', 'beta')}
    del _L3_ffn_all
    return {'x': x, 'src': src, 'dst': dst, 'edge_attr_64': edge_attr_64, 'edge_weight': edge_weight, 'L0_gnn_W': _L0_gnn_in['W'], 'L0_gnn_att_src': _L0_gnn_in['att_src'], 'L0_gnn_att_dst': _L0_gnn_in['att_dst'], 'L0_gnn_bias': _L0_gnn_in['bias'], 'L0_gnn_ln_w': _L0_gnn_in['ln_w'], 'L0_gnn_ln_b': _L0_gnn_in['ln_b'], 'L0_ffn_router_w': _L0_ffn_in['router_w'], 'L0_ffn_w1': _L0_ffn_in['w1'], 'L0_ffn_b1': _L0_ffn_in['b1'], 'L0_ffn_w2': _L0_ffn_in['w2'], 'L0_ffn_b2': _L0_ffn_in['b2'], 'L1_gnn_W1': _L1_gnn_in['W1'], 'L1_gnn_b1': _L1_gnn_in['b1'], 'L1_gnn_W2': _L1_gnn_in['W2'], 'L1_gnn_b2': _L1_gnn_in['b2'], 'L1_gnn_W_ih': _L1_gnn_in['W_ih'], 'L1_gnn_b_ih': _L1_gnn_in['b_ih'], 'L1_gnn_W_hh': _L1_gnn_in['W_hh'], 'L1_gnn_b_hh': _L1_gnn_in['b_hh'], 'L1_ffn_router_w': _L1_ffn_in['router_w'], 'L1_ffn_router_b': _L1_ffn_in['router_b'], 'L1_ffn_W1': _L1_ffn_in['W1'], 'L1_ffn_b1': _L1_ffn_in['b1'], 'L1_ffn_W2': _L1_ffn_in['W2'], 'L1_ffn_b2': _L1_ffn_in['b2'], 'L2_gnn_weight': _L2_gnn_in['weight'], 'L2_gnn_bias': _L2_gnn_in['bias'], 'L2_ffn_Wr': _L2_ffn_in['Wr'], 'L2_ffn_br': _L2_ffn_in['br'], 'L2_ffn_W1': _L2_ffn_in['W1'], 'L2_ffn_b1': _L2_ffn_in['b1'], 'L2_ffn_g1': _L2_ffn_in['g1'], 'L2_ffn_be1': _L2_ffn_in['be1'], 'L2_ffn_m1': _L2_ffn_in['m1'], 'L2_ffn_v1': _L2_ffn_in['v1'], 'L2_ffn_W2': _L2_ffn_in['W2'], 'L2_ffn_b2': _L2_ffn_in['b2'], 'L2_ffn_g2': _L2_ffn_in['g2'], 'L2_ffn_be2': _L2_ffn_in['be2'], 'L2_ffn_m2': _L2_ffn_in['m2'], 'L2_ffn_v2': _L2_ffn_in['v2'], 'L2_ffn_Wo': _L2_ffn_in['Wo'], 'L2_ffn_bo': _L2_ffn_in['bo'], 'L3_gnn_c1_w1': _L3_gnn_in['c1_w1'], 'L3_gnn_c1_b1': _L3_gnn_in['c1_b1'], 'L3_gnn_c1_w2': _L3_gnn_in['c1_w2'], 'L3_gnn_c1_b2': _L3_gnn_in['c1_b2'], 'L3_gnn_c1_g': _L3_gnn_in['c1_g'], 'L3_gnn_c1_b': _L3_gnn_in['c1_b'], 'L3_gnn_bn1_g': _L3_gnn_in['bn1_g'], 'L3_gnn_bn1_b': _L3_gnn_in['bn1_b'], 'L3_gnn_c2_w1': _L3_gnn_in['c2_w1'], 'L3_gnn_c2_b1': _L3_gnn_in['c2_b1'], 'L3_gnn_c2_w2': _L3_gnn_in['c2_w2'], 'L3_gnn_c2_b2': _L3_gnn_in['c2_b2'], 'L3_gnn_c2_g': _L3_gnn_in['c2_g'], 'L3_gnn_c2_b': _L3_gnn_in['c2_b'], 'L3_gnn_bn2_g': _L3_gnn_in['bn2_g'], 'L3_gnn_bn2_b': _L3_gnn_in['bn2_b'], 'L3_ffn_gate_w': _L3_ffn_in['gate_w'], 'L3_ffn_gate_b': _L3_ffn_in['gate_b'], 'L3_ffn_w1': _L3_ffn_in['w1'], 'L3_ffn_b1': _L3_ffn_in['b1'], 'L3_ffn_w2': _L3_ffn_in['w2'], 'L3_ffn_b2': _L3_ffn_in['b2'], 'L3_ffn_gamma': _L3_ffn_in['gamma'], 'L3_ffn_beta': _L3_ffn_in['beta']}

def reference(x, src, dst, edge_attr_64, edge_weight, L0_gnn_W, L0_gnn_att_src, L0_gnn_att_dst, L0_gnn_bias, L0_gnn_ln_w, L0_gnn_ln_b, L0_ffn_router_w, L0_ffn_w1, L0_ffn_b1, L0_ffn_w2, L0_ffn_b2, L1_gnn_W1, L1_gnn_b1, L1_gnn_W2, L1_gnn_b2, L1_gnn_W_ih, L1_gnn_b_ih, L1_gnn_W_hh, L1_gnn_b_hh, L1_ffn_router_w, L1_ffn_router_b, L1_ffn_W1, L1_ffn_b1, L1_ffn_W2, L1_ffn_b2, L2_gnn_weight, L2_gnn_bias, L2_ffn_Wr, L2_ffn_br, L2_ffn_W1, L2_ffn_b1, L2_ffn_g1, L2_ffn_be1, L2_ffn_m1, L2_ffn_v1, L2_ffn_W2, L2_ffn_b2, L2_ffn_g2, L2_ffn_be2, L2_ffn_m2, L2_ffn_v2, L2_ffn_Wo, L2_ffn_bo, L3_gnn_c1_w1, L3_gnn_c1_b1, L3_gnn_c1_w2, L3_gnn_c1_b2, L3_gnn_c1_g, L3_gnn_c1_b, L3_gnn_bn1_g, L3_gnn_bn1_b, L3_gnn_c2_w1, L3_gnn_c2_b1, L3_gnn_c2_w2, L3_gnn_c2_b2, L3_gnn_c2_g, L3_gnn_c2_b, L3_gnn_bn2_g, L3_gnn_bn2_b, L3_ffn_gate_w, L3_ffn_gate_b, L3_ffn_w1, L3_ffn_b1, L3_ffn_w2, L3_ffn_b2, L3_ffn_gamma, L3_ffn_beta):
    import jax
    import jax.numpy as jnp

    def _L0_gnn_ref(x, edge_index, W, att_src, att_dst, bias, ln_w, ln_b):
        import jax, jax.numpy as jnp
        import numpy as np
        N, D, H = (50000, 256, 8)
        C = D // H
        E = 50000
        NEG_SLOPE = 0.2
        EPS = 1e-05

        def _gat_block(x, src, dst, W, att_src, att_dst, bias, ln_w, ln_b):
            n = x.shape[0]
            h = (x @ W).reshape(n, H, C)
            a_src = jnp.einsum('nhc,hc->nh', h, att_src)
            a_dst = jnp.einsum('nhc,hc->nh', h, att_dst)
            e = a_src[src] + a_dst[dst]
            e = jnp.where(e > 0, e, NEG_SLOPE * e)
            m = jax.ops.segment_max(e, dst, num_segments=n)
            m = jnp.where(jnp.isfinite(m), m, 0.0)
            ex = jnp.exp(e - m[dst])
            denom = jax.ops.segment_sum(ex, dst, num_segments=n)
            alpha = ex / denom[dst]
            msg = h[src] * alpha[..., None]
            out = jax.ops.segment_sum(msg, dst, num_segments=n).reshape(n, H * C) + bias
            y = out + x
            mu = y.mean(axis=-1, keepdims=True)
            var = y.var(axis=-1, keepdims=True)
            return (y - mu) / jnp.sqrt(var + EPS) * ln_w + ln_b
        n = x.shape[0]
        loop = jnp.arange(n, dtype=edge_index.dtype)
        src = jnp.concatenate([edge_index[0], loop])
        dst = jnp.concatenate([edge_index[1], loop])
        return _gat_block(x, src, dst, W, att_src, att_dst, bias, ln_w, ln_b)

    def _L0_ffn_ref(input_embeddings, router_w, w1, b1, w2, b2):
        import jax, jax.numpy as jnp
        import numpy as np
        NUM_EXPERTS = 8
        TOP_K = 2
        B, S, D = (8, 256, 256)

        def _moe(tokens, router_w, w1, b1, w2, b2):
            N = tokens.shape[0]
            E = router_w.shape[0]
            logits = tokens.astype(jnp.float32) @ router_w.astype(jnp.float32).T
            probs = jax.nn.softmax(logits, axis=-1)
            rw, re = jax.lax.top_k(probs, TOP_K)
            if TOP_K > 1:
                rw = rw / jnp.maximum(rw.sum(-1, keepdims=True), 1e-12)
            rw = rw.astype(tokens.dtype)
            combine = jnp.zeros((N, E), tokens.dtype).at[jnp.arange(N)[:, None], re].set(rw)
            out = tokens
            for e in range(E):
                h = jax.nn.gelu(tokens @ w1[e] + b1[e], approximate=False)
                y = h @ w2[e] + b2[e]
                out = out + combine[:, e:e + 1] * y
            return out
        b, s, d = input_embeddings.shape
        tokens = input_embeddings.reshape(b * s, d)
        return _moe(tokens, router_w, w1, b1, w2, b2).reshape(b, s, d)

    def _L1_gnn_ref(h, edge_indices, edge_attr, W1, b1, W2, b2, W_ih, b_ih, W_hh, b_hh):
        import jax, jax.numpy as jnp
        import numpy as np
        N, E, H, ED = (625, 10000, 256, 64)
        row, col = (edge_indices[0], edge_indices[1])
        edge_in = jnp.concatenate([h[row], h[col], edge_attr], axis=-1)
        msg = jax.nn.relu(edge_in @ W1.T + b1) @ W2.T + b2
        agg = jax.ops.segment_sum(msg, row, num_segments=h.shape[0])
        gx = agg @ W_ih.T + b_ih
        gh = h @ W_hh.T + b_hh
        xr, xz, xn = jnp.split(gx, 3, axis=-1)
        hr, hz, hn = jnp.split(gh, 3, axis=-1)
        r = jax.nn.sigmoid(xr + hr)
        z = jax.nn.sigmoid(xz + hz)
        n = jnp.tanh(xn + r * hn)
        h_new = (1.0 - z) * n + z * h
        return h_new

    def _L1_ffn_ref(x, router_w, router_b, W1, b1, W2, b2):
        import jax, jax.numpy as jnp
        import numpy as np
        B, K, D = (512, 16, 256)
        E = 32
        H = int(D * 0.25)
        xf = x.reshape(-1, D)
        logits = xf @ router_w.T + router_b
        idx = jnp.argmax(logits, axis=-1)
        w1t = jnp.take(W1, idx, axis=0)
        h = jnp.einsum('nd,ndh->nh', xf, w1t) + jnp.take(b1, idx, axis=0)
        h = jax.nn.relu(h)
        w2t = jnp.take(W2, idx, axis=0)
        out = jnp.einsum('nh,nhd->nd', h, w2t) + jnp.take(b2, idx, axis=0)
        out = jax.nn.relu(out)
        return out.reshape(x.shape)

    def _L2_gnn_ref(x, weight, bias, edge_index, edge_weight):
        import jax, jax.numpy as jnp
        import numpy as np
        MIN_NORM = 1e-15
        BALL_EPS = 1e-05
        C = 1.0
        N_NODES, N_EDGES, D_IN, D_OUT = (1250, 10000, 256, 256)

        def _sqnorm(x):
            return jnp.sum(x * x, axis=-1, keepdims=True)

        def _norm(x):
            return jnp.maximum(jnp.sqrt(_sqnorm(x)), MIN_NORM)

        def _artanh(x):
            return jnp.arctanh(jnp.clip(x, -1.0 + 1e-07, 1.0 - 1e-07))

        def _lam(x, c):
            return jnp.maximum(2.0 / jnp.maximum(1.0 - c * _sqnorm(x), MIN_NORM), MIN_NORM)

        def mobius_add(x, y, c):
            x2, y2 = (_sqnorm(x), _sqnorm(y))
            xy = jnp.sum(x * y, axis=-1, keepdims=True)
            num = (1.0 + 2.0 * c * xy + c * y2) * x + (1.0 - c * x2) * y
            den = 1.0 + 2.0 * c * xy + c * c * x2 * y2
            return num / jnp.maximum(den, MIN_NORM)

        def expmap0(u, c):
            sc = jnp.sqrt(c)
            un = _norm(u)
            return jnp.tanh(sc * un) * u / (sc * un)

        def logmap0(p, c):
            sc = jnp.sqrt(c)
            pn = _norm(p)
            return _artanh(sc * pn) * p / (sc * pn)

        def expmap(u, base, c):
            sc = jnp.sqrt(c)
            un = _norm(u)
            second = jnp.tanh(sc * _lam(base, c) * un / 2.0) * u / (sc * un)
            return mobius_add(base, second, c)

        def logmap(p, base, c):
            sub = mobius_add(-base, p, c)
            sn = _norm(sub)
            sc = jnp.sqrt(c)
            return 2.0 / (sc * _lam(base, c)) * _artanh(sc * sn) * sub / sn

        def mobius_matvec(W, x, c):
            sc = jnp.sqrt(c)
            xn = _norm(x)
            mx = x @ W.T
            mxn = _norm(mx)
            res = jnp.tanh(mxn / xn * _artanh(sc * xn)) * mx / (mxn * sc)
            is_zero = jnp.all(mx == 0.0, axis=-1, keepdims=True)
            return jnp.where(is_zero, jnp.zeros_like(res), res)

        def project(x, c):
            n = _norm(x)
            maxn = (1.0 - BALL_EPS) / jnp.sqrt(c)
            return jnp.where(n > maxn, x / n * maxn, x)
        c = jnp.float32(C)
        N = x.shape[0]
        src, dst = (edge_index[0], edge_index[1])
        x_src = x[src]
        x_dst = x[dst]
        msg = logmap(x_src, x_dst, c)
        msg = msg * edge_weight[:, None]
        agg = jax.ops.segment_sum(msg, dst, num_segments=N)
        u = expmap(agg, x, c)
        h = mobius_matvec(weight, u, c)
        b_ball = expmap0(jnp.broadcast_to(bias, h.shape), c)
        h = mobius_add(h, b_ball, c)
        h_tan = jax.nn.relu(logmap0(h, c))
        h = expmap0(h_tan, c)
        return project(h, c)

    def _L2_ffn_ref(x, Wr, br, W1, b1, g1, be1, m1, v1, W2, b2, g2, be2, m2, v2, Wo, bo):
        import jax, jax.numpy as jnp
        import numpy as np
        BN_EPS = 0.001

        def _bn(h, g, b, m, v):
            return g * (h - m) * jax.lax.rsqrt(v + BN_EPS) + b
        feat = jnp.mean(x, axis=0)
        w = jax.nn.softmax(feat @ Wr + br, axis=-1)
        h = jnp.einsum('bfd,edh->bfeh', x, W1) + b1
        h = jax.nn.relu(_bn(h, g1, be1, m1, v1))
        h = jnp.einsum('bfeh,ehk->bfek', h, W2) + b2
        h = jax.nn.relu(_bn(h, g2, be2, m2, v2))
        y = jnp.einsum('bfeh,ehd->bfed', h, Wo) + bo
        return jnp.einsum('bfed,fe->bfd', y, w)

    def _L3_gnn_ref(x, hyperedge_index, hyperedge_weight, c1_w1, c1_b1, c1_w2, c1_b2, c1_g, c1_b, bn1_g, bn1_b, c2_w1, c2_b1, c2_w2, c2_b2, c2_g, c2_b, bn2_g, bn2_b):
        import jax, jax.numpy as jnp
        import numpy as np
        EPS = 1e-05

        def _bn(x, gamma, beta):
            m = jnp.mean(x, axis=0)
            v = jnp.mean((x - m) ** 2, axis=0)
            return gamma * (x - m) * jax.lax.rsqrt(v + EPS) + beta

        def _hconv(x, src, dst, ew, w1, b1, w2, b2, g, b):
            h = jax.nn.relu(x @ w1 + b1)
            msg = ew[:, None] * h[src]
            agg = jax.ops.segment_sum(msg, dst, num_segments=x.shape[0])
            h = agg @ w2 + b2
            return jax.nn.relu(_bn(h, g, b))
        src, dst = (hyperedge_index[0], hyperedge_index[1])
        residual = x
        h = _hconv(x, src, dst, hyperedge_weight, c1_w1, c1_b1, c1_w2, c1_b2, c1_g, c1_b)
        h = jax.nn.relu(_bn(h, bn1_g, bn1_b))
        h = _hconv(h, src, dst, hyperedge_weight, c2_w1, c2_b1, c2_w2, c2_b2, c2_g, c2_b)
        h = _bn(h, bn2_g, bn2_b)
        return jax.nn.relu(h + residual)

    def _L3_ffn_ref(x, gate_w, gate_b, w1, b1, w2, b2, gamma, beta):
        import jax, jax.numpy as jnp
        import numpy as np
        B, S, H, F, E, K = (8, 128, 256, 512, 16, 2)
        EPS = 1e-05
        gate_logits = x @ gate_w + gate_b
        topk_vals, topk_idx = jax.lax.top_k(gate_logits, K)
        topk_w = jax.nn.softmax(topk_vals, axis=-1)
        h = jax.nn.relu(jnp.einsum('bsh,ehf->bsef', x, w1) + b1)
        expert_out = jnp.einsum('bsef,efh->bseh', h, w2) + b2
        sel = jnp.take_along_axis(expert_out, topk_idx[:, :, :, None], axis=2)
        moe = jnp.sum(topk_w[..., None] * sel, axis=2)
        y = x + moe
        mu = jnp.mean(y, axis=-1, keepdims=True)
        var = jnp.var(y, axis=-1, keepdims=True)
        return (y - mu) / jnp.sqrt(var + EPS) * gamma + beta
    edge_index = jnp.stack([src, dst])
    x = x + _L0_gnn_ref(_layernorm(x, axis=-1), edge_index, L0_gnn_W, L0_gnn_att_src, L0_gnn_att_dst, L0_gnn_bias, L0_gnn_ln_w, L0_gnn_ln_b)
    x = x + _L0_ffn_ref(_layernorm(x, axis=-1)[None], L0_ffn_router_w, L0_ffn_w1, L0_ffn_b1, L0_ffn_w2, L0_ffn_b2)[0]
    x = x + _L1_gnn_ref(_layernorm(x, axis=-1), edge_index, edge_attr_64, L1_gnn_W1, L1_gnn_b1, L1_gnn_W2, L1_gnn_b2, L1_gnn_W_ih, L1_gnn_b_ih, L1_gnn_W_hh, L1_gnn_b_hh)
    x = x + _L1_ffn_ref(_layernorm(x, axis=-1)[None], L1_ffn_router_w, L1_ffn_router_b, L1_ffn_W1, L1_ffn_b1, L1_ffn_W2, L1_ffn_b2)[0]
    x = x + _L2_gnn_ref(_layernorm(x, axis=-1), L2_gnn_weight, L2_gnn_bias, edge_index, edge_weight)
    x = x + _L2_ffn_ref(_layernorm(x, axis=-1)[None], L2_ffn_Wr, L2_ffn_br, L2_ffn_W1, L2_ffn_b1, L2_ffn_g1, L2_ffn_be1, L2_ffn_m1, L2_ffn_v1, L2_ffn_W2, L2_ffn_b2, L2_ffn_g2, L2_ffn_be2, L2_ffn_m2, L2_ffn_v2, L2_ffn_Wo, L2_ffn_bo)[0]
    x = x + _L3_gnn_ref(_layernorm(x, axis=-1), edge_index, edge_weight, L3_gnn_c1_w1, L3_gnn_c1_b1, L3_gnn_c1_w2, L3_gnn_c1_b2, L3_gnn_c1_g, L3_gnn_c1_b, L3_gnn_bn1_g, L3_gnn_bn1_b, L3_gnn_c2_w1, L3_gnn_c2_b1, L3_gnn_c2_w2, L3_gnn_c2_b2, L3_gnn_c2_g, L3_gnn_c2_b, L3_gnn_bn2_g, L3_gnn_bn2_b)
    x = x + _L3_ffn_ref(_layernorm(x, axis=-1)[None], L3_ffn_gate_w, L3_ffn_gate_b, L3_ffn_w1, L3_ffn_b1, L3_ffn_w2, L3_ffn_b2, L3_ffn_gamma, L3_ffn_beta)[0]
    return x

_drawn_inputs = setup_inputs


def setup_inputs(seed=0):
    import zlib

    import numpy as np

    out = dict(_drawn_inputs(seed))
    spreads = {'L0_gnn_bias': (0.0, 0.1),
     'L0_gnn_ln_w': (1.0, 0.2),
     'L0_gnn_ln_b': (0.0, 0.1),
     'L0_ffn_b1': (0.0, 0.409),
     'L0_ffn_b2': (0.0, 0.282),
     'L1_gnn_b1': (0.0, 0.1),
     'L1_gnn_b2': (0.0, 0.1),
     'L1_gnn_b_ih': (0.0, 0.8),
     'L1_gnn_b_hh': (0.0, 0.8),
     'L2_ffn_br': (0.0, 0.8),
     'L2_ffn_b1': (0.0, 0.8),
     'L2_ffn_g1': (1.0, 0.6),
     'L2_ffn_be1': (0.0, 0.8),
     'L2_ffn_m1': (0.0, 0.8),
     'L2_ffn_v1': (1.0, 0.6),
     'L2_ffn_b2': (0.0, 0.78),
     'L2_ffn_g2': (1.0, 0.6),
     'L2_ffn_be2': (0.0, 0.8),
     'L2_ffn_m2': (0.0, 0.752),
     'L2_ffn_v2': (1.0, 0.6),
     'L2_ffn_bo': (0.0, 0.562),
     'L3_gnn_c1_b1': (0.0, 0.269),
     'L3_gnn_c1_b2': (0.0, 0.8),
     'L3_gnn_c1_g': (1.0, 0.6),
     'L3_gnn_c1_b': (0.0, 0.726),
     'L3_gnn_bn1_g': (1.0, 0.2),
     'L3_gnn_bn1_b': (0.0, 0.433),
     'L3_gnn_c2_b1': (0.0, 0.281),
     'L3_gnn_c2_b2': (0.0, 0.8),
     'L3_gnn_c2_g': (1.0, 0.6),
     'L3_gnn_c2_b': (0.0, 0.775),
     'L3_gnn_bn2_g': (1.0, 0.2),
     'L3_gnn_bn2_b': (0.0, 0.504),
     'L3_ffn_gate_b': (0.0, 0.574),
     'L3_ffn_b1': (0.0, 0.8),
     'L3_ffn_b2': (0.0, 0.56),
     'L3_ffn_gamma': (1.0, 0.2),
     'L3_ffn_beta': (0.0, 0.436)}
    factors = {'L0_gnn_att_dst': 3.008,
     'L1_ffn_router_b': 4.103,
     'L1_ffn_b1': 8.0,
     'L1_ffn_b2': 7.793,
     'L2_gnn_weight': 8.0,
     'L2_gnn_bias': 8.0,
     'L3_ffn_gate_w': 2.947,
     'L3_ffn_w1': 4.652,
     'L3_ffn_w2': 3.723}
    for name, (base, spread) in spreads.items():
        noise = np.random.default_rng([zlib.crc32(name.encode()), seed]).standard_normal(out[name].shape)
        drawn = base * np.exp(spread * noise) if base else spread * noise
        out[name] = jnp.asarray(drawn.astype(out[name].dtype))
    for name, factor in factors.items():
        out[name] = (out[name] * factor).astype(out[name].dtype)
    return out
```

```python
from contextlib import ExitStack, contextmanager

import concourse.bass as bass
from concourse import mybir

F32 = mybir.dt.float32
I32 = mybir.dt.int32
BF16 = mybir.dt.bfloat16
ALU = mybir.AluOpType
ACT = mybir.ActivationFunctionType
AX = mybir.AxisListType.X

N, D, E = 3125, 256, 50000
P = 125
NB = N // P
K = D // 128
EC = E // P
NT = (E + NB * 127) // 128 + 1
NT += -NT % 16
SLOTS = NT * 128
G = 8
ITERS = NT // (2 * G)
HEADS, HC = 8, 32
ED = 64
CH = 4
NCHUNK = -(-NB // CH)
EPS = 1e-5
MIN_NORM = 1e-15
PAD_KEY = -1.0e6
XG = D + 8


def chunk_blocks(c):
    return range(CH * c, min(CH * c + CH, NB))


class Chain:

    def __init__(self, eng, sem, base=0):
        self.eng, self.sem, self.base, self.n = eng, sem, base, 0

    def step(self, ins):
        ins.then_inc(self.sem, 1)
        self.n += 1

    def sync(self):
        self.eng.wait_ge(self.sem, self.base + self.n)

    def link(self, ins):
        self.step(ins)
        self.sync()

    def loop(self, i, per):
        body = Chain(self.eng, self.sem, self.base + self.n + i * per)
        body.per = per
        return body

    def after(self, body, iterations):
        assert body.n == body.per, (body.n, body.per)
        self.n += body.n * iterations


def peeled(eng, n):
    yield 0
    if n > 1:
        with eng.Fori(1, n) as i:
            yield i


def later(i):
    return not isinstance(i, int)


@contextmanager
def phase(nc, name):
    with nc.cleanup_on_exit(), ExitStack() as ctx:
        def sb(what, shape, dt=F32):
            return ctx.enter_context(nc.sbuf_tensor(f"{name}_{what}", shape, dt))

        def sem(what):
            return nc.alloc_semaphore(f"{name}_{what}")

        yield sb, sem


def bc(ap, n):
    return ap.unsqueeze(2).to_broadcast([ap.shape[0], ap.shape[1], n])


def bc_mid(ap, n):
    return ap.unsqueeze(1).to_broadcast([ap.shape[0], n, ap.shape[1]])


def row(ap, n=P):
    return ap.rearrange("(a d) -> a d", a=1).to_broadcast([n, ap.shape[0]])


class Shared:
    pass


VECTORS = [
    ("L0_ffn_b1", 8, 256), ("L1_ffn_b1", 32, 64), ("L3_ffn_b1", 16, 512),
    *[(f"L2_ffn_{v}{i}", 8, 256) for i in (1, 2) for v in ("b", "g", "be", "m", "v")],
    *[(f"L3_gnn_{v}", 1, 256) for v in ("c1_b1", "c1_b2", "c1_g", "c1_b", "bn1_g", "bn1_b",
                                        "c2_b1", "c2_b2", "c2_g", "c2_b", "bn2_g", "bn2_b")],
]


def place_vectors():
    place, tile, at = {}, 0, 0
    for name, e, f in VECTORS:
        rows = e * f // 128
        if at + rows > 128:
            tile, at = tile + 1, 0
        place[name] = (tile, at, rows)
        at += rows
    return place, tile + 1


TURNED = [
    ("L0_ffn_router_w", 8, 256), ("L1_gnn_W1", 256, 576), ("L1_gnn_W2", 256, 256),
    ("L1_gnn_W_ih", 768, 256), ("L1_gnn_W_hh", 768, 256), ("L1_ffn_router_w", 32, 256),
    ("L2_gnn_weight", 256, 256),
]


def setup(nc, S, A):
    place, ntiles = place_vectors()
    S.column = {name: tile * 128 + at for name, (tile, at, _) in place.items()}
    with phase(nc, "setup") as (sb, sem):
        vec = sb("vec", [128, ntiles, 128])
        natural = {n: sb(n, [128, -(-r // 128), c]) for n, r, c in TURNED}
        turned = {n: sb(n + "_t", [128, -(-c // 128), r]) for n, r, c in TURNED}
        loaded, constants, turned_sem, copied, stored, zeroed = (
            sem(x) for x in ("loaded", "constants", "blocks_turned", "blocks_copied", "stored", "zeroed"))
        jobs = [(vec[:, t, :], S.pcol[:, t * 128:(t + 1) * 128], 128, 128) for t in range(ntiles)]
        for n, r, c in TURNED:
            for a in range(-(-r // 128)):
                for b in range(-(-c // 128)):
                    rows, cols = min(128, r - a * 128), min(128, c - b * 128)
                    jobs.append((natural[n][0:rows, a, b * 128:b * 128 + cols],
                                 turned[n][0:cols, b, a * 128:a * 128 + rows], rows, cols))
        loads = []
        for name, e, f in VECTORS:
            tile, at, rows = place[name]
            src = A[name].rearrange("(k p) -> k p", p=128) if e == 1 else (
                A[name].rearrange("(e j) p -> e (j p)", j=2) if f == 64 else
                A[name].rearrange("e (k p) -> (e k) p", p=128))
            loads.append((vec[at:at + rows, tile, :], src))
        for n, r, c in TURNED:
            if r < 128:
                loads.append((natural[n][0:r, 0, :], A[n]))
            else:
                loads.append((natural[n][:, :, :], A[n].rearrange("(a p) c -> p a c", p=128)))
        loads.append((S.x[:, :, :], A["x"].rearrange("(t p) d -> p t d", p=P)))

        with nc.Block() as block:
            @block.sync
            def _(sp):
                sp.wait_ge(zeroed, 1)
                for dst, src in loads:
                    sp.dma_start(dst, src).then_inc(loaded, 16)
                sp.wait_ge(copied, len(jobs))
                n_stores = 0
                for n, r, c in TURNED:
                    full = c // 128
                    sp.dma_start(S.turned[n][0:full * 128, :].rearrange("(b p) r -> p b r", p=128),
                                 turned[n][:, 0:full, :]).then_inc(stored, 16)
                    n_stores += 1
                    if c % 128:
                        sp.dma_start(S.turned[n][full * 128:c, :], turned[n][0:c % 128, full, :]).then_inc(stored, 16)
                        n_stores += 1
                sp.wait_ge(stored, 16 * n_stores)

            @block.gpsimd
            def _(pool):
                pool.memset(vec[:], 0.0).then_inc(zeroed, 1)
                pool.memset(S.ident[:], 0.0).then_inc(constants, 1)
                pool.wait_ge(constants, 1)
                pool.affine_select(out=S.ident[:], in_=S.ident[:], compare_op=ALU.not_equal, fill=1.0,
                                   base=0, pattern=[[-1, 128]], channel_multiplier=1).then_inc(constants, 1)
                pool.iota(S.iota[:], pattern=[[1, 128]], base=0, channel_multiplier=0,
                          allow_small_or_imprecise_dtypes=True).then_inc(constants, 1)
                pool.memset(S.ones[:], 1.0).then_inc(constants, 1)

            @block.tensor
            def _(pe):
                pe.wait_ge(loaded, 16 * len(loads))
                pe.wait_ge(constants, 4)
                for j, (src, _, rows, cols) in enumerate(jobs):
                    if j >= 8:
                        pe.wait_ge(copied, j - 7)
                    pe.transpose(S.ps[0:cols, j % 8, 0:rows], src, S.ident[0:rows, 0:rows]).then_inc(turned_sem, 1)

            @block.vector
            def _(dve):
                for j, (_, dst, rows, cols) in enumerate(jobs):
                    dve.wait_ge(turned_sem, j + 1)
                    dve.tensor_copy(dst, S.ps[0:cols, j % 8, 0:rows]).then_inc(copied, 1)


def sort_edges(nc, S, A, by, attributes):
    name = f"sort_{by}"
    other = "src" if by == "dst" else "dst"
    W = 2 + ED if attributes else 3
    table = S.records[by]
    PADS = 16
    SG = 8
    with phase(nc, name) as (sb, sem):
        key_i, other_i = sb("key_i", [P, EC], I32), sb("other_i", [P, EC], I32)
        key, oth, weight = sb("key", [P, EC]), sb("oth", [P, EC]), sb("weight", [P, EC])
        ge = sb("ge", [P, NB + 1, EC], BF16)
        onehot = sb("onehot", [P, NB, EC], BF16)
        one_t = sb("one_t", [128, EC])
        before = sb("before", [P, P], BF16)
        ones_b = sb("ones_b", [P, 128], BF16)
        count, ones_p = sb("count", [P, NB]), sb("ones_p", [P, 128])
        tiles_i, tiles = sb("tiles_i", [128, NB], I32), sb("tiles", [128, NB])
        upto, start, slot0 = sb("upto", [128, NB]), sb("start", [128, NB]), sb("slot0", [128, NB])
        iota_t, blk = sb("iota_t", [128, NT]), sb("blk", [128, NT])
        cum, pos = sb("cum", [P, 2, EC]), sb("pos", [P, EC])
        hi_i, hi, addr = sb("hi_i", [P, EC], I32), sb("hi", [P, EC]), sb("addr", [P, EC], I32)
        pad = sb("pad", [128, PADS, W])
        stage = sb("stage", [P, 2, SG, W])
        idx = sb("idx", [P, 2, SG], I32)
        back = None if attributes else sb("back", [128, NT, W])
        backs = sb("backs", [128, NT, 2]) if attributes else None
        loaded, consts, padded = sem("loaded"), sem("consts"), sem("pads_stored")
        dve_step, counts_ready, ranks = sem("dve_step"), sem("counts_ready"), sem("ranks_ready")
        ranks_used, pool_step = sem("ranks_used"), sem("pool_step")
        staged = [sem(f"staged{h}") for h in range(2)]
        attr_in = [sem(f"attributes_loaded{h}") for h in range(2)]
        scattered = [sem(f"scattered{h}") for h in range(2)]
        addresses, back_in, go = sem("addresses_ready"), sem("records_back"), sem("go")
        view = table.rearrange("(p t) w -> p t w", p=128)
        edge_view = A["edge_attr_64"].rearrange("(p t) c -> p t c", p=P)
        HALVES = EC // (2 * SG)

        with nc.Block() as block:
            @block.sync
            def _(sp):
                sp.dma_start(key_i[:], A[by].rearrange("(p t) -> p t", p=P)).then_inc(loaded, 16)
                sp.dma_start(other_i[:], A[other].rearrange("(p t) -> p t", p=P)).then_inc(loaded, 16)
                sp.dma_start(weight[:], A["edge_weight"].rearrange("(p t) -> p t", p=P)).then_inc(loaded, 16)
                sp.wait_ge(consts, 4)
                for t in range(0, NT, PADS):
                    sp.dma_start(view[:, t:t + PADS, :], pad[:]).then_inc(padded, 16)
                if attributes:
                    for i in peeled(sp, HALVES):
                        for h in range(2):
                            if later(i):
                                sp.wait_ge(scattered[h], i * 16 * SG)
                            sp.dma_start(stage[:, h, :, 2:W],
                                         edge_view[:, bass.ds((2 * i + h) * SG, SG), :]).then_inc(attr_in[h], 16)
                for h in range(2):
                    sp.wait_ge(scattered[h], 16 * SG * HALVES)
                if attributes:
                    sp.dma_start(backs[:], view[:, :, 0:2], allow_slow_non_contiguous=True).then_inc(back_in, 16)
                else:
                    sp.dma_start(back[:], view).then_inc(back_in, 16)
                sp.wait_ge(back_in, 16)

            @block.gpsimd
            def _(pool):
                ch = Chain(pool, pool_step)
                ch.link(pool.memset(pad[:], 0.0))
                pool.memset(pad[:, :, 1:2], PAD_KEY).then_inc(consts, 1)
                ch.link(pool.memset(before[:], 0.0))
                pool.affine_select(out=before[:], in_=before[:], compare_op=ALU.is_gt, fill=-1.0, base=0,
                                   pattern=[[1, P]], channel_multiplier=-1).then_inc(consts, 1)
                pool.iota(iota_t[:], pattern=[[1, NT]], base=0, channel_multiplier=0,
                          allow_small_or_imprecise_dtypes=True).then_inc(consts, 1)
                pool.memset(ones_b[:], 1.0).then_inc(consts, 1)
                pool.wait_ge(padded, 16 * (NT // PADS))
                with pool.Fori(0, HALVES) as i:
                    for h in range(2):
                        if attributes:
                            pool.wait_ge(attr_in[h], (i + 1) * 16)
                        pool.wait_ge(staged[h], i + 1)
                        pool.sem_inc(go, 1)
                        for t in range(SG):
                            pool.indirect_dma_start(
                                out=table, out_offset=bass.IndirectOffsetOnAxis(ap=idx[:, h, t:t + 1], axis=0),
                                in_=stage[:, h, t, :], in_offset=None).then_inc(scattered[h], 16)

            @block.tensor
            def _(pe):
                pe.wait_ge(counts_ready, 1)
                pe.matmul(S.ps[:, 7, 0:NB], ones_p[:], count[:], start=True, stop=True).then_inc(ranks, 1)
                pe.wait_ge(consts, 4)
                for b in range(NB):
                    if b >= 3:
                        pe.wait_ge(ranks_used, b - 2)
                    k = 2 * (b % 3)
                    pe.matmul(S.ps[0:P, k, 0:EC], ones_b[:, 0:P], onehot[:, b, :], start=True, stop=True)
                    pe.matmul(S.ps[0:P, k + 1, 0:EC], before[:], onehot[:, b, :],
                              start=True, stop=True).then_inc(ranks, 1)

            @block.vector
            def _(dve):
                ch = Chain(dve, dve_step)
                ch.step(dve.memset(one_t[:], 1.0))
                ch.step(dve.memset(ones_p[:], 1.0))
                ch.step(dve.memset(ge[:, 0, :], 1.0))
                ch.step(dve.memset(ge[:, NB, :], 0.0))
                dve.wait_ge(loaded, 48)
                ch.step(dve.tensor_copy(oth[:], other_i[:]))
                ch.link(dve.tensor_copy(key[:], key_i[:]))
                for b in range(1, NB):
                    ch.step(dve.tensor_scalar(ge[:, b, :], key[:], float(P * b), None, ALU.is_ge))
                ch.sync()
                ch.link(dve.tensor_tensor(onehot[:], ge[:, 0:NB, :], ge[:, 1:NB + 1, :], ALU.subtract))
                ch.link(dve.tensor_reduce(count[:], onehot[:], AX, ALU.add))
                dve.sem_inc(counts_ready, 1)
                dve.wait_ge(ranks, 1)
                ch.link(dve.tensor_scalar(tiles_i[:], S.ps[:, 7, 0:NB], 127.0, None, ALU.add))
                ch.link(dve.tensor_scalar(tiles_i[:], tiles_i[:], 7, None, ALU.arith_shift_right))
                ch.link(dve.tensor_copy(tiles[:], tiles_i[:]))
                ch.link(dve.tensor_tensor_scan(upto[:], one_t[:, 0:NB], tiles[:], 0.0, ALU.mult, ALU.add))
                ch.link(dve.tensor_tensor(start[:], upto[:], tiles[:], ALU.subtract))
                ch.link(dve.tensor_scalar(slot0[:], start[:], 128.0, None, ALU.mult))
                dve.wait_ge(consts, 4)
                ch.link(dve.tensor_scalar(blk[:], iota_t[:], start[:, 1:2], None, ALU.is_ge))
                for b in range(2, NB):
                    ch.link(dve.scalar_tensor_tensor(blk[:], iota_t[:], start[:, b:b + 1], blk[:],
                                                     ALU.is_ge, ALU.add))
                ch.step(dve.tensor_copy(S.blk[by][:], blk[0:1, :]))
                ch.link(dve.memset(pos[:], 0.0))
                for b in range(NB):
                    k = 2 * (b % 3)
                    dve.wait_ge(ranks, b + 2)
                    ch.link(dve.tensor_tensor_scan(cum[:, 0, :], one_t[0:P, :], S.ps[0:P, k, 0:EC],
                                                   slot0[0:P, b:b + 1], ALU.mult, ALU.add))
                    ch.link(dve.tensor_tensor(cum[:, 1, :], cum[:, 0, :], S.ps[0:P, k + 1, 0:EC], ALU.add))
                    dve.sem_inc(ranks_used, 1)
                    ch.link(dve.tensor_tensor(cum[:, 1, :], cum[:, 1, :], onehot[:, b, :], ALU.mult))
                    ch.link(dve.tensor_tensor(pos[:], pos[:], cum[:, 1, :], ALU.add))
                ch.link(dve.tensor_copy(hi_i[:], pos[:]))
                ch.link(dve.tensor_scalar(hi_i[:], hi_i[:], 7, None, ALU.arith_shift_right))
                ch.link(dve.tensor_copy(hi[:], hi_i[:]))
                ch.link(dve.scalar_tensor_tensor(pos[:], hi[:], -128.0, pos[:], ALU.mult, ALU.add))
                ch.link(dve.scalar_tensor_tensor(addr[:], pos[:], float(NT), hi[:], ALU.mult, ALU.add))
                for i in peeled(dve, HALVES):
                    body = ch.loop(i, 2 * (4 if not attributes else 3))
                    for h in range(2):
                        if later(i):
                            dve.wait_ge(scattered[h], i * 16 * SG)
                        at = bass.ds((2 * i + h) * SG, SG)
                        body.step(dve.tensor_copy(idx[:, h, :], addr[:, at]))
                        body.step(dve.tensor_copy(stage[:, h, :, 0], oth[:, at]))
                        if not attributes:
                            body.step(dve.tensor_copy(stage[:, h, :, 2], weight[:, at]))
                        body.link(dve.tensor_copy(stage[:, h, :, 1], key[:, at]))
                        dve.sem_inc(staged[h], 1)
                ch.after(body, HALVES)
                dve.wait_ge(back_in, 16)
                recs = backs if attributes else back
                ch.step(dve.tensor_copy(S.end[by][:], recs[:, :, 0]))
                if not attributes:
                    ch.step(dve.tensor_copy(S.edge_w[:], recs[:, :, 2]))
                ch.link(dve.scalar_tensor_tensor(S.local[by][:], blk[:], -float(P), recs[:, :, 1],
                                                 ALU.mult, ALU.add))


def layer_norm(nc, S, name, turn=True):
    with phase(nc, name) as (sb, sem):
        stats, mv = sb("stats", [P, NB, 6]), sb("mv", [P, NB, 2])
        var, root, inv = sb("var", [P, NB]), sb("root", [P, NB]), sb("inv", [P, NB])
        dve_step, var_ready, root_ready = sem("dve_step"), sem("var_ready"), sem("root_ready")
        normed, turned, emptied = sem("blocks_normed"), sem("blocks_turned"), sem("banks_emptied")
        with nc.Block() as block:
            @block.vector
            def _(dve):
                ch = Chain(dve, dve_step)
                for t in range(NB):
                    ch.step(dve.bn_stats(stats[:, t, :], S.x[:, t, :]))
                ch.sync()
                for t in range(NB):
                    ch.step(dve.bn_aggr(mv[:, t, :], stats[:, t, :]))
                ch.sync()
                inverse_root(ch, dve, S, mv[:, :, 1], EPS, var, root, inv, var_ready, root_ready)
                for t in range(NB):
                    dve.tensor_scalar(S.xn[:, t, :], S.x[:, t, :], mv[:, t, 0:1], inv[:, t:t + 1],
                                      ALU.subtract, ALU.mult).then_inc(normed, 1)

            @block.scalar
            def _(act):
                act.wait_ge(var_ready, 1)
                act.activation(root[:], var[:], ACT.Sqrt).then_inc(root_ready, 1)
                if turn:
                    for t in range(NB):
                        act.wait_ge(turned, t + 1)
                        act.copy(S.xT[:, :, t * P:(t + 1) * P],
                                 S.ps[:, t % 8, 0:K * P].rearrange("q (k p) -> q k p", k=K)).then_inc(emptied, 1)

            @block.tensor
            def _(pe):
                for t in range(NB if turn else 0):
                    pe.wait_ge(normed, t + 1)
                    if t >= 8:
                        pe.wait_ge(emptied, t - 7)
                    for k in range(K):
                        ins = pe.transpose(S.ps[:, t % 8, k * P:(k + 1) * P],
                                           S.xn[:, t, k * 128:(k + 1) * 128], S.ident[0:P, 0:P])
                    ins.then_inc(turned, 1)


def inverse_root(ch, dve, S, src, eps, var, root, inv, var_ready, root_ready, n=1):
    ch.link(dve.tensor_scalar(var[:], src, eps, None, ALU.add))
    dve.sem_inc(var_ready, 1)
    dve.wait_ge(root_ready, n)
    ch.link(dve.reciprocal(inv[:], root[:]))
    ch.link(dve.tensor_tensor(inv[:], inv[:], var[:], ALU.mult))
    ch.link(dve.tensor_tensor(root[:], root[:], inv[:], ALU.add))
    ch.link(dve.tensor_scalar(root[:], root[:], 0.5, None, ALU.mult))
    ch.link(dve.reciprocal(inv[:], root[:]))


def gather_groups(pool, ends, table, idx, rows, free, gathered, copied, go, iters=ITERS):
    for i in peeled(pool, iters):
        for h in range(2):
            if later(i):
                pool.wait_ge(free[h], i)
            pool.tensor_copy(idx[:, h, :], ends[:, bass.ds((2 * i + h) * G, G)]).then_inc(copied, 1)
            pool.wait_ge(copied, 2 * i + h + 1)
            pool.sem_inc(go, 1)
            for t in range(G):
                pool.indirect_dma_start(
                    out=rows[:, h, t, :], out_offset=None, in_=table,
                    in_offset=bass.IndirectOffsetOnAxis(ap=idx[:, h, t:t + 1], axis=0)).then_inc(gathered[h], 16)


def block_of(eng, blk, i, h, t):
    return eng.value_load(blk[0:1, bass.ds((2 * i + h) * G + t, 1)], min_val=0, max_val=NB - 1)


def at_block(table, b):
    return table[:, bass.ds(b, 1), :].rearrange("p a c -> p (a c)")


def leaky(ch, dve, out, x):
    ch.link(dve.scalar_tensor_tensor(out, x, 0.2, x, ALU.mult, ALU.max))


def gat(nc, S, A):
    ends, local, blk = S.end["dst"], S.local["dst"], S.blk["dst"]
    NEG = -float(2 ** 100)
    with phase(nc, "gat") as (sb, sem):
        w = sb("w", [128, K, D])
        att = sb("att", [P, 2, D])
        bias, ln_w, ln_b = sb("bias", [P, D]), sb("ln_w", [P, D]), sb("ln_b", [P, D])
        work = sb("work", [P, NB, D])
        a_src, node = sb("a_src", [P, NB, HEADS]), sb("node", [P, NB, 2 * HEADS])
        most, self_e = sb("most", [P, NB, HEADS]), sb("self_e", [P, NB, HEADS])
        dve_step, act_step = sem("dve_step"), sem("act_step")

        loaded, product, evacuated, scored, stored = (
            sem(x) for x in ("loaded", "product", "evacuated", "scored", "stored"))
        ch = Chain(None, dve_step)
        with nc.Block() as block:
            @block.sync
            def _(sp):
                sp.dma_start(w[:], A["L0_gnn_W"].rearrange("(k p) f -> p k f", p=128)).then_inc(loaded, 16)
                for j, n in enumerate(("L0_gnn_att_src", "L0_gnn_att_dst")):
                    sp.dma_start(att[:, j, :], row(A[n].rearrange("h c -> (h c)"))).then_inc(loaded, 16)
                for t, n in ((bias, "L0_gnn_bias"), (ln_w, "L0_gnn_ln_w"), (ln_b, "L0_gnn_ln_b")):
                    sp.dma_start(t[:], row(A[n])).then_inc(loaded, 16)
                sp.wait_ge(evacuated, NB)
                sp.wait_ge(scored, 1)
                sp.dma_start(S.rows.rearrange("(t p) c -> p t c", p=P), S.acc[:]).then_inc(stored, 16)
                sp.dma_start(S.rows8.rearrange("(t p) c -> p t c", p=P), a_src[:]).then_inc(stored, 16)
                sp.wait_ge(stored, 32)

            @block.tensor
            def _(pe):
                pe.wait_ge(loaded, 96)
                for t in range(NB):
                    if t >= 8:
                        pe.wait_ge(evacuated, t - 7)
                    for k in range(K):
                        ins = pe.matmul(S.ps[0:P, t % 8, 0:D], S.xT[:, k, t * P:(t + 1) * P], w[:, k, :],
                                        start=k == 0, stop=k == K - 1)
                    ins.then_inc(product, 1)

            @block.scalar
            def _(act):
                for t in range(NB):
                    act.wait_ge(product, t + 1)
                    act.copy(S.acc[:, t, 0:D], S.ps[0:P, t % 8, 0:D]).then_inc(evacuated, 1)

            @block.vector
            def _(dve):
                ch.eng = dve
                dve.wait_ge(loaded, 96)
                dve.wait_ge(evacuated, NB)
                for j, out in enumerate((a_src[:, :, :], node[:, :, 0:HEADS])):
                    ch.link(dve.tensor_tensor(work[:], S.acc[:, :, 0:D], bc_mid(att[:, j, :], NB), ALU.mult))
                    ch.link(dve.tensor_reduce(out, work[:].rearrange("p t (h c) -> p t h c", h=HEADS),
                                              AX, ALU.add))
                ch.link(dve.tensor_copy(S.acc[:, :, D:XG], a_src[:]))
                dve.sem_inc(scored, 1)
                ch.link(dve.tensor_copy(most[:], a_src[:]))

        gathered = [sem(f"max_gathered{h}") for h in range(2)]
        used = [sem(f"max_used{h}") for h in range(2)]
        copied, go, prepared, spread = (sem(x) for x in ("max_copied", "max_go", "max_prepared", "max_spread"))
        reduced, consts = sem("max_reduced"), sem("max_consts")
        with nc.Block() as block, ExitStack() as ctx:
            def mb(what, shape, dt=F32):
                return ctx.enter_context(nc.sbuf_tensor(f"gat_{what}", shape, dt))

            idx, rows = mb("idx", [128, 2, G], I32), mb("rows8", [128, 2, G, HEADS])
            loc = mb("loc", [128, 2, G])
            other_node = mb("other_node", [128, 2, G, P], BF16)
            parts = mb("parts", [128, 2, 2, G, HEADS], BF16)
            ident_b = mb("ident_b", [128, 128], BF16)
            red = mb("red", [P, 2, HEADS])

            @block.gpsimd
            def _(pool):
                gather_groups(pool, ends, S.rows8, idx, rows, used, gathered, copied, go)

            @block.vector
            def _(dve):
                ch.eng = dve
                ch.link(dve.tensor_copy(ident_b[:], S.ident[:]))
                dve.sem_inc(consts, 1)
                for i in peeled(dve, ITERS):
                    c = ch.loop(i, 2 * (G + 4) + 4 * G)
                    for h in range(2):
                        at = bass.ds((2 * i + h) * G, G)
                        c.link(dve.tensor_copy(loc[:, h, :], local[:, at]))
                        for t in range(G):
                            c.step(dve.tensor_scalar(other_node[:, h, t, :], S.iota[:, 0:P], loc[:, h, t:t + 1], NEG,
                                                     ALU.not_equal, ALU.mult))
                        dve.wait_ge(gathered[h], (i + 1) * 16 * G)
                        c.link(dve.tensor_copy(parts[:, h, 0], rows[:, h]))
                        c.link(dve.tensor_tensor(rows[:, h], rows[:, h], parts[:, h, 0], ALU.subtract))
                        c.link(dve.tensor_copy(parts[:, h, 1], rows[:, h]))
                        dve.sem_inc(used[h], 1)
                        dve.sem_inc(prepared, 1)
                    for j in range(2 * G):
                        b = block_of(dve, blk, i, j // G, j % G)
                        dve.wait_ge(spread, i * 2 * G + j + 1)
                        k = 2 * (j % 4)
                        c.link(dve.tensor_reduce(
                            red[:, j % 2, :], S.ps[0:P, k:k + 2, :].rearrange("p k (h e) -> p (k h) e", e=128),
                            AX, ALU.max))
                        dve.sem_inc(reduced, 1)
                        here = at_block(most, b)
                        c.link(dve.tensor_tensor(here, here, red[:, j % 2, :], ALU.max))
                ch.after(c, ITERS)

            @block.tensor
            def _(pe):
                pe.wait_ge(consts, 1)
                for i in peeled(pe, ITERS):
                    for j in range(2 * G):
                        h, t, k = j // G, j % G, 2 * (j % 4)
                        if t == 0:
                            pe.wait_ge(prepared, 2 * i + h + 1)
                        if later(i) or j >= 4:
                            pe.wait_ge(reduced, i * 2 * G + j - 3)
                        for q in range(2):
                            pe.matmul(S.ps[0:P, k + q, :], other_node[:, h, t, :], bc_mid(ident_b[:], 4),
                                      start=True, stop=False, skip_group_check=True)
                        for hd in range(HEADS):
                            for part in range(2):
                                ins = pe.matmul(S.ps[0:P, k + hd // 4, (hd % 4) * 128:(hd % 4 + 1) * 128],
                                                parts[:, h, part, t, hd:hd + 1].to_broadcast([128, P]),
                                                ident_b[:], start=False, stop=part == 1, skip_group_check=True)
                        ins.then_inc(spread, 1)

        gathered = [sem(f"gathered{h}") for h in range(2)]
        used = [sem(f"used{h}") for h in range(2)]
        copied, go, selected, turned, turned_out, looked_up = (
            sem(x) for x in ("copied", "go", "selected", "turned", "turned_out", "looked_up"))
        shifted, weighted, scaled, summed, added, self_ready, self_exp, nodes_ready = (
            sem(x) for x in ("shifted", "weighted", "scaled", "summed", "added", "self_ready", "self_exp",
                             "nodes_ready"))
        with nc.Block() as block, ExitStack() as ctx:
            def mb(what, shape, dt=F32):
                return ctx.enter_context(nc.sbuf_tensor(f"gat_{what}2", shape, dt))

            idx, rows = mb("idx", [128, 2, G], I32), mb("rows", [128, 2, G, XG])
            loc = mb("loc", [128, 2, G])
            onehot, onehot_t = mb("onehot", [128, 2, G, P]), mb("onehot_t", [P, 2, G, 128])
            score = mb("score", [128, 2, G, HEADS])

            @block.gpsimd
            def _(pool):
                gather_groups(pool, ends, S.rows, idx, rows, used, gathered, copied, go)

            @block.vector
            def _(dve):
                ch.eng = dve
                ch.link(dve.tensor_tensor(most[:], most[:], node[:, :, 0:HEADS], ALU.add))
                leaky(ch, dve, node[:, :, HEADS:], most[:])
                ch.link(dve.tensor_tensor(self_e[:], a_src[:], node[:, :, 0:HEADS], ALU.add))
                leaky(ch, dve, self_e[:], self_e[:])
                ch.link(dve.tensor_tensor(self_e[:], self_e[:], node[:, :, HEADS:], ALU.subtract))
                dve.sem_inc(self_ready, 1)
                dve.wait_ge(self_exp, 1)
                v = S.acc[:, :, 0:D].rearrange("p t (h c) -> p t h c", h=HEADS)
                for t in range(NB):
                    ch.step(dve.tensor_tensor(v[:, t], v[:, t], bc(self_e[:, t, :], HC), ALU.mult))
                ch.link(dve.tensor_copy(S.acc[:, :, D:XG], self_e[:]))
                dve.sem_inc(nodes_ready, 1)
                for i in peeled(dve, ITERS):
                    c = ch.loop(i, 2 * (G + 1) + 2 * 5 + 2 * G)
                    for h in range(2):
                        c.link(dve.tensor_copy(loc[:, h, :], local[:, bass.ds((2 * i + h) * G, G)]))
                        for t in range(G):
                            c.step(dve.tensor_scalar(onehot[:, h, t, :], S.iota[:, 0:P], loc[:, h, t:t + 1], None,
                                                     ALU.is_equal))
                        c.sync()
                        dve.sem_inc(selected, 1)
                    for h in range(2):
                        dve.wait_ge(gathered[h], (i + 1) * 16 * G)
                        dve.wait_ge(looked_up, 2 * i + h + 1)
                        of_node = S.ps[:, 6 + h, 0:128].rearrange("e (t c) -> e t c", t=G)
                        c.link(dve.tensor_tensor(score[:, h], rows[:, h, :, D:XG], of_node[:, :, 0:HEADS], ALU.add))
                        leaky(c, dve, score[:, h], score[:, h])
                        c.link(dve.tensor_tensor(score[:, h], score[:, h], of_node[:, :, HEADS:], ALU.subtract))
                        c.link(dve.tensor_scalar(score[:, h], score[:, h], 60.0, None, ALU.min))
                        dve.sem_inc(shifted, 1)
                        dve.wait_ge(weighted, 2 * i + h + 1)
                        v = rows[:, h, :, 0:D].rearrange("e t (h c) -> e t h c", h=HEADS)
                        wt = rows[:, h, :, D:XG].unsqueeze(3).to_broadcast([128, G, HEADS, HC])
                        c.link(dve.tensor_tensor(v, v, wt, ALU.mult))
                        dve.sem_inc(scaled, 1)
                    for j in range(2 * G):
                        b = block_of(dve, blk, i, j // G, j % G)
                        dve.wait_ge(summed, i * 2 * G + j + 1)
                        here = at_block(S.acc, b)
                        c.link(dve.tensor_tensor(here, here, S.ps[0:P, j % 4, 0:XG], ALU.add))
                        dve.sem_inc(added, 1)
                        if j % G == G - 1:
                            dve.sem_inc(used[j // G], 1)
                ch.after(c, ITERS)

            @block.scalar
            def _(act):
                act.wait_ge(self_ready, 1)
                act.activation(self_e[:], self_e[:], ACT.Exp).then_inc(self_exp, 1)
                for i in peeled(act, ITERS):
                    for h in range(2):
                        act.wait_ge(turned, 2 * i + h + 1)
                        act.copy(onehot_t[:, h], S.ps[0:P, 4:6, :].rearrange("p k (t e) -> p (k t) e", e=128))\
                           .then_inc(turned_out, 1)
                    for h in range(2):
                        act.wait_ge(shifted, 2 * i + h + 1)
                        act.activation(rows[:, h, :, D:XG], score[:, h], ACT.Exp).then_inc(weighted, 1)

            @block.tensor
            def _(pe):
                pe.wait_ge(nodes_ready, 1)
                for i in peeled(pe, ITERS):
                    for h in range(2):
                        pe.wait_ge(selected, 2 * i + h + 1)
                        if later(i) or h:
                            pe.wait_ge(turned_out, 2 * i + h)
                        for t in range(G):
                            ins = pe.transpose(S.ps[0:P, 4 + t // 4, (t % 4) * 128:(t % 4 + 1) * 128],
                                               onehot[:, h, t, :], S.ident[:])
                        ins.then_inc(turned, 1)
                    for h in range(2):
                        pe.wait_ge(turned_out, 2 * i + h + 1)
                        for t in range(G):
                            b = block_of(pe, blk, i, h, t)
                            ins = pe.matmul(S.ps[:, 6 + h, t * 16:(t + 1) * 16],
                                            onehot_t[:, h, t, :], at_block(node, b), start=True, stop=True)
                        ins.then_inc(looked_up, 1)
                    for j in range(2 * G):
                        h, t = j // G, j % G
                        if t == 0:
                            pe.wait_ge(scaled, 2 * i + h + 1)
                        if later(i) or j >= 4:
                            pe.wait_ge(added, i * 2 * G + j - 3)
                        ins = pe.matmul(S.ps[0:P, j % 4, 0:XG], onehot[:, h, t, :], rows[:, h, t, :],
                                        start=True, stop=True)
                        ins.then_inc(summed, 1)

        var_ready, root_ready = sem("var_ready"), sem("root_ready")
        with nc.Block() as block, ExitStack() as ctx:
            stats = ctx.enter_context(nc.sbuf_tensor("gat_stats", [P, NB, 6], F32))
            mv = ctx.enter_context(nc.sbuf_tensor("gat_mv", [P, NB, 2], F32))
            var, root, inv = (ctx.enter_context(nc.sbuf_tensor(f"gat_{x}", [P, NB], F32)) for x in ("var", "root", "inv"))

            @block.scalar
            def _(act):
                act.wait_ge(var_ready, 1)
                act.activation(root[:], var[:], ACT.Sqrt).then_inc(root_ready, 1)

            @block.vector
            def _(dve):
                ch.eng = dve
                ch.link(dve.reciprocal(self_e[:], S.acc[:, :, D:XG]))
                v = S.acc[:, :, 0:D].rearrange("p t (h c) -> p t h c", h=HEADS)
                for t in range(NB):
                    ch.step(dve.tensor_tensor(v[:, t], v[:, t], bc(self_e[:, t, :], HC), ALU.mult))
                ch.sync()
                y = S.acc[:, :, 0:D]
                ch.link(dve.tensor_tensor(y, y, bc_mid(bias[:], NB), ALU.add))
                ch.link(dve.tensor_tensor(y, y, S.xn[:], ALU.add))
                norm_into(ch, dve, S, y, stats, mv, var, root, inv, var_ready, root_ready)
                ch.link(dve.tensor_tensor(y, y, bc_mid(ln_w[:], NB), ALU.mult))
                ch.link(dve.tensor_tensor(S.x[:], S.x[:], bc_mid(ln_b[:], NB), ALU.add))
                ch.link(dve.tensor_tensor(S.x[:], S.x[:], y, ALU.add))


def norm_into(ch, dve, S, y, stats, mv, var, root, inv, var_ready, root_ready):
    for t in range(NB):
        ch.step(dve.bn_stats(stats[:, t, :], y[:, t, :]))
    ch.sync()
    for t in range(NB):
        ch.step(dve.bn_aggr(mv[:, t, :], stats[:, t, :]))
    ch.sync()
    inverse_root(ch, dve, S, mv[:, :, 1], EPS, var, root, inv, var_ready, root_ready)
    for t in range(NB):
        ch.step(dve.tensor_scalar(y[:, t, :], y[:, t, :], mv[:, t, 0:1], inv[:, t:t + 1],
                                  ALU.subtract, ALU.mult))
    ch.sync()


def expert_weights(nc, S, A, name, n, rule, weights, bias, comb, comb_t, b2=None, target=None, base=None):
    with phase(nc, name) as (sb, sem):
        w = sb("w", [128, K, n])
        b_row = sb("b_row", [P, n]) if bias is not None else None
        b2_s = sb("b2", [n, D]) if b2 is not None else None
        logits, ex = sb("logits", [P, NB, n]), sb("ex", [P, NB, n])
        best, best_at, at_f = sb("best", [P, NB, 8]), sb("best_at", [P, NB, 8], mybir.dt.uint32), sb("at_f", [P, NB, 2])
        col, pair = sb("col", [P, NB]), sb("pair", [P, NB, 2])
        dve_step, act_step = sem("dve_step"), sem("act_step")
        loaded, product, exp_ready, exp_done, combined, turned, emptied, biased, added = (
            sem(x) for x in ("loaded", "product", "exp_ready", "exp_done", "combined", "turned", "emptied",
                             "biased", "added"))
        n_loads = 1 + (bias is not None) + (b2 is not None)
        per_bank = 512 // n
        nbanks = -(-NB // per_bank)
        with nc.Block() as block:
            @block.sync
            def _(sp):
                sp.dma_start(w[:], weights.rearrange("(k p) e -> p k e", p=128)).then_inc(loaded, 16)
                if bias is not None:
                    sp.dma_start(b_row[:], row(bias)).then_inc(loaded, 16)
                if b2 is not None:
                    sp.dma_start(b2_s[:], b2).then_inc(loaded, 16)
                sp.wait_ge(loaded, 16 * n_loads)

            @block.tensor
            def _(pe):
                pe.wait_ge(loaded, 16 * n_loads)
                for t in range(NB):
                    bank, at = t // per_bank, (t % per_bank) * n
                    for k in range(K):
                        ins = pe.matmul(S.ps[0:P, bank, at:at + n], S.xT[:, k, t * P:(t + 1) * P], w[:, k, :],
                                        start=k == 0, stop=k == K - 1)
                    ins.then_inc(product, 1)
                pe.wait_ge(combined, 1)
                for t in range(NB):
                    if t >= 2:
                        pe.wait_ge(emptied, t - 1)
                    pe.transpose(S.ps[0:n, 2 + t % 2, 0:P], comb[:, t, :], S.ident[0:P, 0:P]).then_inc(turned, 1)
                    if b2 is not None:
                        pe.wait_ge(emptied, t + 1)
                        if t >= 4:
                            pe.wait_ge(added, t - 3)
                        pe.matmul(S.ps[0:P, 4 + t % 4, 0:D], comb_t[0:n, t * P:(t + 1) * P], b2_s[:],
                                  start=True, stop=True).then_inc(biased, 1)

            @block.scalar
            def _(act):
                if rule != "top1":
                    act.wait_ge(exp_ready, 1)
                    src = pair if rule == "gates" else ex
                    act.activation(src[:], src[:], ACT.Exp).then_inc(exp_done, 1)
                for t in range(NB):
                    act.wait_ge(turned, t + 1)
                    act.copy(comb_t[0:n, t * P:(t + 1) * P], S.ps[0:n, 2 + t % 2, 0:P]).then_inc(emptied, 1)

            @block.vector
            def _(dve):
                ch = Chain(dve, dve_step)
                dve.wait_ge(product, NB)
                for b in range(nbanks):
                    t0, t1 = b * per_bank, min(NB, (b + 1) * per_bank)
                    src = S.ps[0:P, b, 0:(t1 - t0) * n].rearrange("p (t e) -> p t e", e=n)
                    if bias is not None:
                        dve.wait_ge(loaded, 16 * n_loads)
                        ch.step(dve.tensor_tensor(logits[:, t0:t1, :], src, bc_mid(b_row[:], t1 - t0), ALU.add))
                    else:
                        ch.step(dve.tensor_copy(logits[:, t0:t1, :], src))
                ch.sync()
                ranked = logits
                if rule in ("top2", "soft"):
                    ch.link(dve.tensor_reduce(col[:], logits[:], AX, ALU.max))
                    ch.link(dve.tensor_tensor(ex[:], logits[:], bc(col[:], n), ALU.subtract))
                    dve.sem_inc(exp_ready, 1)
                    dve.wait_ge(exp_done, 1)
                    ch.link(dve.tensor_reduce(col[:], ex[:], AX, ALU.add))
                    ch.link(dve.reciprocal(col[:], col[:]))
                    out = comb if rule == "soft" else ex
                    ch.link(dve.tensor_tensor(out[:], ex[:], bc(col[:], n), ALU.mult))
                    ranked = ex
                if rule != "soft":
                    for t in range(NB):
                        ch.step(dve.max(best[:, t, :], ranked[:, t, :]))
                    ch.sync()
                    for t in range(NB):
                        ch.step(dve.max_index(best_at[:, t, :], best[:, t, :], ranked[:, t, :]))
                    ch.sync()
                    ch.link(dve.tensor_copy(at_f[:], best_at[:, :, 0:2]))
                    if rule == "gates":
                        ch.link(dve.tensor_tensor(pair[:], best[:, :, 0:2], bc(best[:, :, 0], 2), ALU.subtract))
                        dve.sem_inc(exp_ready, 1)
                        dve.wait_ge(exp_done, 1)
                    elif rule == "top2":
                        ch.link(dve.tensor_copy(pair[:], best[:, :, 0:2]))
                    if rule != "top1":
                        ch.link(dve.tensor_tensor(col[:], pair[:, :, 0], pair[:, :, 1], ALU.add))
                        ch.link(dve.tensor_scalar(col[:], col[:], 1e-12, None, ALU.max))
                        ch.link(dve.reciprocal(col[:], col[:]))
                        ch.link(dve.tensor_tensor(pair[:], pair[:], bc(col[:], 2), ALU.mult))
                    ids = bc_mid(S.iota[0:P, 0:n], NB)
                    ch.link(dve.tensor_tensor(comb[:], ids, bc(at_f[:, :, 0], n), ALU.is_equal))
                    if rule != "top1":
                        ch.link(dve.tensor_tensor(comb[:], comb[:], bc(pair[:, :, 0], n), ALU.mult))
                        ch.link(dve.tensor_tensor(logits[:], ids, bc(at_f[:, :, 1], n), ALU.is_equal))
                        ch.link(dve.tensor_tensor(logits[:], logits[:], bc(pair[:, :, 1], n), ALU.mult))
                        ch.link(dve.tensor_tensor(comb[:], comb[:], logits[:], ALU.add))
                dve.sem_inc(combined, 1)
                if b2 is not None:
                    if base is not None and not isinstance(base, str):
                        ch.link(dve.tensor_tensor(target, target, base, ALU.add))
                    for t in range(NB):
                        dve.wait_ge(biased, t + 1)
                        src = S.ps[0:P, 4 + t % 4, 0:D]
                        if base is not None:
                            ins = dve.tensor_tensor(target[:, t, :], target[:, t, :], src, ALU.add)
                        else:
                            ins = dve.tensor_copy(target[:, t, :], src)
                        ins.then_inc(added, 1)


def bank_before(m, banks, per):
    return m - banks if m >= banks else max(n for n in range(per) if n % banks == m % banks) - per


def experts(nc, S, name, steps, w_first, w_second, w_last, F, act_first, act_second, comb, target,
            masked=None):
    KF = F // 128
    deep = w_second is not None
    BANKS = 2 if (deep or masked is not None) else 4
    with phase(nc, name) as (sb, sem):
        w1, w2 = sb("w1", [128, 2, K, F]), sb("w2", [128, 2, KF, D])
        wm = sb("wm", [128, 2, KF, F]) if deep else None
        hid = sb("hid", [128, 2, KF, CH * P])
        hid2 = sb("hid2", [128, 2, KF, CH * P]) if deep else None
        consts = sb("consts", [128, 2, len(act_first.tables) + len(act_second.tables if deep else ()), KF])
        fetched, go, pe_go = sem("constants_fetched"), sem("go"), sem("pe_go")
        loaded = [sem(f"weights_loaded{h}") for h in range(2)]
        done = [sem(f"weights_used{h}") for h in range(2)]
        first, hidden, middle, hidden2, last, added, masks, masked_sem = (
            sem(x) for x in ("first", "hidden", "middle", "hidden2", "last", "added", "masks", "masked"))
        LOADS = 2 if not deep and masked is None else 3
        PER = steps // 2
        items = [(h, c) for h in range(2) for c in range(NCHUNK)]
        NI = len(items)

        def cols(c):
            return CH * c * P, len(chunk_blocks(c)) * P

        with nc.Block() as block:
            @block.sync
            def _(sp):
                for i in peeled(sp, PER):
                    for h in range(2):
                        if later(i):
                            sp.wait_ge(done[h], i)
                        e = 2 * i + h
                        if masked is not None:
                            for j in range(2):
                                sp.dma_start(w1[:, h, :, j * 64:(j + 1) * 64], w_first(e)[:, j]).then_inc(loaded[h], 16)
                        else:
                            sp.dma_start(w1[:, h], w_first(e)).then_inc(loaded[h], 16)
                        if deep:
                            sp.dma_start(wm[:, h], w_second(e)).then_inc(loaded[h], 16)
                        sp.dma_start(w2[:, h], w_last(e)).then_inc(loaded[h], 16)

            @block.tensor
            def _(pe):
                def stage_first(i, j):
                    h, c = items[j]
                    at, width = cols(c)
                    if c == 0:
                        pe.wait_ge(loaded[h], (i + 1) * 16 * LOADS)
                    for f in range(KF):
                        m = j * KF + f
                        if later(i) or m >= BANKS:
                            pe.wait_ge(hidden, i * NI * KF + m - BANKS + 1)
                        for k in range(K):
                            ins = pe.matmul(S.ps[:, m % BANKS, 0:width], w1[:, h, k, f * 128:(f + 1) * 128],
                                            S.xT[:, k, at:at + width], start=k == 0, stop=k == K - 1)
                        ins.then_inc(first, 1)
                    if masked is not None:
                        sel, comb_b = masked
                        if later(i) or j >= 2:
                            pe.wait_ge(masked_sem, i * NI + j - 1)
                            pe.sem_inc(pe_go, 1)
                        which = (2 * i + h) if later(i) else h
                        pe.matmul(S.ps[:, 2 + j % 2, 0:width],
                                  sel[:, bass.ds(which, 1), :].rearrange("e a p -> e (a p)"),
                                  comb_b[:, at:at + width], start=True, stop=True).then_inc(masks, 1)

                def stage_middle(i, j):
                    h, c = items[j]
                    at, width = cols(c)
                    pe.wait_ge(hidden, i * NI * KF + (j + 1) * KF)
                    for f in range(KF):
                        m = j * KF + f
                        if later(i) or m >= 2:
                            pe.wait_ge(hidden2, i * NI * KF + m - 1)
                        for k in range(KF):
                            ins = pe.matmul(S.ps[:, 2 + m % 2, 0:width], wm[:, h, k, f * 128:(f + 1) * 128],
                                            hid[:, j % 2, k, 0:width], start=k == 0, stop=k == KF - 1)
                        ins.then_inc(middle, 1)

                def stage_last(i, j):
                    h, c = items[j]
                    src = hid2 if deep else hid
                    if masked is not None:
                        pe.wait_ge(masked_sem, i * NI + j + 1)
                    else:
                        pe.wait_ge(hidden2 if deep else hidden, i * NI * KF + (j + 1) * KF)
                    for n, t in enumerate(chunk_blocks(c)):
                        m = h * NB + t
                        if later(i) or m >= 4:
                            pe.wait_ge(added, i * 2 * NB + bank_before(m, 4, 2 * NB) + 1)
                        for k in range(KF):
                            ins = pe.matmul(S.ps[0:P, 4 + m % 4, 0:D], src[:, j % 2, k, n * P:(n + 1) * P],
                                            w2[:, h, k, :], start=k == 0, stop=k == KF - 1)
                        ins.then_inc(last, 1)

                lag = 2 if deep else 1
                for i in peeled(pe, PER):
                    for s in range(NI + lag):
                        if s < NI:
                            stage_first(i, s)
                        if deep and 1 <= s <= NI:
                            stage_middle(i, s - 1)
                        if s >= lag:
                            stage_last(i, s - lag)

            @block.scalar
            def _(act):
                def layer(i, j, src_sem, out_sem, out, bank0, fn, n0, free_after):
                    h, c = items[j]
                    at, width = cols(c)
                    for f in range(KF):
                        m = j * KF + f
                        act.wait_ge(src_sem, i * NI * KF + m + 1)
                        if f == 0 and (later(i) or j >= 2):
                            free_after(i, j)
                        mine = [consts[:, h, n0 + n, f:f + 1] for n in range(len(fn.tables))]
                        fn.apply(act, out[:, j % 2, f, 0:width],
                                 S.ps[:, bank0 + m % (BANKS if bank0 == 0 else 2), 0:width],
                                 mine).then_inc(out_sem, 1)

                def products_over(i, j):
                    h, c = items[j - 2] if j >= 2 else items[NI - 2 + j]
                    upto = h * NB + chunk_blocks(c)[-1] + 1
                    act.wait_ge(last, (i * 2 * NB + upto) if j >= 2 else (i * 2 * NB - 2 * NB + upto))

                def middle_over(i, j):
                    act.wait_ge(middle, i * NI * KF + (j - 1) * KF)

                def fetch(i, h):
                    e = 2 * i + h
                    if later(i):
                        act.wait_ge(hidden2 if deep else hidden, i * NI * KF - NI * KF + (h + 1) * NCHUNK * KF)
                        act.sem_inc(go, 1)
                    tables = act_first.tables + (act_second.tables if deep else [])
                    for n, (table, at) in enumerate(tables):
                        src = table[:, bass.ds(e * KF + at, KF)] if later(i) else table[:, at + e * KF:at + (e + 1) * KF]
                        ins = act.copy(consts[:, h, n, :], src)
                        ins.then_inc(fetched, 1)
                    act.wait_ge(fetched, (2 * i + h + 1) * len(tables))

                for i in peeled(act, PER):
                    for s in range(NI + (1 if deep else 0)):
                        if s < NI and items[s][1] == 0:
                            fetch(i, items[s][0])
                        if s < NI:
                            layer(i, s, first, hidden, hid, 0, act_first, 0, middle_over if deep else products_over)
                        if deep and s >= 1:
                            layer(i, s - 1, middle, hidden2, hid2, 2, act_second,
                                  len(act_first.tables), products_over)

            @block.vector
            def _(dve):
                def mask(i, j):
                    at, width = cols(items[j][1])
                    dve.wait_ge(masks, i * NI + j + 1)
                    dve.wait_ge(hidden, i * NI + j + 1)
                    v = hid[:, j % 2, 0, 0:width]
                    dve.tensor_tensor(v, v, S.ps[:, 2 + j % 2, 0:width], ALU.mult).then_inc(masked_sem, 1)

                for i in peeled(dve, PER):
                    for j in range(NI + (1 if masked is not None else 0)):
                        if masked is not None and j < NI:
                            mask(i, j)
                        jj = j - 1 if masked is not None else j
                        if jj < 0:
                            continue
                        h, c = items[jj]
                        e = 2 * i + h
                        for t in chunk_blocks(c):
                            m = h * NB + t
                            dve.wait_ge(last, i * 2 * NB + m + 1)
                            src, dst = S.ps[0:P, 4 + m % 4, 0:D], target[:, t, 0:D]
                            if later(i) or m >= NB:
                                dve.wait_ge(added, i * 2 * NB + m - NB + 1)
                            if masked is not None:
                                ins = dve.tensor_tensor(dst, dst, src, ALU.add)
                            else:
                                ins = dve.scalar_tensor_tensor(
                                    dst, src, comb[:, t, bass.ds(e, 1)] if later(i) else comb[:, t, e:e + 1],
                                    dst, ALU.mult, ALU.add)
                            ins.then_inc(added, 1)
                            if t == NB - 1:
                                dve.sem_inc(done[h], 1)


class Layer:

    def __init__(self, function, bias, scale=None):
        self.function, self.tables = function, [bias] + ([scale] if scale else [])

    def apply(self, act, out, in_, mine):
        scale = {"scale": mine[1]} if len(mine) > 1 else {}
        return act.activation(out, in_, self.function, bias=mine[0], **scale)


def by_expert(w):
    return lambda e: (w[e] if isinstance(e, int) else w[bass.ds(e, 1)].rearrange("a k f -> (a k) f"))\
        .rearrange("(k p) f -> p k f", p=128)


def ffn0(nc, S, A):
    with phase(nc, "ffn0") as (sb, sem):
        comb, comb_t = sb("comb", [P, NB, 8]), sb("comb_t", [8, N])
        expert_weights(nc, S, A, "route0", 8, "top2", S.turned["L0_ffn_router_w"], None, comb, comb_t,
                       b2=A["L0_ffn_b2"], target=S.x[:], base=S.xn[:])
        experts(nc, S, "experts0", 8, by_expert(A["L0_ffn_w1"]), None, by_expert(A["L0_ffn_w2"]), 256,
                Layer(ACT.Gelu, (S.pcol, S.column["L0_ffn_b1"])), None, comb, S.x)


def one_hots(c, dve, S, onehot, loc, local, at, h):
    c.link(dve.tensor_copy(loc[:, h, :], local[:, at]))
    for t in range(G):
        c.step(dve.tensor_scalar(onehot[:, h, t, :], S.iota[:, 0:P], loc[:, h, t:t + 1], None, ALU.is_equal))
    c.sync()


def mpnn(nc, S, A):
    ends, local, blk = S.end["src"], S.local["src"], S.blk["src"]
    w1t = S.turned["L1_gnn_W1"]
    with phase(nc, "mpnn") as (sb, sem):
        dve_step = sem("dve_step")
        ch = Chain(None, dve_step)
        own = sb("own", [P, NB, D])
        w1c = sb("w1c", [ED, D])
        loaded, product, out_own, out_other, stored = (
            sem(x) for x in ("loaded", "product", "out_own", "out_other", "stored"))
        with nc.Block() as block, ExitStack() as ctx:
            w1 = ctx.enter_context(nc.sbuf_tensor("mpnn_w1", [128, 2, K, D], F32))
            b1 = ctx.enter_context(nc.sbuf_tensor("mpnn_b1", [P, D], F32))

            @block.sync
            def _(sp):
                for j in range(2):
                    sp.dma_start(w1[:, j], w1t[j * D:(j + 1) * D, :].rearrange("(k p) f -> p k f", p=128))\
                      .then_inc(loaded, 16)
                sp.dma_start(w1c[:], w1t[2 * D:2 * D + ED, :]).then_inc(loaded, 16)
                sp.dma_start(b1[:], row(A["L1_gnn_b1"])).then_inc(loaded, 16)
                sp.wait_ge(loaded, 64)
                sp.wait_ge(out_other, NB)
                sp.dma_start(S.rows_b.rearrange("(t p) c -> p t c", p=P), S.acc[:, :, 0:D]).then_inc(stored, 16)
                sp.wait_ge(stored, 16)

            @block.tensor
            def _(pe):
                pe.wait_ge(loaded, 64)
                for t in range(NB):
                    if t >= 4:
                        pe.wait_ge(out_own, t - 3)
                        pe.wait_ge(out_other, t - 3)
                    for j in range(2):
                        for k in range(K):
                            ins = pe.matmul(S.ps[0:P, 2 * (t % 4) + j, 0:D], S.xT[:, k, t * P:(t + 1) * P],
                                            w1[:, j, k, :], start=k == 0, stop=k == K - 1)
                    ins.then_inc(product, 1)

            @block.scalar
            def _(act):
                for t in range(NB):
                    act.wait_ge(product, t + 1)
                    act.copy(S.acc[:, t, 0:D], S.ps[0:P, 2 * (t % 4) + 1, 0:D]).then_inc(out_other, 1)

            @block.vector
            def _(dve):
                dve.wait_ge(loaded, 64)
                for t in range(NB):
                    dve.wait_ge(product, t + 1)
                    dve.tensor_tensor(own[:, t, :], S.ps[0:P, 2 * (t % 4), 0:D], b1[:], ALU.add).then_inc(out_own, 1)

        gathered = [sem(f"gathered{h}") for h in range(2)]
        used = [sem(f"used{h}") for h in range(2)]
        attr_in = [sem(f"attributes{h}") for h in range(2)]
        (copied, go, selected, turned, turned_out, products, messages, rectified, summed, added, ready) = (
            sem(x) for x in ("copied", "go", "selected", "turned", "turned_out", "products", "messages",
                             "rectified", "summed", "added", "ready"))
        with nc.Block() as block, ExitStack() as ctx:
            def mb(what, shape, dt=F32):
                return ctx.enter_context(nc.sbuf_tensor(f"mpnn_{what}", shape, dt))

            idx, rows = mb("idx", [128, 2, G], I32), mb("rows", [128, 2, G, D + 1])
            attr, attr_t = mb("attr", [128, 2, G, 2 + ED]), mb("attr_t", [ED, 2, G, 128])
            loc = mb("loc", [128, 2, G])
            onehot, onehot_t = mb("onehot", [128, 2, G, P]), mb("onehot_t", [P, 2, G, 128])
            view = S.records["src"].rearrange("(p t) w -> p t w", p=128)

            @block.sync
            def _(sp):
                for i in peeled(sp, ITERS):
                    for h in range(2):
                        if later(i):
                            sp.wait_ge(turned_out, 2 * (2 * i - 2 + h) + 2)
                        sp.dma_start(attr[:, h], view[:, bass.ds((2 * i + h) * G, G), :]).then_inc(attr_in[h], 16)

            @block.gpsimd
            def _(pool):
                gather_groups(pool, ends, S.rows_b, idx, rows[:, :, :, 0:D], used, gathered, copied, go)

            @block.vector
            def _(dve):
                ch.eng = dve
                ch.step(dve.memset(S.acc[:], 0.0))
                ch.link(dve.memset(rows[:, :, :, D:D + 1], 1.0))
                dve.sem_inc(ready, 1)
                for i in peeled(dve, ITERS):
                    c = ch.loop(i, 2 * (G + 1) + 2 * G)
                    for h in range(2):
                        one_hots(c, dve, S, onehot, loc, local, bass.ds((2 * i + h) * G, G), h)
                        dve.sem_inc(selected, 1)
                    for j in range(2 * G):
                        h, t = j // G, j % G
                        if t == 0:
                            dve.wait_ge(gathered[h], (i + 1) * 16 * G)
                        dve.wait_ge(products, i * 2 * G + j + 1)
                        v = rows[:, h, t, 0:D]
                        dve.tensor_tensor(v, v, S.ps[:, 2 + j % 2, 0:D], ALU.add).then_inc(messages, 1)
                    for j in range(2 * G):
                        b = block_of(dve, blk, i, j // G, j % G)
                        dve.wait_ge(summed, i * 2 * G + j + 1)
                        here = S.acc[:, bass.ds(b, 1), 0:D + 1].rearrange("p a c -> p (a c)")
                        c.link(dve.tensor_tensor(here, here, S.ps[0:P, j % 2, 0:D + 1], ALU.add))
                        dve.sem_inc(added, 1)
                        if j % G == G - 1:
                            dve.sem_inc(used[j // G], 1)
                ch.after(c, ITERS)

            @block.scalar
            def _(act):
                for i in peeled(act, ITERS):
                    for h in range(2):
                        act.wait_ge(turned, 2 * i + h + 1)
                        act.copy(onehot_t[:, h], S.ps[0:P, 4:6, :].rearrange("p k (t e) -> p (k t) e", e=128))\
                           .then_inc(turned_out, 1)
                        act.copy(attr_t[:, h], S.ps[0:ED, 6:8, :].rearrange("p k (t e) -> p (k t) e", e=128))\
                           .then_inc(turned_out, 1)
                    for j in range(4):
                        h, t = j // 2, (j % 2) * (G // 2)
                        act.wait_ge(messages, i * 2 * G + (j + 1) * (G // 2))
                        v = rows[:, h, t:t + G // 2, 0:D]
                        act.activation(v, v, ACT.Relu).then_inc(rectified, 1)

            @block.tensor
            def _(pe):
                pe.wait_ge(ready, 1)
                for i in peeled(pe, ITERS):
                    for h in range(2):
                        pe.wait_ge(selected, 2 * i + h + 1)
                        pe.wait_ge(attr_in[h], (i + 1) * 16)
                        if later(i) or h:
                            pe.wait_ge(turned_out, 2 * (2 * i + h))
                        for t in range(G):
                            pe.transpose(S.ps[0:P, 4 + t // 4, (t % 4) * 128:(t % 4 + 1) * 128],
                                         onehot[:, h, t, :], S.ident[:])
                            ins = pe.transpose(S.ps[0:ED, 6 + t // 4, (t % 4) * 128:(t % 4 + 1) * 128],
                                               attr[:, h, t, 2:2 + ED], S.ident[:])
                        ins.then_inc(turned, 1)
                    for j in range(2 * G):
                        h, t = j // G, j % G
                        if t == 0:
                            pe.wait_ge(turned_out, 2 * (2 * i + h) + 2)
                        b = block_of(pe, blk, i, h, t)
                        if later(i) or j >= 2:
                            pe.wait_ge(messages, i * 2 * G + j - 1)
                        pe.matmul(S.ps[:, 2 + j % 2, 0:D], onehot_t[:, h, t, :], at_block(own, b),
                                  start=True, stop=False)
                        pe.matmul(S.ps[:, 2 + j % 2, 0:D], attr_t[:, h, t, :], w1c[:],
                                  start=False, stop=True).then_inc(products, 1)
                    for j in range(2 * G):
                        h, t = j // G, j % G
                        if t % (G // 2) == 0:
                            pe.wait_ge(rectified, 4 * i + j // (G // 2) + 1)
                        if later(i) or j >= 2:
                            pe.wait_ge(added, i * 2 * G + j - 1)
                        pe.matmul(S.ps[0:P, j % 2, 0:D + 1], onehot[:, h, t, :], rows[:, h, t, :],
                                  start=True, stop=True).then_inc(summed, 1)
        gru(nc, S, A)


def gru(nc, S, A):
    with phase(nc, "gru") as (sb, sem):
        w2, wi, wh = sb("w2", [128, K, D]), sb("wi", [128, K, 3 * D]), sb("wh", [128, K, 3 * D])
        b2, bi, bh = sb("b2", [1, D]), sb("bi", [P, 3 * D]), sb("bh", [P, 3 * D])
        b_rz, b_n = sb("b_rz", [P, 2 * D]), sb("b_n", [P, 2 * D])
        sums_t, degree = sb("sums_t", [128, 2, K, P]), sb("degree", [1, 2, P])
        agg = sb("agg", [128, 2, K, P])
        rz, nn = sb("rz", [P, 3, 2 * D]), sb("nn", [P, 3, 2 * D])
        (loaded, dve_step, turned, turned_out, aggregated, agg_out, gates, gates_out, sig, cand, tanh) = (
            sem(x) for x in ("loaded", "dve_step", "turned", "turned_out", "aggregated", "agg_out", "gates",
                             "gates_out", "sigmoids", "candidates", "tanhs"))
        with nc.Block() as block:
            @block.sync
            def _(sp):
                for dst, n in ((w2, "L1_gnn_W2"), (wi, "L1_gnn_W_ih"), (wh, "L1_gnn_W_hh")):
                    sp.dma_start(dst[:], S.turned[n].rearrange("(k p) f -> p k f", p=128)).then_inc(loaded, 16)
                sp.dma_start(b2[:], A["L1_gnn_b2"].rearrange("(a d) -> a d", a=1)).then_inc(loaded, 16)
                sp.dma_start(bi[:], row(A["L1_gnn_b_ih"])).then_inc(loaded, 16)
                sp.dma_start(bh[:], row(A["L1_gnn_b_hh"])).then_inc(loaded, 16)
                sp.wait_ge(loaded, 96)

            @block.tensor
            def _(pe):
                pe.wait_ge(loaded, 96)
                for s in range(NB + 2):
                    if s < NB:
                        if s >= 2:
                            pe.wait_ge(turned_out, 2 * (s - 1))
                        for k in range(K):
                            pe.transpose(S.ps[:, s % 2, k * P:(k + 1) * P], S.acc[:, s, k * 128:(k + 1) * 128],
                                         S.ident[0:P, 0:P])
                        pe.transpose(S.ps[0:1, s % 2, K * P:(K + 1) * P], S.acc[:, s, D:D + 1],
                                     S.ident[0:P, 0:P]).then_inc(turned, 1)
                    if 1 <= s <= NB:
                        t = s - 1
                        pe.wait_ge(turned_out, 2 * (t + 1))
                        if t >= 2:
                            pe.wait_ge(agg_out, t - 1)
                        for f in range(K):
                            o = S.ps[:, 2 + t % 2, f * P:(f + 1) * P]
                            for k in range(K):
                                pe.matmul(o, w2[:, k, f * 128:(f + 1) * 128], sums_t[:, t % 2, k, :],
                                          start=k == 0, stop=False)
                            ins = pe.matmul(o, b2[0:1, f * 128:(f + 1) * 128], degree[0:1, t % 2, :],
                                            start=False, stop=True)
                        ins.then_inc(aggregated, 1)
                    if s >= 2:
                        t = s - 2
                        pe.wait_ge(agg_out, t + 1)
                        if t >= 2:
                            pe.wait_ge(gates_out, 2 * (t - 1))
                        q = 4 + 2 * (t % 2)
                        hx = S.xT[:, :, t * P:(t + 1) * P]
                        for k in range(K):
                            pe.matmul(S.ps[0:P, q, :], agg[:, t % 2, k, :], wi[:, k, 0:2 * D], start=k == 0, stop=False)
                        for k in range(K):
                            pe.matmul(S.ps[0:P, q, :], hx[:, k], wh[:, k, 0:2 * D], start=False, stop=k == K - 1)
                        for k in range(K):
                            pe.matmul(S.ps[0:P, q + 1, 0:D], agg[:, t % 2, k, :], wi[:, k, 2 * D:], start=k == 0,
                                      stop=k == K - 1)
                        for k in range(K):
                            ins = pe.matmul(S.ps[0:P, q + 1, D:2 * D], hx[:, k], wh[:, k, 2 * D:], start=k == 0,
                                            stop=k == K - 1)
                        ins.then_inc(gates, 1)

            @block.scalar
            def _(act):
                for s in range(NB + 4):
                    if s < NB:
                        act.wait_ge(turned, s + 1)
                        if s >= 2:
                            act.wait_ge(aggregated, s - 1)
                        act.copy(sums_t[:, s % 2], S.ps[:, s % 2, 0:K * P].rearrange("p (k n) -> p k n", k=K))\
                           .then_inc(turned_out, 1)
                        act.copy(degree[:, s % 2, :], S.ps[0:1, s % 2, K * P:(K + 1) * P]).then_inc(turned_out, 1)
                    if 1 <= s <= NB:
                        t = s - 1
                        act.wait_ge(aggregated, t + 1)
                        if t >= 2:
                            act.wait_ge(gates, t - 1)
                        act.copy(agg[:, t % 2], S.ps[:, 2 + t % 2, 0:K * P].rearrange("p (k n) -> p k n", k=K))\
                           .then_inc(agg_out, 1)
                    if 3 <= s < NB + 3:
                        t = s - 3
                        act.wait_ge(gates_out, 2 * (t + 1))
                        act.activation(rz[:, t % 3, :], rz[:, t % 3, :], ACT.Sigmoid).then_inc(sig, 1)
                    if s >= 4:
                        t = s - 4
                        act.wait_ge(cand, t + 1)
                        act.activation(nn[:, t % 3, 0:D], nn[:, t % 3, 0:D], ACT.Tanh).then_inc(tanh, 1)

            @block.vector
            def _(dve):
                ch = Chain(dve, dve_step)
                dve.wait_ge(loaded, 96)
                ch.step(dve.tensor_tensor(b_rz[:], bi[:, 0:2 * D], bh[:, 0:2 * D], ALU.add))
                ch.step(dve.tensor_copy(b_n[:, 0:D], bi[:, 2 * D:]))
                ch.link(dve.tensor_copy(b_n[:, D:], bh[:, 2 * D:]))
                for s in range(NB + 2):
                    if s < NB:
                        q = 4 + 2 * (s % 2)
                        dve.wait_ge(gates, s + 1)
                        dve.tensor_tensor(rz[:, s % 3, :], S.ps[0:P, q, :], b_rz[:], ALU.add).then_inc(gates_out, 1)
                        dve.tensor_tensor(nn[:, s % 3, :], S.ps[0:P, q + 1, :], b_n[:], ALU.add).then_inc(gates_out, 1)
                    if 1 <= s <= NB:
                        t = s - 1
                        a, r = nn[:, t % 3, :], rz[:, t % 3, 0:D]
                        dve.wait_ge(sig, t + 1)
                        dve.wait_ge(gates_out, 2 * (t + 1))
                        ch.link(dve.tensor_tensor(a[:, D:], a[:, D:], r, ALU.mult))
                        ch.link(dve.tensor_tensor(a[:, 0:D], a[:, 0:D], a[:, D:], ALU.add))
                        dve.sem_inc(cand, 1)
                    if s >= 2:
                        t = s - 2
                        a, z = nn[:, t % 3, :], rz[:, t % 3, D:]
                        dve.wait_ge(tanh, t + 1)
                        ch.link(dve.tensor_tensor(a[:, D:], S.xn[:, t, :], a[:, 0:D], ALU.subtract))
                        ch.link(dve.tensor_tensor(a[:, D:], a[:, D:], z, ALU.mult))
                        ch.link(dve.tensor_tensor(S.x[:, t, :], S.x[:, t, :], a[:, 0:D], ALU.add))
                        ch.link(dve.tensor_tensor(S.x[:, t, :], S.x[:, t, :], a[:, D:], ALU.add))


def ffn1(nc, S, A):
    n = 32
    with phase(nc, "ffn1") as (sb, sem):
        comb, comb_t = sb("comb", [P, NB, n]), sb("comb_t", [n, N])
        expert_weights(nc, S, A, "route1", n, "top1", S.turned["L1_ffn_router_w"], A["L1_ffn_router_b"],
                       comb, comb_t, b2=A["L1_ffn_b2"], target=S.acc[:, :, 0:D])
        with phase(nc, "ffn1m") as (sb2, sem2):
            comb_b = sb2("comb_b", [n, N], BF16)
            sel = sb2("sel", [n, n // 2, 128], BF16)
            steps, zeroed, ready = sem2("steps"), sem2("zeroed"), sem2("ready")
            with nc.Block() as block:
                @block.gpsimd
                def _(pool):
                    pool.memset(sel[:], 1.0).then_inc(zeroed, 1)
                    pool.wait_ge(zeroed, 1)
                    v = sel[:].rearrange("e q (j f) -> e q j f", j=2)
                    pool.affine_select(out=v, in_=v, compare_op=ALU.is_equal, fill=0.0, base=0,
                                       pattern=[[-2, n // 2], [-1, 2], [0, 64]], channel_multiplier=1).then_inc(zeroed, 1)
                    pool.wait_ge(zeroed, 2)

                @block.vector
                def _(dve):
                    dve.tensor_copy(comb_b[:], comb_t[:]).then_inc(ready, 1)
                    dve.wait_ge(ready, 1)

            def first(e):
                pick = A["L1_ffn_W1"][bass.ds(e * 2, 2)] if not isinstance(e, int) else A["L1_ffn_W1"][2 * e:2 * e + 2]
                return pick.rearrange("j (k p) f -> p j k f", p=128)

            def last(e):
                v = A["L1_ffn_W2"].rearrange("(q j) h d -> q (j h) d", j=2)
                pick = v[bass.ds(e, 1)] if not isinstance(e, int) else v[e:e + 1]
                return pick.rearrange("a p d -> p a d")

            experts(nc, S, "experts1", n // 2, first, None, last, 128,
                    Layer(ACT.Relu, (S.pcol, S.column["L1_ffn_b1"])), None, comb, S.acc, masked=(sel, comb_b))
            with nc.Block() as block:
                @block.vector
                def _(dve):
                    ch = Chain(dve, steps)
                    ch.link(dve.scalar_tensor_tensor(S.x[:], S.acc[:, :, 0:D], 0.0, S.x[:], ALU.max, ALU.add))


def coefficients(c, dve, b, X, Y, V, w, ask, NG):
    tt, ts, stt = dve.tensor_tensor, dve.tensor_scalar, dve.scalar_tensor_tensor
    den, rd, A, B, s2, s2m, r1, s, p, m, r2, cw = (b(k) for k in range(12))
    c.link(tt(den, X, Y, ALU.mult))
    c.link(stt(den, V, -2.0, den, ALU.mult, ALU.add))
    c.link(ts(den, den, 1.0, None, ALU.add))
    c.link(ts(rd, den, MIN_NORM, None, ALU.max))
    c.link(dve.reciprocal(rd, rd))
    c.step(stt(A, V, -2.0, Y, ALU.mult, ALU.add))
    c.link(ts(B, X, -1.0, 1.0, ALU.mult, ALU.add))
    c.link(tt(s2, A, X, ALU.add))
    c.link(ts(s2, s2, 0.0, None, ALU.max))
    c.step(ts(A, A, 1.0, None, ALU.add))
    c.link(ts(den, den, 0.0, None, ALU.max))
    c.link(tt(den, den, rd, ALU.mult))
    c.link(tt(s2, s2, den, ALU.mult))
    c.link(tt(s2, s2, rd, ALU.mult))
    c.link(ts(s, s2, 1e-18, None, ALU.max))
    ask(ACT.Ln, p, s, 1.0)
    ask(ACT.Exp, p, p, 0.5)
    c.link(dve.reciprocal(m, p))
    c.link(tt(m, m, s, ALU.mult))
    c.link(tt(p, p, m, ALU.add))
    c.link(ts(s, p, 0.5, None, ALU.mult))
    artanh_ratio(c, dve, s2, s, s2m, r1, p, m, r2, ask)
    c.link(ts(cw, B, MIN_NORM, None, ALU.max))
    c.link(tt(cw, cw, w, ALU.mult))
    c.link(tt(cw, cw, rd, ALU.mult))
    c.link(tt(cw, cw, r1, ALU.mult))
    c.step(stt(A, A, -1.0, cw, ALU.mult, ALU.mult))
    c.link(tt(B, B, cw, ALU.mult))
    return A, B


def artanh_ratio(c, dve, s2, s, s2m, r1, p, m, r2, ask):
    tt, ts, stt = dve.tensor_tensor, dve.tensor_scalar, dve.scalar_tensor_tensor
    c.link(ts(s2m, s2, 0.05, None, ALU.min))
    c.link(ts(r1, s2m, 1.0 / 11, None, ALU.mult))
    for k in (9, 7, 5, 3):
        c.link(stt(r1, r1, 1.0 / k, s2m, ALU.add, ALU.mult))
    c.link(ts(r1, r1, 1.0, None, ALU.add))
    c.link(ts(p, s, 1.0 - 2.0 ** -23, None, ALU.min))
    c.link(ts(m, p, -1.0, 1.0, ALU.mult, ALU.add))
    c.link(dve.reciprocal(m, m))
    c.link(stt(p, p, 1.0, m, ALU.add, ALU.mult))
    ask(ACT.Ln, p, p, 1.0)
    c.link(dve.reciprocal(m, s))
    c.link(stt(r2, p, 0.5, m, ALU.mult, ALU.mult))
    c.link(tt(r2, r2, r1, ALU.subtract))
    c.link(ts(m, s2, 0.04, None, ALU.is_gt))
    c.link(tt(r2, r2, m, ALU.mult))
    c.link(tt(r1, r1, r2, ALU.add))


def hyperbolic(nc, S, A):
    ends, local, blk = S.end["dst"], S.local["dst"], S.blk["dst"]
    COEF = 42
    with phase(nc, "hyp") as (sb, sem):
        dve_step, act_ask, act_done = sem("dve_step"), sem("act_ask"), sem("act_done")
        ch = Chain(None, dve_step)
        with ExitStack() as ctx:
            nodes = ctx.enter_context(nc.sbuf_tensor("hyp_nodes", [P, NB, D + 8], F32))
            junk = ctx.enter_context(nc.sbuf_tensor("hyp_junk", [128, 2, D], F32))
            stored, filled = sem("stored"), sem("filled")
            with nc.Block() as block:
                @block.sync
                def _(sp):
                    sp.wait_ge(filled, 1)
                    sp.dma_start(S.rows.rearrange("(t p) c -> p t c", p=P), nodes[:]).then_inc(stored, 16)
                    sp.wait_ge(stored, 16)

                @block.vector
                def _(dve):
                    ch.eng = dve
                    ch.step(dve.memset(S.acc[:], 0.0))
                    ch.step(dve.tensor_copy(nodes[:, :, 0:D], S.xn[:]))
                    ch.link(dve.memset(nodes[:, :, D:], 0.0))
                    for t in range(NB):
                        ch.link(dve.tensor_tensor_reduce(junk[0:P, t % 2, :], S.xn[:, t, :], S.xn[:, t, :], 1.0, 0.0,
                                                         ALU.mult, ALU.add, nodes[:, t, D:D + 1]))
                    ch.sync()
                    dve.sem_inc(filled, 1)

            gathered = [sem(f"gathered{h}") for h in range(2)]
            used = [sem(f"used{h}") for h in range(2)]
            (copied, go, selected, turned, turned_out, looked_up, dotted, ready, scaled, summed, added) = (
                sem(x) for x in ("copied", "go", "selected", "turned", "turned_out", "looked_up", "dotted",
                                 "coefs_ready", "scaled", "summed", "added"))
            jobs = []
            with nc.Block() as block, ExitStack() as ctx2:
                def mb(what, shape, dt=F32):
                    return ctx2.enter_context(nc.sbuf_tensor(f"hyp_{what}", shape, dt))

                idx, rows = mb("idx", [128, 2, G], I32), mb("rows", [128, 2, G, XG])
                loc, wts = mb("loc", [128, 2, G]), mb("wts", [128, 2 * G])
                onehot, onehot_t = mb("onehot", [128, 2, G, P]), mb("onehot_t", [P, 2, G, 128])
                X, V, Y = mb("X", [128, 2 * G]), mb("V", [128, 2 * G]), mb("Y", [128, 2 * G])
                cols = mb("cols", [128, 12, 2 * G])

                @block.gpsimd
                def _(pool):
                    gather_groups(pool, ends, S.rows, idx, rows, used, gathered, copied, go)

                @block.vector
                def _(dve):
                    ch.eng = dve
                    for i in peeled(dve, ITERS):
                        c = ch.loop(i, 2 * (G + 1) + 1 + 3 * 2 * G + COEF + 2 + 2 * G)
                        asked = [0]

                        def ask(func, out, in_, scale):
                            if not later(i):
                                jobs.append((func, out, in_, scale))
                            asked[0] += 1
                            dve.sem_inc(act_ask, 1)
                            dve.wait_ge(act_done, i * 3 + asked[0])

                        for h in range(2):
                            one_hots(c, dve, S, onehot, loc, local, bass.ds((2 * i + h) * G, G), h)
                            dve.sem_inc(selected, 1)
                        c.step(dve.tensor_copy(wts[:], S.edge_w[:, bass.ds(2 * i * G, 2 * G)]))
                        for j in range(2 * G):
                            h, t = j // G, j % G
                            if t == 0:
                                dve.wait_ge(gathered[h], (i + 1) * 16 * G)
                            dve.wait_ge(looked_up, i * 2 * G + j + 1)
                            src = S.ps[:, 2 + j % 2, 0:D + 1]
                            c.link(dve.tensor_tensor_reduce(junk[:, j % 2, :], src[:, 0:D], rows[:, h, t, 0:D],
                                                            1.0, 0.0, ALU.mult, ALU.add, V[:, j:j + 1]))
                            c.link(dve.tensor_copy(X[:, j:j + 1], src[:, D:D + 1]))
                            c.link(dve.tensor_copy(Y[:, j:j + 1], rows[:, h, t, D:D + 1]))
                            dve.sem_inc(dotted, 1)
                        al, be = coefficients(c, dve, lambda k: cols[:, k, :], X[:], Y[:], V[:], wts[:], ask, 2 * G)
                        for h in range(2):
                            c.link(dve.tensor_copy(rows[:, h, :, D], al[:, h * G:(h + 1) * G]))
                        dve.sem_inc(ready, 1)
                        for j in range(2 * G):
                            b = block_of(dve, blk, i, j // G, j % G)
                            dve.wait_ge(summed, i * 2 * G + j + 1)
                            here = S.acc[:, bass.ds(b, 1), 0:D + 1].rearrange("p a c -> p (a c)")
                            c.link(dve.tensor_tensor(here, here, S.ps[0:P, j % 2, 0:D + 1], ALU.add))
                            dve.sem_inc(added, 1)
                            if j % G == G - 1:
                                dve.sem_inc(used[j // G], 1)
                    ch.after(c, ITERS)

                @block.scalar
                def _(act):
                    for i in peeled(act, ITERS):
                        for h in range(2):
                            act.wait_ge(turned, 2 * i + h + 1)
                            act.copy(onehot_t[:, h], S.ps[0:P, 4:6, :].rearrange("p k (t e) -> p (k t) e", e=128))\
                               .then_inc(turned_out, 1)
                        for n, (func, out, in_, scale) in enumerate(jobs):
                            act.wait_ge(act_ask, i * 3 + n + 1)
                            act.activation(out, in_, func, scale=scale).then_inc(act_done, 1)
                        act.wait_ge(ready, i + 1)
                        for j in range(2 * G):
                            v = rows[:, j // G, j % G, 0:D]
                            act.activation(v, v, ACT.Copy, scale=cols[:, 3, j:j + 1]).then_inc(scaled, 1)

                @block.tensor
                def _(pe):
                    for i in peeled(pe, ITERS):
                        for h in range(2):
                            pe.wait_ge(selected, 2 * i + h + 1)
                            if later(i) or h:
                                pe.wait_ge(turned_out, 2 * i + h)
                            for t in range(G):
                                ins = pe.transpose(S.ps[0:P, 4 + t // 4, (t % 4) * 128:(t % 4 + 1) * 128],
                                                   onehot[:, h, t, :], S.ident[:])
                            ins.then_inc(turned, 1)
                        for j in range(2 * G):
                            h, t = j // G, j % G
                            if t == 0:
                                pe.wait_ge(turned_out, 2 * i + h + 1)
                            b = block_of(pe, blk, i, h, t)
                            if later(i) or j >= 2:
                                pe.wait_ge(dotted, i * 2 * G + j - 1)
                            pe.matmul(S.ps[:, 2 + j % 2, 0:D + 1], onehot_t[:, h, t, :],
                                      nodes[:, bass.ds(b, 1), 0:D + 1].rearrange("p a c -> p (a c)"),
                                      start=True, stop=True).then_inc(looked_up, 1)
                        for j in range(2 * G):
                            h, t = j // G, j % G
                            pe.wait_ge(scaled, i * 2 * G + j + 1)
                            if later(i) or j >= 2:
                                pe.wait_ge(added, i * 2 * G + j - 1)
                            pe.matmul(S.ps[0:P, j % 2, 0:D + 1], onehot[:, h, t, :], rows[:, h, t, 0:D + 1],
                                      start=True, stop=True).then_inc(summed, 1)

    with phase(nc, "hypn") as (sb, sem):
        dve_step, act_ask, act_done = sem("dve_step"), sem("act_ask"), sem("act_done")
        w, bias = sb("w", [128, K, D]), sb("bias", [P, D])
        v, cols = sb("v", [P, NB, D]), sb("cols", [P, 18, NB])
        uT = sb("uT", [128, 2, K, P])
        junk = sb("junk", [P, D])
        tiny = sb("tiny", [P, 12])
        loaded, u_ready, turned, turned_out, product, emptied = (
            sem(x) for x in ("loaded", "u_ready", "turned", "turned_out", "product", "emptied"))
        jobs = []
        with nc.Block() as block:
            @block.sync
            def _(sp):
                sp.dma_start(w[:], S.turned["L2_gnn_weight"].rearrange("(k p) f -> p k f", p=128)).then_inc(loaded, 16)
                sp.dma_start(bias[:], row(A["L2_gnn_bias"])).then_inc(loaded, 16)
                sp.wait_ge(loaded, 32)

            @block.vector
            def _(dve):
                ch = Chain(dve, dve_step)
                tt, ts, stt = dve.tensor_tensor, dve.tensor_scalar, dve.scalar_tensor_tensor
                acc = S.acc[:, :, 0:D]
                x2, V, Y, X, n2, n1, c1, c2, rd, p, m, un, pn, at, g, s2m, r1, r2 = (cols[:, k, :] for k in range(18))

                def ask(func, out, in_, scale):
                    jobs.append((func, out, in_, scale))
                    dve.sem_inc(act_ask, 1)
                    dve.wait_ge(act_done, len(jobs))

                def dots(out, a, b):
                    for t in range(NB):
                        ch.link(dve.tensor_tensor_reduce(junk[:], a[:, t, :], b[:, t, :], 1.0, 0.0, ALU.mult, ALU.add,
                                                         out[:, t:t + 1]))

                def norm(out, sq, p, m):
                    ch.link(ts(sq, sq, MIN_NORM ** 2, None, ALU.max))
                    ask(ACT.Sqrt, p, sq, 1.0)
                    ch.link(dve.reciprocal(m, p))
                    ch.link(tt(m, m, sq, ALU.mult))
                    ch.link(tt(p, p, m, ALU.add))
                    ch.link(ts(out, p, 0.5, None, ALU.mult))

                def mobius(Xc, Yc, Vc):
                    ch.link(tt(rd, Xc, Yc, ALU.mult))
                    ch.link(stt(rd, Vc, 2.0, rd, ALU.mult, ALU.add))
                    ch.link(ts(rd, rd, 1.0, MIN_NORM, ALU.add, ALU.max))
                    ch.link(dve.reciprocal(rd, rd))
                    ch.link(stt(c1, Vc, 2.0, Yc, ALU.mult, ALU.add))
                    ch.link(stt(c1, c1, 1.0, rd, ALU.add, ALU.mult))
                    ch.link(ts(c2, Xc, -1.0, 1.0, ALU.mult, ALU.add))
                    ch.link(tt(c2, c2, rd, ALU.mult))

                def combine(out, a, b):
                    for t in range(NB):
                        ch.step(ts(out[:, t, :], a[:, t, :], c1[:, t:t + 1], None, ALU.mult))
                    ch.sync()
                    for t in range(NB):
                        bt = b[:, t, :] if b is not bias else bias[:]
                        ch.step(stt(out[:, t, :], bt, c2[:, t:t + 1], out[:, t, :], ALU.mult, ALU.add))
                    ch.sync()

                def scale(y, by):
                    for t in range(NB):
                        ch.step(ts(y[:, t, :], y[:, t, :], by[:, t:t + 1], None, ALU.mult))
                    ch.sync()

                for t in range(NB):
                    ch.step(stt(acc[:, t, :], S.xn[:, t, :], S.acc[:, t, D:D + 1], acc[:, t, :], ALU.mult, ALU.add))
                ch.sync()
                dots(n2, acc, acc)
                dots(x2, S.xn, S.xn)
                norm(un, n2, p, m)
                ch.link(ts(g, x2, -1.0, 1.0, ALU.mult, ALU.add))
                ch.link(ts(g, g, MIN_NORM, None, ALU.max))
                ch.link(dve.reciprocal(g, g))
                ch.link(ts(g, g, 2.0, MIN_NORM, ALU.mult, ALU.max))
                ch.link(tt(g, g, un, ALU.mult))
                ask(ACT.Tanh, g, g, 0.5)
                ch.link(dve.reciprocal(m, un))
                ch.link(tt(g, g, m, ALU.mult))
                scale(acc, g)
                dots(V, S.xn, acc)
                dots(Y, acc, acc)
                mobius(x2, Y, V)
                combine(v, S.xn, acc)
                dve.sem_inc(u_ready, 1)
                dots(n2, v, v)
                norm(un, n2, p, m)
                artanh_ratio(ch, dve, n2, un, s2m, r1, p, m, r2, ask)
                for t in range(NB):
                    dve.wait_ge(product, t + 1)
                    dve.tensor_copy(acc[:, t, :], S.ps[0:P, 4 + t % 4, 0:D]).then_inc(emptied, 1)
                dve.wait_ge(emptied, NB)
                dots(n2, acc, acc)
                norm(pn, n2, p, m)
                ch.link(tt(g, pn, r1, ALU.mult))
                ask(ACT.Tanh, g, g, 1.0)
                ch.link(dve.reciprocal(m, pn))
                ch.link(tt(g, g, m, ALU.mult))
                scale(acc, g)
                tc = lambda k: tiny[:, k:k + 1]
                dve.wait_ge(loaded, 32)
                ch.link(dve.tensor_tensor_reduce(junk[:], bias[:], bias[:], 1.0, 0.0, ALU.mult, ALU.add, tc(0)))
                norm(tc(1), tc(0), tc(2), tc(3))
                ask(ACT.Tanh, tc(4), tc(1), 1.0)
                ch.link(dve.reciprocal(tc(5), tc(1)))
                ch.link(tt(tc(4), tc(4), tc(5), ALU.mult))
                ch.link(ts(bias[:], bias[:], tc(4), None, ALU.mult))
                ch.link(dve.tensor_tensor_reduce(junk[:], bias[:], bias[:], 1.0, 0.0, ALU.mult, ALU.add, tc(6)))
                dots(X, acc, acc)
                for t in range(NB):
                    ch.link(dve.tensor_tensor_reduce(junk[:], acc[:, t, :], bias[:], 1.0, 0.0, ALU.mult, ALU.add,
                                                     V[:, t:t + 1]))
                mobius(X, tc(6).to_broadcast([P, NB]), V)
                combine(v, acc, bias)
                dots(n2, v, v)
                norm(un, n2, p, m)
                artanh_ratio(ch, dve, n2, un, s2m, r1, p, m, r2, ask)
                for t in range(NB):
                    ch.step(ts(v[:, t, :], v[:, t, :], 0.0, r1[:, t:t + 1], ALU.max, ALU.mult))
                ch.sync()
                dots(n2, v, v)
                norm(un, n2, p, m)
                ask(ACT.Tanh, g, un, 1.0)
                ch.link(dve.reciprocal(m, un))
                ch.link(ts(g, g, 1.0 - 1e-5, None, ALU.min))
                ch.link(tt(g, g, m, ALU.mult))
                for t in range(NB):
                    ch.step(stt(S.x[:, t, :], v[:, t, :], g[:, t:t + 1], S.x[:, t, :], ALU.mult, ALU.add))
                ch.sync()

            @block.scalar
            def _(act):
                for n, (func, out, in_, scale) in enumerate(jobs[:4]):
                    act.wait_ge(act_ask, n + 1)
                    act.activation(out, in_, func, scale=scale).then_inc(act_done, 1)
                for t in range(NB):
                    act.wait_ge(turned, t + 1)
                    if t >= 2:
                        act.wait_ge(product, t - 1)
                    act.copy(uT[:, t % 2], S.ps[:, t % 2, 0:K * P].rearrange("p (k n) -> p k n", k=K))\
                       .then_inc(turned_out, 1)
                for n, (func, out, in_, scale) in enumerate(jobs[4:]):
                    act.wait_ge(act_ask, 4 + n + 1)
                    act.activation(out, in_, func, scale=scale).then_inc(act_done, 1)

            @block.tensor
            def _(pe):
                pe.wait_ge(loaded, 32)
                pe.wait_ge(u_ready, 1)
                for s in range(NB + 1):
                    if s < NB:
                        if s >= 2:
                            pe.wait_ge(turned_out, s - 1)
                        for k in range(K):
                            ins = pe.transpose(S.ps[:, s % 2, k * P:(k + 1) * P], v[:, s, k * 128:(k + 1) * 128],
                                               S.ident[0:P, 0:P])
                        ins.then_inc(turned, 1)
                    if s >= 1:
                        t = s - 1
                        pe.wait_ge(turned_out, t + 1)
                        if t >= 4:
                            pe.wait_ge(emptied, t - 3)
                        for k in range(K):
                            ins = pe.matmul(S.ps[0:P, 4 + t % 4, 0:D], uT[:, t % 2, k, :], w[:, k, :],
                                            start=k == 0, stop=k == K - 1)
                        ins.then_inc(product, 1)


def ffn2(nc, S, A):
    n = 8
    with phase(nc, "ffn2") as (sb, sem):
        comb, comb_t = sb("comb", [P, NB, n]), sb("comb_t", [n, N])
        aff = sb("aff", [128, 2, 2, 2 * n])
        expert_weights(nc, S, A, "route2", n, "soft", A["L2_ffn_Wr"], A["L2_ffn_br"], comb, comb_t,
                       b2=A["L2_ffn_bo"], target=S.x[:], base="keep")
        with phase(nc, "ffn2a") as (sb2, sem2):
            tmp = sb2("tmp", [128, 2, 3, 2 * n])
            dve_step, ask, done = sem2("dve_step"), sem2("ask"), sem2("done")
            with nc.Block() as block:
                @block.scalar
                def _(act):
                    for l in range(2):
                        act.wait_ge(ask, l + 1)
                        act.activation(tmp[:, l, 1, :], tmp[:, l, 0, :], ACT.Sqrt).then_inc(done, 1)

                @block.vector
                def _(dve):
                    ch = Chain(dve, dve_step)
                    for l in range(2):
                        b, g, be, m, var = (S.pcol[:, S.column[f"L2_ffn_{x}{l + 1}"]:S.column[f"L2_ffn_{x}{l + 1}"] + 2 * n]
                                            for x in ("b", "g", "be", "m", "v"))
                        bias, scale = aff[:, l, 0, :], aff[:, l, 1, :]
                        a, r, t = tmp[:, l, 0, :], tmp[:, l, 1, :], tmp[:, l, 2, :]
                        ch.link(dve.tensor_scalar(a, var, 1e-3, None, ALU.add))
                        dve.sem_inc(ask, 1)
                        dve.wait_ge(done, l + 1)
                        newton(ch, dve, a, r, t)
                        ch.link(dve.reciprocal(t, r))
                        ch.link(dve.tensor_tensor(scale, g, t, ALU.mult))
                        ch.link(dve.tensor_tensor(bias, b, m, ALU.subtract))
                        ch.link(dve.tensor_tensor(bias, bias, scale, ALU.mult))
                        ch.link(dve.tensor_tensor(bias, bias, be, ALU.add))
        t = aff[:].rearrange("p l a e -> p (l a e)")
        layer = [Layer(ACT.Relu, (t, l * 4 * n), (t, l * 4 * n + 2 * n)) for l in range(2)]
        experts(nc, S, "experts2", n, by_expert(A["L2_ffn_W1"]), by_expert(A["L2_ffn_W2"]),
                by_expert(A["L2_ffn_Wo"]), 256, layer[0], layer[1], comb, S.x)


def newton(ch, dve, value, root, tmp):
    ch.link(dve.reciprocal(tmp, root))
    ch.link(dve.tensor_tensor(tmp, tmp, value, ALU.mult))
    ch.link(dve.tensor_tensor(root, root, tmp, ALU.add))
    ch.link(dve.tensor_scalar(root, root, 0.5, None, ALU.mult))


def column_norm(ch, dve, src, stats, mv, sem_ask, sem_done, count, eps, gamma, beta, tmp, affine):
    for k in range(K):
        for c in range(NCHUNK):
            at = CH * c * P
            width = len(chunk_blocks(c)) * P
            ch.step(dve.bn_stats(stats[:, k, c, :], src[:, k, at:at + width]))
    ch.sync()
    for k in range(K):
        ch.step(dve.bn_aggr(mv[:, k, :], stats[:, k, :, :]))
    ch.sync()
    var, root, inv = tmp[:, 0, :], tmp[:, 1, :], tmp[:, 2, :]
    ch.link(dve.tensor_scalar(var, mv[:, :, 1], eps, None, ALU.add))
    dve.sem_inc(sem_ask, 1)
    dve.wait_ge(sem_done, count)
    newton(ch, dve, var, root, inv)
    ch.link(dve.reciprocal(inv, root))
    ch.link(dve.tensor_tensor(affine[:, 0, :], gamma, inv, ALU.mult))
    ch.link(dve.tensor_tensor(inv, mv[:, :, 0], affine[:, 0, :], ALU.mult))
    ch.link(dve.tensor_tensor(affine[:, 1, :], beta, inv, ALU.subtract))


def hyperconv(nc, S, A, n, hT):
    ends, local, blk = S.end["dst"], S.local["dst"], S.blk["dst"]
    col = lambda v: S.pcol[:, S.column[f"L3_gnn_{v}"]:S.column[f"L3_gnn_{v}"] + K]
    source = S.xT if n == 1 else hT
    with phase(nc, f"conv{n}") as (sb, sem):
        w1, w2, b1 = sb("w1", [128, K, D]), sb("w2", [128, K, D]), sb("b1", [P, D])
        loaded, dve_step, product, out, stored = (
            sem(x) for x in ("loaded", "dve_step", "product", "out", "stored"))
        ch = Chain(None, dve_step)
        with nc.Block() as block:
            @block.sync
            def _(sp):
                for dst, v in ((w1, "w1"), (w2, "w2")):
                    sp.dma_start(dst[:], A[f"L3_gnn_c{n}_{v}"].rearrange("(k p) f -> p k f", p=128)).then_inc(loaded, 16)
                sp.dma_start(b1[:], row(A[f"L3_gnn_c{n}_b1"])).then_inc(loaded, 16)
                sp.wait_ge(loaded, 48)
                sp.wait_ge(out, NB)
                sp.dma_start(S.rows_b.rearrange("(t p) c -> p t c", p=P), S.acc[:, :, 0:D]).then_inc(stored, 16)
                sp.wait_ge(stored, 16)

            @block.tensor
            def _(pe):
                pe.wait_ge(loaded, 48)
                for t in range(NB):
                    if t >= 8:
                        pe.wait_ge(out, t - 7)
                    for k in range(K):
                        ins = pe.matmul(S.ps[0:P, t % 8, 0:D], source[:, k, t * P:(t + 1) * P], w1[:, k, :],
                                        start=k == 0, stop=k == K - 1)
                    ins.then_inc(product, 1)

            @block.vector
            def _(dve):
                ch.eng = dve
                dve.wait_ge(loaded, 48)
                for t in range(NB):
                    dve.wait_ge(product, t + 1)
                    ch.link(dve.tensor_tensor(S.acc[:, t, 0:D], S.ps[0:P, t % 8, 0:D], b1[:], ALU.add))
                    dve.tensor_scalar(S.acc[:, t, 0:D], S.acc[:, t, 0:D], 0.0, None, ALU.max).then_inc(out, 1)

        gathered = [sem(f"gathered{h}") for h in range(2)]
        used = [sem(f"used{h}") for h in range(2)]
        copied, go, selected, summed, added = (sem(x) for x in ("copied", "go", "selected", "summed", "added"))
        with nc.Block() as block, ExitStack() as ctx:
            def mb(what, shape, dt=F32):
                return ctx.enter_context(nc.sbuf_tensor(f"conv{n}_{what}", shape, dt))

            idx, rows = mb("idx", [128, 2, G], I32), mb("rows", [128, 2, G, D])
            loc, wts, weight_of = mb("loc", [128, 2, G]), mb("wts", [128, 2, G]), mb("weight_of", [128, 2, G, P])

            @block.gpsimd
            def _(pool):
                gather_groups(pool, ends, S.rows_b, idx, rows, used, gathered, copied, go)

            @block.vector
            def _(dve):
                ch.eng = dve
                ch.link(dve.memset(S.acc[:], 0.0))
                for i in peeled(dve, ITERS):
                    c = ch.loop(i, 2 * (G + 2) + 2 * G)
                    for h in range(2):
                        at = bass.ds((2 * i + h) * G, G)
                        c.step(dve.tensor_copy(loc[:, h, :], local[:, at]))
                        c.link(dve.tensor_copy(wts[:, h, :], S.edge_w[:, at]))
                        for t in range(G):
                            c.step(dve.tensor_scalar(weight_of[:, h, t, :], S.iota[:, 0:P], loc[:, h, t:t + 1],
                                                     wts[:, h, t:t + 1], ALU.is_equal, ALU.mult))
                        c.sync()
                        dve.sem_inc(selected, 1)
                    for j in range(2 * G):
                        b = block_of(dve, blk, i, j // G, j % G)
                        dve.wait_ge(summed, i * 2 * G + j + 1)
                        here = S.acc[:, bass.ds(b, 1), 0:D].rearrange("p a c -> p (a c)")
                        c.link(dve.tensor_tensor(here, here, S.ps[0:P, j % 8, 0:D], ALU.add))
                        dve.sem_inc(added, 1)
                        if j % G == G - 1:
                            dve.sem_inc(used[j // G], 1)
                ch.after(c, ITERS)

            @block.tensor
            def _(pe):
                for i in peeled(pe, ITERS):
                    for j in range(2 * G):
                        h, t = j // G, j % G
                        if t == 0:
                            pe.wait_ge(selected, 2 * i + h + 1)
                            pe.wait_ge(gathered[h], (i + 1) * 16 * G)
                        if later(i) or j >= 8:
                            pe.wait_ge(added, i * 2 * G + j - 7)
                        pe.matmul(S.ps[0:P, j % 8, 0:D], weight_of[:, h, t, :], rows[:, h, t, :],
                                  start=True, stop=True).then_inc(summed, 1)

        turned, turned_out, product2, out2, ask, root, shown, applied, last = (
            sem(x) for x in ("turned", "turned_out", "product2", "out2", "ask", "root", "shown", "applied", "last"))
        with nc.Block() as block, ExitStack() as ctx:
            def mb(what, shape, dt=F32):
                return ctx.enter_context(nc.sbuf_tensor(f"conv{n}_{what}", shape, dt))

            aggT = mb("aggT", [128, 2, K, CH * P])
            stats, mv, tmp, affine = (mb("stats", [128, K, NCHUNK, 6]), mb("mv", [128, K, 2]), mb("tmp", [128, 3, K]),
                                      mb("affine", [128, 2, 2, K]))

            @block.tensor
            def _(pe):
                for s in range(NCHUNK + 1):
                    if s < NCHUNK:
                        for m, t in enumerate(chunk_blocks(s)):
                            if t >= 4:
                                pe.wait_ge(turned_out, t - 3)
                            for k in range(K):
                                ins = pe.transpose(S.ps[:, t % 4, k * P:(k + 1) * P], S.acc[:, t, k * 128:(k + 1) * 128],
                                                   S.ident[0:P, 0:P])
                            ins.then_inc(turned, 1)
                    if s >= 1:
                        c = s - 1
                        width = len(chunk_blocks(c)) * P
                        pe.wait_ge(turned_out, chunk_blocks(c)[-1] + 1)
                        for f in range(K):
                            m = c * K + f
                            if m >= 4:
                                pe.wait_ge(out2, m - 3)
                            for k in range(K):
                                ins = pe.matmul(S.ps[:, 4 + m % 4, 0:width], w2[:, k, f * 128:(f + 1) * 128],
                                                aggT[:, c % 2, k, 0:width], start=k == 0, stop=k == K - 1)
                            ins.then_inc(product2, 1)
                if n == 2:
                    pe.wait_ge(applied, 4)
                    for t in range(NB):
                        if t >= 4:
                            pe.wait_ge(last, t - 3)
                        for k in range(K):
                            ins = pe.transpose(S.ps[0:P, t % 4, k * 128:(k + 1) * 128], hT[:, k, t * P:(t + 1) * P],
                                               S.ident[:])
                        ins.then_inc(shown, 1)

            @block.scalar
            def _(act):
                for t in range(NB):
                    c, m = t // CH, t % CH
                    act.wait_ge(turned, t + 1)
                    if c >= 2:
                        act.wait_ge(product2, (c - 1) * K)
                    act.copy(aggT[:, c % 2, :, m * P:(m + 1) * P],
                             S.ps[:, t % 4, 0:K * P].rearrange("p (k n) -> p k n", k=K)).then_inc(turned_out, 1)
                for a in range(2):
                    act.wait_ge(ask, 2 * a + 1)
                    act.activation(tmp[:, 1, :], tmp[:, 0, :], ACT.Sqrt).then_inc(root, 1)
                    act.wait_ge(ask, 2 * a + 2)
                    function = ACT.Identity if (n == 2 and a == 1) else ACT.Relu
                    for k in range(K):
                        act.activation(hT[:, k, :], hT[:, k, :], function, bias=affine[:, a, 1, k:k + 1],
                                       scale=affine[:, a, 0, k:k + 1]).then_inc(applied, 1)

            @block.vector
            def _(dve):
                ch.eng = dve
                for m in range(NCHUNK * K):
                    c, f = m // K, m % K
                    width = len(chunk_blocks(c)) * P
                    at = c * CH * P
                    dve.wait_ge(product2, m + 1)
                    dve.tensor_scalar(hT[:, f, at:at + width], S.ps[:, 4 + m % 4, 0:width],
                                      col(f"c{n}_b2")[:, f:f + 1], None, ALU.add).then_inc(out2, 1)
                dve.wait_ge(out2, NCHUNK * K)
                for a, v in enumerate((f"c{n}_", f"bn{n}_")):
                    if a:
                        dve.wait_ge(applied, 2)
                    column_norm(ch, dve, hT, stats, mv, ask, root, a + 1, EPS, col(v + "g"), col(v + "b"),
                                tmp, affine[:, a])
                    dve.sem_inc(ask, 1)
                if n == 2:
                    dve.wait_ge(applied, 4 - 0)
                    for t in range(NB):
                        dve.wait_ge(shown, t + 1)
                        ch.link(dve.tensor_tensor(S.acc[:, t, 0:D], S.xn[:, t, :], S.ps[0:P, t % 4, 0:D], ALU.add))
                        dve.sem_inc(last, 1)
                        ch.link(dve.scalar_tensor_tensor(S.x[:, t, :], S.acc[:, t, 0:D], 0.0, S.x[:, t, :],
                                                         ALU.max, ALU.add))


def hypergraph(nc, S, A):
    with phase(nc, "hgraph") as (sb, sem):
        hT = sb("hT", [128, K, N])
        hyperconv(nc, S, A, 1, hT)
        hyperconv(nc, S, A, 2, hT)


def ffn3(nc, S, A, out):
    n = 16
    with phase(nc, "ffn3") as (sb, sem):
        comb, comb_t = sb("comb", [P, NB, n]), sb("comb_t", [n, N])
        expert_weights(nc, S, A, "route3", n, "gates", A["L3_ffn_gate_w"], A["L3_ffn_gate_b"], comb, comb_t,
                       b2=A["L3_ffn_b2"], target=S.acc[:, :, 0:D])
        experts(nc, S, "experts3", n, by_expert(A["L3_ffn_w1"]), None, by_expert(A["L3_ffn_w2"]), 512,
                Layer(ACT.Relu, (S.pcol, S.column["L3_ffn_b1"])), None, comb, S.acc)
    with phase(nc, "final") as (sb, sem):
        stats, mv = sb("stats", [P, NB, 6]), sb("mv", [P, NB, 2])
        var, root, inv = sb("var", [P, NB]), sb("root", [P, NB]), sb("inv", [P, NB])
        gamma, beta = sb("gamma", [P, D]), sb("beta", [P, D])
        loaded, dve_step, var_ready, root_ready, finished, stored = (
            sem(x) for x in ("loaded", "dve_step", "var_ready", "root_ready", "finished", "stored"))
        with nc.Block() as block:
            @block.sync
            def _(sp):
                sp.dma_start(gamma[:], row(A["L3_ffn_gamma"])).then_inc(loaded, 16)
                sp.dma_start(beta[:], row(A["L3_ffn_beta"])).then_inc(loaded, 16)
                sp.wait_ge(finished, 1)
                sp.dma_start(out.rearrange("(t p) c -> p t c", p=P), S.x[:]).then_inc(stored, 16)
                sp.wait_ge(stored, 16)

            @block.scalar
            def _(act):
                act.wait_ge(var_ready, 1)
                act.activation(root[:], var[:], ACT.Sqrt).then_inc(root_ready, 1)

            @block.vector
            def _(dve):
                ch = Chain(dve, dve_step)
                y = S.acc[:, :, 0:D]
                ch.link(dve.tensor_tensor(y, y, S.xn[:], ALU.add))
                norm_into(ch, dve, S, y, stats, mv, var, root, inv, var_ready, root_ready)
                dve.wait_ge(loaded, 32)
                ch.link(dve.tensor_tensor(y, y, bc_mid(gamma[:], NB), ALU.mult))
                ch.link(dve.tensor_tensor(S.x[:], S.x[:], bc_mid(beta[:], NB), ALU.add))
                ch.link(dve.tensor_tensor(S.x[:], S.x[:], y, ALU.add))
                dve.sem_inc(finished, 1)


def plan(nc, S, A, out):
    return [
        lambda: setup(nc, S, A),
        lambda: sort_edges(nc, S, A, "dst", False),
        lambda: sort_edges(nc, S, A, "src", True),
        lambda: layer_norm(nc, S, "ln0"),
        lambda: gat(nc, S, A),
        lambda: layer_norm(nc, S, "ln1"),
        lambda: ffn0(nc, S, A),
        lambda: layer_norm(nc, S, "ln2"),
        lambda: mpnn(nc, S, A),
        lambda: layer_norm(nc, S, "ln3"),
        lambda: ffn1(nc, S, A),
        lambda: layer_norm(nc, S, "ln4"),
        lambda: hyperbolic(nc, S, A),
        lambda: layer_norm(nc, S, "ln5"),
        lambda: ffn2(nc, S, A),
        lambda: layer_norm(nc, S, "ln6"),
        lambda: hypergraph(nc, S, A),
        lambda: layer_norm(nc, S, "ln7"),
        lambda: ffn3(nc, S, A, out),
    ]


def build(nc, A, out):
    S = Shared()
    with ExitStack() as ctx:
        def sb(name, shape, dt=F32):
            return ctx.enter_context(nc.sbuf_tensor(name, shape, dt))

        def dram(name, shape, dt=F32):
            return nc.dram_tensor(name, shape, dt, kind="Internal").ap()

        S.x, S.xn = sb("x", [P, NB, D]), sb("xn", [P, NB, D])
        S.acc = sb("acc", [P, NB, XG])
        S.xT = sb("xT", [128, K, N])
        S.ident, S.iota, S.ones = sb("ident", [128, 128]), sb("iota", [128, 128]), sb("ones", [128, 128])
        S.pcol = sb("pcol", [128, place_vectors()[1] * 128])
        S.end = {k: sb(f"end_{k}", [128, NT], I32) for k in ("dst", "src")}
        S.local = {k: sb(f"local_{k}", [128, NT]) for k in ("dst", "src")}
        S.blk = {k: sb(f"blk_{k}", [1, NT], I32) for k in ("dst", "src")}
        S.edge_w = sb("edge_w", [128, NT])
        S.ps = ctx.enter_context(nc.psum_tensor("ps", [128, 8, 512], F32))
        S.turned = {n: dram(f"turned_{n}", (c, r)) for n, r, c in TURNED}
        S.records = {"dst": dram("records_dst", (SLOTS, 3)), "src": dram("records_src", (SLOTS, 2 + ED))}
        S.rows = dram("rows", (N, XG))
        S.rows8 = dram("rows8", (N, HEADS))
        S.rows_b = dram("rows_b", (N, D))
        S.rows_c = dram("rows_c", (N, D + 1))
        for step in plan(nc, S, A, out):
            step()


def kernel(**inputs):
    import numpy as np
    import concourse.bacc as bacc
    from concourse.bass_utils import run_bass_kernel_spmd

    nc = bacc.Bacc("TRN2", target_bir_lowering=False, num_devices=1)
    arrays, A = {}, {}
    for name, value in inputs.items():
        a = np.ascontiguousarray(value)
        arrays[f"in_{name}"] = a
        A[name] = nc.dram_tensor(f"in_{name}", a.shape, mybir.dt.from_np(a.dtype), kind="ExternalInput").ap()
    out = nc.dram_tensor("out_x", (N, D), F32, kind="ExternalOutput").ap()
    build(nc, A, out)
    return run_bass_kernel_spmd(nc, [arrays], core_ids=[0]).results[0]["out_x"]
```

```python
from contextlib import ExitStack, contextmanager

import concourse.bass as bass
from concourse import mybir

F32 = mybir.dt.float32
I32 = mybir.dt.int32
BF16 = mybir.dt.bfloat16
ALU = mybir.AluOpType
ACT = mybir.ActivationFunctionType
AX = mybir.AxisListType.X

N, D, E = 3125, 256, 50000
P = 125
NB = N // P
K = D // 128
EC = E // P
NT = (E + NB * 127) // 128 + 1
NT += -NT % 32
SLOTS = NT * 128
G = 8
GROUPS = NT // G
U = 4
HEADS, HC = 8, 32
ED = 64
CH = 4
NCHUNK = -(-NB // CH)
EPS = 1e-5
MIN_NORM = 1e-15
PAD_KEY = -1.0e6
XG = D + 8


def chunk_blocks(c):
    return range(CH * c, min(CH * c + CH, NB))


class Chain:

    def __init__(self, eng, sem, base=0):
        self.eng, self.sem, self.base, self.n = eng, sem, base, 0
        self.meanwhile = None

    def step(self, ins):
        ins.then_inc(self.sem, 1)
        self.n += 1

    def sync(self):
        self.eng.wait_ge(self.sem, self.base + self.n)

    def link(self, ins):
        self.step(ins)
        if self.meanwhile:
            self.meanwhile()
        self.sync()

    def loop(self, i, per):
        body = Chain(self.eng, self.sem, self.base + self.n + i * per)
        body.per = per
        return body

    def after(self, body, iterations):
        assert body.n == body.per, (body.n, body.per)
        self.n += body.n * iterations


def peeled(eng, n):
    yield 0
    if n > 1:
        with eng.Fori(1, n) as i:
            yield i


def later(i):
    return not isinstance(i, int)


@contextmanager
def phase(nc, name):
    with nc.cleanup_on_exit(), ExitStack() as ctx:
        def sb(what, shape, dt=F32):
            return ctx.enter_context(nc.sbuf_tensor(f"{name}_{what}", shape, dt))

        def sem(what):
            return nc.alloc_semaphore(f"{name}_{what}")

        yield sb, sem


def bc(ap, n):
    return ap.unsqueeze(2).to_broadcast([ap.shape[0], ap.shape[1], n])


def bc_mid(ap, n):
    return ap.unsqueeze(1).to_broadcast([ap.shape[0], n, ap.shape[1]])


def row(ap, n=P):
    return ap.rearrange("(a d) -> a d", a=1).to_broadcast([n, ap.shape[0]])


class Shared:
    pass


VECTORS = [
    ("L0_ffn_b1", 8, 256), ("L1_ffn_b1", 32, 64), ("L3_ffn_b1", 16, 512),
    *[(f"L2_ffn_{v}{i}", 8, 256) for i in (1, 2) for v in ("b", "g", "be", "m", "v")],
    *[(f"L3_gnn_{v}", 1, 256) for v in ("c1_b1", "c1_b2", "c1_g", "c1_b", "bn1_g", "bn1_b",
                                        "c2_b1", "c2_b2", "c2_g", "c2_b", "bn2_g", "bn2_b")],
]


def place_vectors():
    place, tile, at = {}, 0, 0
    for name, e, f in VECTORS:
        rows = e * f // 128
        if at + rows > 128:
            tile, at = tile + 1, 0
        place[name] = (tile, at, rows)
        at += rows
    return place, tile + 1


TURNED = [
    ("L0_ffn_router_w", 8, 256), ("L1_gnn_W1", 256, 576), ("L1_gnn_W2", 256, 256),
    ("L1_gnn_W_ih", 768, 256), ("L1_gnn_W_hh", 768, 256), ("L1_ffn_router_w", 32, 256),
    ("L2_gnn_weight", 256, 256),
]


def setup(nc, S, A):
    place, ntiles = place_vectors()
    S.column = {name: tile * 128 + at for name, (tile, at, _) in place.items()}
    with phase(nc, "setup") as (sb, sem):
        vec = sb("vec", [128, ntiles, 128])
        natural = {n: sb(n, [128, -(-r // 128), c]) for n, r, c in TURNED}
        turned = {n: sb(n + "_t", [128, -(-c // 128), r]) for n, r, c in TURNED}
        loaded, constants, turned_sem, copied, stored, zeroed = (
            sem(x) for x in ("loaded", "constants", "blocks_turned", "blocks_copied", "stored", "zeroed"))
        jobs = [(vec[:, t, :], S.pcol[:, t * 128:(t + 1) * 128], 128, 128) for t in range(ntiles)]
        for n, r, c in TURNED:
            for a in range(-(-r // 128)):
                for b in range(-(-c // 128)):
                    rows, cols = min(128, r - a * 128), min(128, c - b * 128)
                    jobs.append((natural[n][0:rows, a, b * 128:b * 128 + cols],
                                 turned[n][0:cols, b, a * 128:a * 128 + rows], rows, cols))
        loads = []
        for name, e, f in VECTORS:
            tile, at, rows = place[name]
            src = A[name].rearrange("(k p) -> k p", p=128) if e == 1 else (
                A[name].rearrange("(e j) p -> e (j p)", j=2) if f == 64 else
                A[name].rearrange("e (k p) -> (e k) p", p=128))
            loads.append((vec[at:at + rows, tile, :], src))
        for n, r, c in TURNED:
            if r < 128:
                loads.append((natural[n][0:r, 0, :], A[n]))
            else:
                loads.append((natural[n][:, :, :], A[n].rearrange("(a p) c -> p a c", p=128)))
        loads.append((S.x[:, :, :], A["x"].rearrange("(t p) d -> p t d", p=P)))

        with nc.Block() as block:
            @block.sync
            def _(sp):
                sp.wait_ge(zeroed, 1)
                for dst, src in loads:
                    sp.dma_start(dst, src).then_inc(loaded, 16)
                sp.wait_ge(copied, len(jobs))
                n_stores = 0
                for n, r, c in TURNED:
                    full = c // 128
                    sp.dma_start(S.turned[n][0:full * 128, :].rearrange("(b p) r -> p b r", p=128),
                                 turned[n][:, 0:full, :]).then_inc(stored, 16)
                    n_stores += 1
                    if c % 128:
                        sp.dma_start(S.turned[n][full * 128:c, :], turned[n][0:c % 128, full, :]).then_inc(stored, 16)
                        n_stores += 1
                sp.wait_ge(stored, 16 * n_stores)

            @block.gpsimd
            def _(pool):
                pool.memset(vec[:], 0.0).then_inc(zeroed, 1)
                pool.memset(S.ident[:], 0.0).then_inc(constants, 1)
                pool.wait_ge(constants, 1)
                pool.affine_select(out=S.ident[:], in_=S.ident[:], compare_op=ALU.not_equal, fill=1.0,
                                   base=0, pattern=[[-1, 128]], channel_multiplier=1).then_inc(constants, 1)
                pool.iota(S.iota[:], pattern=[[1, 128]], base=0, channel_multiplier=0,
                          allow_small_or_imprecise_dtypes=True).then_inc(constants, 1)
                pool.memset(S.ident_b[:], 0.0).then_inc(constants, 1)
                pool.wait_ge(constants, 4)
                pool.affine_select(out=S.ident_b[:], in_=S.ident_b[:], compare_op=ALU.not_equal, fill=1.0,
                                   base=0, pattern=[[-1, 128]], channel_multiplier=1).then_inc(constants, 1)

            @block.tensor
            def _(pe):
                pe.wait_ge(loaded, 16 * len(loads))
                pe.wait_ge(constants, 5)
                for j, (src, _, rows, cols) in enumerate(jobs):
                    if j >= 8:
                        pe.wait_ge(copied, j - 7)
                    pe.transpose(S.ps[0:cols, j % 8, 0:rows], src, S.ident[0:rows, 0:rows]).then_inc(turned_sem, 1)

            @block.vector
            def _(dve):
                for j, (_, dst, rows, cols) in enumerate(jobs):
                    dve.wait_ge(turned_sem, j + 1)
                    dve.tensor_copy(dst, S.ps[0:cols, j % 8, 0:rows]).then_inc(copied, 1)


def sort_edges(nc, S, A, by, kept=None):
    attributes = kept is not None
    name = f"sort_{by}"
    other = "src" if by == "dst" else "dst"
    W = 2 + ED if attributes else 3
    table = S.records[by]
    PADS = 16
    SG = 8
    with phase(nc, name) as (sb, sem):
        key_i, other_i = sb("key_i", [P, EC], I32), sb("other_i", [P, EC], I32)
        weight = sb("weight", [P, EC])
        if attributes:
            key, oth, addr, blk = kept
        else:
            key, oth, addr, blk = sb("key", [P, EC]), sb("oth", [P, EC]), sb("addr", [P, EC], I32), sb("blk", [128, NT])
        ge = sb("ge", [P, NB + 1, EC], BF16)
        onehot = sb("onehot", [P, NB, EC], BF16)
        one_t = sb("one_t", [128, EC])
        before = sb("before", [P, P], BF16)
        ones_b = sb("ones_b", [P, 128], BF16)
        count, ones_p = sb("count", [P, NB]), sb("ones_p", [P, 128])
        tiles_i, tiles = sb("tiles_i", [128, NB], I32), sb("tiles", [128, NB])
        upto, start, slot0 = sb("upto", [128, NB]), sb("start", [128, NB]), sb("slot0", [128, NB])
        iota_t = sb("iota_t", [128, NT])
        cum, pos = sb("cum", [P, 2, EC]), sb("pos", [P, EC])
        hi_i, hi = sb("hi_i", [P, EC], I32), sb("hi", [P, EC])
        pad = sb("pad", [128, PADS, W])
        stage = sb("stage", [P, 2, SG, 3])
        idx = sb("idx", [P, 2, SG], I32)
        back = sb("back", [128, NT, 3])
        loaded, consts, padded = sem("loaded"), sem("consts"), sem("pads_stored")
        dve_step, counts_ready, ranks = sem("dve_step"), sem("counts_ready"), sem("ranks_ready")
        ranks_used, pool_step = sem("ranks_used"), sem("pool_step")
        staged = [sem(f"staged{h}") for h in range(2)]
        scattered = [sem(f"scattered{h}") for h in range(2)]
        addresses, back_in, go = sem("addresses_ready"), sem("records_back"), sem("go")
        view = table.rearrange("(p t) w -> p t w", p=128)
        HALVES = EC // (2 * SG)

        with nc.Block() as block:
            @block.sync
            def _(sp):
                sp.dma_start(key_i[:], A[by].rearrange("(p t) -> p t", p=P)).then_inc(loaded, 16)
                sp.dma_start(other_i[:], A[other].rearrange("(p t) -> p t", p=P)).then_inc(loaded, 16)
                sp.dma_start(weight[:], A["edge_weight"].rearrange("(p t) -> p t", p=P)).then_inc(loaded, 16)
                sp.wait_ge(consts, 4)
                for t in range(0, NT, PADS):
                    sp.dma_start(view[:, t:t + PADS, :], pad[:]).then_inc(padded, 16)
                sp.wait_ge(padded, 16 * (NT // PADS))
                if not attributes:
                    for h in range(2):
                        sp.wait_ge(scattered[h], 16 * SG * HALVES)
                    sp.dma_start(back[:], view).then_inc(back_in, 16)
                    sp.wait_ge(back_in, 16)

            @block.gpsimd
            def _(pool):
                ch = Chain(pool, pool_step)
                ch.link(pool.memset(pad[:], 0.0))
                pool.memset(pad[:, :, 1:2], PAD_KEY).then_inc(consts, 1)
                ch.link(pool.memset(before[:], 0.0))
                pool.affine_select(out=before[:], in_=before[:], compare_op=ALU.is_gt, fill=-1.0, base=0,
                                   pattern=[[1, P]], channel_multiplier=-1).then_inc(consts, 1)
                pool.iota(iota_t[:], pattern=[[1, NT]], base=0, channel_multiplier=0,
                          allow_small_or_imprecise_dtypes=True).then_inc(consts, 1)
                pool.memset(ones_b[:], 1.0).then_inc(consts, 1)
                pool.wait_ge(padded, 16 * (NT // PADS))
                if attributes:
                    return
                with pool.Fori(0, HALVES) as i:
                    for h in range(2):
                        pool.wait_ge(staged[h], i + 1)
                        pool.sem_inc(go, 1)
                        for t in range(SG):
                            pool.indirect_dma_start(
                                out=table, out_offset=bass.IndirectOffsetOnAxis(ap=idx[:, h, t:t + 1], axis=0),
                                in_=stage[:, h, t, :], in_offset=None).then_inc(scattered[h], 16)

            @block.tensor
            def _(pe):
                pe.wait_ge(counts_ready, 1)
                pe.matmul(S.ps[:, 7, 0:NB], ones_p[:], count[:], start=True, stop=True).then_inc(ranks, 1)
                pe.wait_ge(consts, 4)
                for b in range(NB):
                    if b >= 3:
                        pe.wait_ge(ranks_used, b - 2)
                    k = 2 * (b % 3)
                    pe.matmul(S.ps[0:P, k, 0:EC], ones_b[:, 0:P], onehot[:, b, :], start=True, stop=True)
                    pe.matmul(S.ps[0:P, k + 1, 0:EC], before[:], onehot[:, b, :],
                              start=True, stop=True).then_inc(ranks, 1)

            @block.vector
            def _(dve):
                ch = Chain(dve, dve_step)
                ch.step(dve.memset(one_t[:], 1.0))
                ch.step(dve.memset(ones_p[:], 1.0))
                ch.step(dve.memset(ge[:, 0, :], 1.0))
                ch.step(dve.memset(ge[:, NB, :], 0.0))
                dve.wait_ge(loaded, 48)
                ch.step(dve.tensor_copy(oth[:], other_i[:]))
                ch.link(dve.tensor_copy(key[:], key_i[:]))
                for b in range(1, NB):
                    ch.step(dve.tensor_scalar(ge[:, b, :], key[:], float(P * b), None, ALU.is_ge))
                ch.sync()
                ch.link(dve.tensor_tensor(onehot[:], ge[:, 0:NB, :], ge[:, 1:NB + 1, :], ALU.subtract))
                ch.link(dve.tensor_reduce(count[:], onehot[:], AX, ALU.add))
                dve.sem_inc(counts_ready, 1)
                dve.wait_ge(ranks, 1)
                ch.link(dve.tensor_scalar(tiles_i[:], S.ps[:, 7, 0:NB], 127.0, None, ALU.add))
                ch.link(dve.tensor_scalar(tiles_i[:], tiles_i[:], 7, None, ALU.arith_shift_right))
                ch.link(dve.tensor_copy(tiles[:], tiles_i[:]))
                ch.link(dve.tensor_tensor_scan(upto[:], one_t[:, 0:NB], tiles[:], 0.0, ALU.mult, ALU.add))
                ch.link(dve.tensor_tensor(start[:], upto[:], tiles[:], ALU.subtract))
                ch.link(dve.tensor_scalar(slot0[:], start[:], 128.0, None, ALU.mult))
                dve.wait_ge(consts, 4)
                ch.link(dve.tensor_scalar(blk[:], iota_t[:], start[:, 1:2], None, ALU.is_ge))
                for b in range(2, NB):
                    ch.link(dve.scalar_tensor_tensor(blk[:], iota_t[:], start[:, b:b + 1], blk[:],
                                                     ALU.is_ge, ALU.add))
                ch.step(dve.tensor_copy(S.blk[by][:], blk[0:1, :]))
                ch.link(dve.memset(pos[:], 0.0))
                for b in range(NB):
                    k = 2 * (b % 3)
                    dve.wait_ge(ranks, b + 2)
                    ch.link(dve.tensor_tensor_scan(cum[:, 0, :], one_t[0:P, :], S.ps[0:P, k, 0:EC],
                                                   slot0[0:P, b:b + 1], ALU.mult, ALU.add))
                    ch.link(dve.tensor_tensor(cum[:, 1, :], cum[:, 0, :], S.ps[0:P, k + 1, 0:EC], ALU.add))
                    dve.sem_inc(ranks_used, 1)
                    ch.link(dve.tensor_tensor(cum[:, 1, :], cum[:, 1, :], onehot[:, b, :], ALU.mult))
                    ch.link(dve.tensor_tensor(pos[:], pos[:], cum[:, 1, :], ALU.add))
                ch.link(dve.tensor_copy(hi_i[:], pos[:]))
                ch.link(dve.tensor_scalar(hi_i[:], hi_i[:], 7, None, ALU.arith_shift_right))
                ch.link(dve.tensor_copy(hi[:], hi_i[:]))
                ch.link(dve.scalar_tensor_tensor(pos[:], hi[:], -128.0, pos[:], ALU.mult, ALU.add))
                ch.link(dve.scalar_tensor_tensor(addr[:], pos[:], float(NT), hi[:], ALU.mult, ALU.add))
                if attributes:
                    return
                for i in peeled(dve, HALVES):
                    body = ch.loop(i, 2 * 4)
                    for h in range(2):
                        if later(i):
                            dve.wait_ge(scattered[h], i * 16 * SG)
                        at = bass.ds((2 * i + h) * SG, SG)
                        body.step(dve.tensor_copy(idx[:, h, :], addr[:, at]))
                        body.step(dve.tensor_copy(stage[:, h, :, 0], oth[:, at]))
                        body.step(dve.tensor_copy(stage[:, h, :, 2], weight[:, at]))
                        body.link(dve.tensor_copy(stage[:, h, :, 1], key[:, at]))
                        dve.sem_inc(staged[h], 1)
                ch.after(body, HALVES)
                dve.wait_ge(back_in, 16)
                ch.step(dve.tensor_copy(S.end[by][:], back[:, :, 0]))
                ch.step(dve.tensor_copy(S.edge_w[:], back[:, :, 2]))
                ch.link(dve.scalar_tensor_tensor(S.local[by][:], blk[:], -float(P), back[:, :, 1],
                                                 ALU.mult, ALU.add))


def scatter_attributes(nc, S, A, sb, sem, kept):
    key, oth, addr, _ = kept
    SG, RING = 8, 5
    W = 2 + ED
    TURNS = EC // (SG * RING)
    stage, idx = sb("stage", [P, RING, SG, W]), sb("idx", [P, RING, SG], I32)
    attr_in = [sem(f"attributes_in{r}") for r in range(RING)]
    scattered = [sem(f"scattered{r}") for r in range(RING)]
    staged, go = sem("staged"), sem("go")
    edge_view = A["edge_attr_64"].rearrange("(p t) c -> p t c", p=P)

    def program(pool):
        def prepare(i, r):
            if later(i):
                pool.wait_ge(scattered[r], i * 16 * SG)
            at = bass.ds((i * RING + r) * SG, SG)
            pool.dma_start(stage[:, r, :, 2:W], edge_view[:, at, :]).then_inc(attr_in[r], 16)
            pool.tensor_copy(idx[:, r, :], addr[:, at]).then_inc(staged, 1)
            pool.tensor_copy(stage[:, r, :, 0], oth[:, at]).then_inc(staged, 1)
            pool.tensor_copy(stage[:, r, :, 1], key[:, at]).then_inc(staged, 1)

        def scatter(turns, n, r):
            pool.wait_ge(attr_in[r], turns * 16)
            pool.wait_ge(staged, n * 3)
            pool.sem_inc(go, 1)
            for t in range(SG):
                pool.indirect_dma_start(
                    out=S.records["src"], out_offset=bass.IndirectOffsetOnAxis(ap=idx[:, r, t:t + 1], axis=0),
                    in_=stage[:, r, t, :], in_offset=None).then_inc(scattered[r], 16)

        for i in peeled(pool, TURNS):
            for r in range(RING):
                prepare(i, r)
                if r:
                    scatter(i + 1, i * RING + r, r - 1)
                elif later(i):
                    scatter(i, i * RING, RING - 1)
        scatter(TURNS, TURNS * RING, RING - 1)
        for r in range(RING):
            pool.wait_ge(scattered[r], TURNS * 16 * SG)

    return program


def read_ends(nc, S, kept):
    _, _, _, blk = kept
    with phase(nc, "read_ends") as (sb, sem):
        back = sb("back", [128, NT, 2])
        back_in, taken = sem("back_in"), sem("taken")
        with nc.Block() as block:
            @block.sync
            def _(sp):
                sp.dma_start(back[:], S.records["src"].rearrange("(p t) w -> p t w", p=128)[:, :, 0:2],
                             allow_slow_non_contiguous=True).then_inc(back_in, 16)
                sp.wait_ge(back_in, 16)

            @block.vector
            def _(dve):
                dve.wait_ge(back_in, 16)
                dve.tensor_copy(S.end["src"][:], back[:, :, 0]).then_inc(taken, 1)
                dve.scalar_tensor_tensor(S.local["src"][:], blk[:], -float(P), back[:, :, 1],
                                         ALU.mult, ALU.add).then_inc(taken, 1)
                dve.wait_ge(taken, 2)


def layer_norm(nc, S, name, turn=True):
    with phase(nc, name) as (sb, sem):
        stats, mv = sb("stats", [P, NB, 6]), sb("mv", [P, NB, 2])
        var, root, inv = sb("var", [P, NB]), sb("root", [P, NB]), sb("inv", [P, NB])
        dve_step, var_ready, root_ready = sem("dve_step"), sem("var_ready"), sem("root_ready")
        normed, turned, emptied = sem("blocks_normed"), sem("blocks_turned"), sem("banks_emptied")
        with nc.Block() as block:
            @block.vector
            def _(dve):
                ch = Chain(dve, dve_step)
                for t in range(NB):
                    ch.step(dve.bn_stats(stats[:, t, :], S.x[:, t, :]))
                ch.sync()
                for t in range(NB):
                    ch.step(dve.bn_aggr(mv[:, t, :], stats[:, t, :]))
                ch.sync()
                inverse_root(ch, dve, S, mv[:, :, 1], EPS, var, root, inv, var_ready, root_ready)
                for t in range(NB):
                    dve.tensor_scalar(S.xn[:, t, :], S.x[:, t, :], mv[:, t, 0:1], inv[:, t:t + 1],
                                      ALU.subtract, ALU.mult).then_inc(normed, 1)

            @block.scalar
            def _(act):
                act.wait_ge(var_ready, 1)
                act.activation(root[:], var[:], ACT.Sqrt).then_inc(root_ready, 1)
                if turn:
                    for t in range(NB):
                        act.wait_ge(turned, t + 1)
                        act.copy(S.xT[:, :, t * P:(t + 1) * P],
                                 S.ps[:, t % 8, 0:K * P].rearrange("q (k p) -> q k p", k=K)).then_inc(emptied, 1)

            @block.tensor
            def _(pe):
                for t in range(NB if turn else 0):
                    pe.wait_ge(normed, t + 1)
                    if t >= 8:
                        pe.wait_ge(emptied, t - 7)
                    for k in range(K):
                        ins = pe.transpose(S.ps[:, t % 8, k * P:(k + 1) * P],
                                           S.xn[:, t, k * 128:(k + 1) * 128], S.ident[0:P, 0:P])
                    ins.then_inc(turned, 1)


def inverse_root(ch, dve, S, src, eps, var, root, inv, var_ready, root_ready, n=1):
    ch.link(dve.tensor_scalar(var[:], src, eps, None, ALU.add))
    dve.sem_inc(var_ready, 1)
    dve.wait_ge(root_ready, n)
    ch.link(dve.reciprocal(inv[:], root[:]))
    ch.link(dve.tensor_tensor(inv[:], inv[:], var[:], ALU.mult))
    ch.link(dve.tensor_tensor(root[:], root[:], inv[:], ALU.add))
    ch.link(dve.tensor_scalar(root[:], root[:], 0.5, None, ALU.mult))
    ch.link(dve.reciprocal(inv[:], root[:]))


class Group:

    def __init__(self, n, slot, turn, least):
        self.n, self.slot, self.turn, self.least = n, slot, turn, least

    def tiles(self):
        return bass.ds(self.n * G, G)

    def next(self):
        return Group(self.n + 1, (self.slot + 1) % U, self.turn + (self.slot + 1) // U, self.least + 1)

    def previous(self):
        return Group(self.n - 1, (self.slot - 1) % U, self.turn + (self.slot - 1) // U, self.least - 1)

    def since(self, back):
        assert isinstance(self.n, int) or self.least >= back
        return self.least >= back

    def tile_since(self, t, back):
        assert isinstance(self.n, int) or self.least * G + t >= back
        return self.least * G + t >= back


def pipeline(eng, *stages, groups=GROUPS):
    def step(i, g):
        for lag, stage in stages:
            n = U * i + (g - lag)
            if not isinstance(i, int):
                stage(Group(n, (g - lag) % U, i + (g - lag) // U, 2 * U + g - lag))
            elif 0 <= n < groups:
                stage(Group(n, n % U, n // U, n))

    for i in range(2):
        for g in range(U):
            step(i, g)
    with eng.Fori(2, groups // U) as i:
        for g in range(U):
            step(i, g)
    for g in range(max(lag for lag, _ in stages)):
        step(groups // U, g)


def gather_groups(pool, ends, table, idx, rows, free, gathered, copied, go):
    def gather(q):
        if q.since(U):
            pool.wait_ge(free, (q.n - U + 1) * G)
        pool.tensor_copy(idx[:, q.slot, :], ends[:, q.tiles()]).then_inc(copied, 1)
        pool.wait_ge(copied, q.n + 1)
        pool.sem_inc(go, 1)
        for t in range(G):
            pool.indirect_dma_start(
                out=rows[:, q.slot, t, :], out_offset=None, in_=table,
                in_offset=bass.IndirectOffsetOnAxis(ap=idx[:, q.slot, t:t + 1], axis=0))\
                .then_inc(gathered[q.slot], 16)
    pipeline(pool, (0, gather))


def rows_in(q):
    return (q.turn + 1) * 16 * G


def one_hots(dve, S, q, onehot, loc, local, located, selected):
    dve.tensor_copy(loc[:, q.slot, :], local[:, q.tiles()]).then_inc(located, 1)
    dve.wait_ge(located, q.n + 1)
    for t in range(G):
        dve.tensor_scalar(onehot[:, q.slot % onehot.shape[1], t, :], S.iota[:, 0:P], loc[:, q.slot, t:t + 1], None,
                          ALU.is_equal).then_inc(selected, 1)


def even_turn(q):
    return (q.n // 2 + 1) * 16 if isinstance(q.n, int) else (q.turn * (U // 2) + q.slot // 2 + 1) * 16


def accumulate(dve, S, q, blk, width, banks, summed, added, tiles=range(G)):
    for t in tiles:
        b = block_of(dve, blk, q, t)
        dve.wait_ge(summed, q.n * G + t + 1)
        if q.tile_since(t, 1):
            dve.wait_ge(added, q.n * G + t)
        here = S.acc[:, bass.ds(b, 1), 0:width].rearrange("p a c -> p (a c)")
        dve.tensor_tensor(here, here, S.ps[0:P, t % banks, 0:width], ALU.add).then_inc(added, 1)


def turn(pe, S, q, bank, onehot_b, selected, turned, turned_out, banks=2):
    pe.wait_ge(selected, (q.n + 1) * G)
    if q.since(banks):
        pe.wait_ge(turned_out, 2 * (q.n - banks + 1))
    for t in range(G):
        ins = pe.transpose(S.ps[:, bank + q.slot % banks, :].bitcast(BF16)[0:P, t * 128:(t + 1) * 128],
                           onehot_b[:, q.slot % 2, t, :], S.ident_b[:])
    ins.then_inc(turned, 1)


def widen(act, S, q, bank, onehot_b, onehot, onehot_t, turned, turned_out, banks=2):
    act.wait_ge(turned, q.n + 1)
    act.copy(onehot_t[:, q.slot % 2],
             S.ps[:, bank + q.slot % banks, :].bitcast(BF16)[0:P, :].rearrange("p (t e) -> p t e", e=128))\
        .then_inc(turned_out, 1)
    act.copy(onehot[:, q.slot], onehot_b[:, q.slot % 2]).then_inc(turned_out, 1)


def block_of(eng, blk, q, t):
    return eng.value_load(blk[0:1, bass.ds(q.n * G + t, 1)], min_val=0, max_val=NB - 1)


def at_block(table, b):
    return table[:, bass.ds(b, 1), :].rearrange("p a c -> p (a c)")


def leaky(ch, dve, out, x):
    ch.link(dve.scalar_tensor_tensor(out, x, 0.2, x, ALU.mult, ALU.max))


def gat(nc, S, A):
    ends, local, blk = S.end["dst"], S.local["dst"], S.blk["dst"]
    NEG = -float(2 ** 100)
    with phase(nc, "gat") as (sb, sem):
        w = sb("w", [128, K, D])
        att = sb("att", [P, 2, D])
        bias, ln_w, ln_b = sb("bias", [P, D]), sb("ln_w", [P, D]), sb("ln_b", [P, D])
        a_src, node = sb("a_src", [P, NB, HEADS]), sb("node", [P, NB, 2 * HEADS])
        most, self_e = sb("most", [P, NB, HEADS]), sb("self_e", [P, NB, HEADS])
        dve_step, act_step = sem("dve_step"), sem("act_step")

        loaded, product, evacuated, scored, stored = (
            sem(x) for x in ("loaded", "product", "evacuated", "scored", "stored"))
        ch = Chain(None, dve_step)
        with nc.Block() as block, nc.sbuf_tensor("gat_work", [P, NB, D], F32) as work:
            @block.sync
            def _(sp):
                sp.dma_start(w[:], A["L0_gnn_W"].rearrange("(k p) f -> p k f", p=128)).then_inc(loaded, 16)
                for j, n in enumerate(("L0_gnn_att_src", "L0_gnn_att_dst")):
                    sp.dma_start(att[:, j, :], row(A[n].rearrange("h c -> (h c)"))).then_inc(loaded, 16)
                for t, n in ((bias, "L0_gnn_bias"), (ln_w, "L0_gnn_ln_w"), (ln_b, "L0_gnn_ln_b")):
                    sp.dma_start(t[:], row(A[n])).then_inc(loaded, 16)
                sp.wait_ge(evacuated, NB)
                sp.wait_ge(scored, 1)
                sp.dma_start(S.rows.rearrange("(t p) c -> p t c", p=P), S.acc[:]).then_inc(stored, 16)
                sp.dma_start(S.rows8.rearrange("(t p) c -> p t c", p=P), a_src[:]).then_inc(stored, 16)
                sp.wait_ge(stored, 32)

            @block.tensor
            def _(pe):
                pe.wait_ge(loaded, 96)
                for t in range(NB):
                    if t >= 8:
                        pe.wait_ge(evacuated, t - 7)
                    for k in range(K):
                        ins = pe.matmul(S.ps[0:P, t % 8, 0:D], S.xT[:, k, t * P:(t + 1) * P], w[:, k, :],
                                        start=k == 0, stop=k == K - 1)
                    ins.then_inc(product, 1)

            @block.scalar
            def _(act):
                for t in range(NB):
                    act.wait_ge(product, t + 1)
                    act.copy(S.acc[:, t, 0:D], S.ps[0:P, t % 8, 0:D]).then_inc(evacuated, 1)

            @block.vector
            def _(dve):
                ch.eng = dve
                dve.wait_ge(loaded, 96)
                dve.wait_ge(evacuated, NB)
                for j, out in enumerate((a_src[:, :, :], node[:, :, 0:HEADS])):
                    ch.link(dve.tensor_tensor(work[:], S.acc[:, :, 0:D], bc_mid(att[:, j, :], NB), ALU.mult))
                    ch.link(dve.tensor_reduce(out, work[:].rearrange("p t (h c) -> p t h c", h=HEADS),
                                              AX, ALU.add))
                ch.link(dve.tensor_copy(S.acc[:, :, D:XG], a_src[:]))
                dve.sem_inc(scored, 1)
                ch.link(dve.tensor_copy(most[:], a_src[:]))

        gathered = [sem(f"max_gathered{u}") for u in range(U)]
        copied, go, located, masked, rounded, spread, reduced, merged = (
            sem(f"max_{x}") for x in ("copied", "go", "located", "masked", "rounded", "spread", "reduced", "merged"))
        with nc.Block() as block, ExitStack() as ctx:
            def mb(what, shape, dt=F32):
                return ctx.enter_context(nc.sbuf_tensor(f"gat_{what}", shape, dt))

            idx, rows = mb("idx", [128, U, G], I32), mb("rows8", [128, U, G, HEADS])
            loc = mb("loc", [128, U, G])
            other_node = mb("other_node", [128, U, G, P], BF16)
            short = mb("short", [128, U, G, HEADS], BF16)
            red = mb("red", [P, U, G, HEADS])

            @block.gpsimd
            def _(pool):
                gather_groups(pool, ends, S.rows8, idx, rows, spread, gathered, copied, go)

            @block.scalar
            def _(act):
                def shorten(q):
                    act.wait_ge(gathered[q.slot], rows_in(q))
                    if q.since(U):
                        act.wait_ge(spread, (q.n - U + 1) * G)
                    act.copy(short[:, q.slot], rows[:, q.slot]).then_inc(rounded, 1)
                pipeline(act, (0, shorten))

            @block.vector
            def _(dve):
                def mask(q):
                    dve.tensor_copy(loc[:, q.slot, :], local[:, q.tiles()]).then_inc(located, 1)
                    dve.wait_ge(located, q.n + 1)
                    for t in range(G):
                        dve.tensor_scalar(other_node[:, q.slot, t, :], S.iota[:, 0:P], loc[:, q.slot, t:t + 1], NEG,
                                          ALU.not_equal, ALU.mult).then_inc(masked, 1)

                def greatest_of(t):
                    def stage(q):
                        dve.wait_ge(spread, q.n * G + t + 1)
                        k = 2 * (t % 4)
                        dve.tensor_reduce(red[:, q.slot, t, :],
                                          S.ps[0:P, k:k + 2, :].rearrange("p k (h e) -> p (k h) e", e=128),
                                          AX, ALU.max).then_inc(reduced, 1)
                    return stage

                def merge(t):
                    def stage(q):
                        b = block_of(dve, blk, q, t)
                        dve.wait_ge(reduced, q.n * G + t + 1)
                        if q.tile_since(t, 1):
                            dve.wait_ge(merged, q.n * G + t)
                        here = at_block(most, b)
                        dve.tensor_tensor(here, here, red[:, q.slot, t, :], ALU.max).then_inc(merged, 1)
                    return stage

                pipeline(dve, (0, mask), *(
                    stage for t in range(G) for stage in ((1, greatest_of(t)), (2, merge(t)))))

            @block.tensor
            def _(pe):
                def scatter(q):
                    pe.wait_ge(masked, (q.n + 1) * G)
                    pe.wait_ge(rounded, q.n + 1)
                    for t in range(G):
                        k = 2 * (t % 4)
                        if q.tile_since(t, 4):
                            pe.wait_ge(reduced, q.n * G + t - 3)
                        for j in range(2):
                            pe.matmul(S.ps[0:P, k + j, :], other_node[:, q.slot, t, :], bc_mid(S.ident_b[:], 4),
                                      start=True, stop=False, skip_group_check=True)
                        for hd in range(HEADS):
                            ins = pe.matmul(S.ps[0:P, k + hd // 4, (hd % 4) * 128:(hd % 4 + 1) * 128],
                                            short[:, q.slot, t, hd:hd + 1].to_broadcast([128, P]),
                                            S.ident_b[:], start=False, stop=True, skip_group_check=True)
                        ins.then_inc(spread, 1)
                pipeline(pe, (0, scatter))

        gathered = [sem(f"gathered{u}") for u in range(U)]
        copied, go, located, selected, turned, turned_out, looked_up, scoring = (
            sem(x) for x in ("copied", "go", "located", "selected", "turned", "turned_out", "looked_up", "scoring"))
        shifted, weighted, scaled, summed, added, self_ready, self_exp, nodes_ready = (
            sem(x) for x in ("shifted", "weighted", "scaled", "summed", "added", "self_ready", "self_exp",
                             "nodes_ready"))
        with nc.Block() as block, ExitStack() as ctx:
            def mb(what, shape, dt=F32):
                return ctx.enter_context(nc.sbuf_tensor(f"gat_{what}2", shape, dt))

            idx, rows = mb("idx", [128, U, G], I32), mb("rows", [128, U, G, XG])
            loc = mb("loc", [128, U, G])
            onehot_b, onehot = mb("onehot_b", [128, 2, G, P], BF16), mb("onehot", [128, U, G, P])
            onehot_t = mb("onehot_t", [P, 2, G, 128])
            score = mb("score", [128, 2, G, HEADS])

            @block.gpsimd
            def _(pool):
                gather_groups(pool, ends, S.rows, idx, rows, summed, gathered, copied, go)

            @block.vector
            def _(dve):
                ch.eng = dve
                ch.link(dve.tensor_tensor(most[:], most[:], node[:, :, 0:HEADS], ALU.add))
                leaky(ch, dve, node[:, :, HEADS:], most[:])
                ch.link(dve.tensor_tensor(self_e[:], a_src[:], node[:, :, 0:HEADS], ALU.add))
                leaky(ch, dve, self_e[:], self_e[:])
                ch.link(dve.tensor_tensor(self_e[:], self_e[:], node[:, :, HEADS:], ALU.subtract))
                dve.sem_inc(self_ready, 1)
                dve.wait_ge(self_exp, 1)
                v = S.acc[:, :, 0:D].rearrange("p t (h c) -> p t h c", h=HEADS)
                for t in range(NB):
                    ch.step(dve.tensor_tensor(v[:, t], v[:, t], bc(self_e[:, t, :], HC), ALU.mult))
                ch.link(dve.tensor_copy(S.acc[:, :, D:XG], self_e[:]))
                dve.sem_inc(nodes_ready, 1)

                def scores(q):
                    dve.wait_ge(gathered[q.slot], rows_in(q))
                    dve.wait_ge(looked_up, q.n + 1)
                    c = Chain(dve, scoring, q.n * 3)
                    e = score[:, q.slot % 2]
                    of_node = S.ps[:, 6 + q.slot % 2, 0:128].rearrange("e (t c) -> e t c", t=G)
                    c.link(dve.tensor_tensor(e, rows[:, q.slot, :, D:XG], of_node[:, :, 0:HEADS], ALU.add))
                    leaky(c, dve, e, e)
                    c.link(dve.tensor_tensor(e, e, of_node[:, :, HEADS:], ALU.subtract))
                    dve.tensor_scalar(e, e, 60.0, None, ALU.min).then_inc(shifted, 1)

                def scale(q):
                    dve.wait_ge(weighted, q.n + 1)
                    v = rows[:, q.slot, :, 0:D].rearrange("e t (h c) -> e t h c", h=HEADS)
                    wt = rows[:, q.slot, :, D:XG].unsqueeze(3).to_broadcast([128, G, HEADS, HC])
                    dve.tensor_tensor(v, v, wt, ALU.mult).then_inc(scaled, 1)

                pipeline(dve, (0, lambda q: one_hots(dve, S, q, onehot_b, loc, local, located, selected)),
                         (1, scores),
                         (2, lambda q: accumulate(dve, S, q, blk, XG, 4, summed, added)),
                         (1, scale))

            @block.scalar
            def _(act):
                act.wait_ge(self_ready, 1)
                act.activation(self_e[:], self_e[:], ACT.Exp).then_inc(self_exp, 1)

                def weigh(q):
                    act.wait_ge(shifted, q.n + 1)
                    act.activation(rows[:, q.slot, :, D:XG], score[:, q.slot % 2], ACT.Exp).then_inc(weighted, 1)

                pipeline(act, (0, lambda q: widen(act, S, q, 4, onehot_b, onehot, onehot_t, turned, turned_out)),
                         (1, weigh))

            @block.tensor
            def _(pe):
                pe.wait_ge(nodes_ready, 1)

                def total(q):
                    pe.wait_ge(scaled, q.n + 1)
                    for t in range(G):
                        if q.tile_since(t, 4):
                            pe.wait_ge(added, q.n * G + t - 3)
                        pe.matmul(S.ps[0:P, t % 4, 0:XG], onehot[:, q.slot, t, :], rows[:, q.slot, t, :],
                                  start=True, stop=True).then_inc(summed, 1)

                def look_up(q):
                    pe.wait_ge(turned_out, 2 * q.n + 2)
                    if q.since(2):
                        pe.wait_ge(shifted, q.n - 1)
                    for t in range(G):
                        b = block_of(pe, blk, q, t)
                        ins = pe.matmul(S.ps[:, 6 + q.slot % 2, t * 16:(t + 1) * 16],
                                        onehot_t[:, q.slot % 2, t, :], at_block(node, b), start=True, stop=True)
                    ins.then_inc(looked_up, 1)

                pipeline(pe, (0, lambda q: turn(pe, S, q, 4, onehot_b, selected, turned, turned_out)),
                         (2, total), (0, look_up))

        var_ready, root_ready = sem("var_ready"), sem("root_ready")
        with nc.Block() as block, ExitStack() as ctx:
            stats = ctx.enter_context(nc.sbuf_tensor("gat_stats", [P, NB, 6], F32))
            mv = ctx.enter_context(nc.sbuf_tensor("gat_mv", [P, NB, 2], F32))
            var, root, inv = (ctx.enter_context(nc.sbuf_tensor(f"gat_{x}", [P, NB], F32)) for x in ("var", "root", "inv"))

            @block.scalar
            def _(act):
                act.wait_ge(var_ready, 1)
                act.activation(root[:], var[:], ACT.Sqrt).then_inc(root_ready, 1)

            @block.vector
            def _(dve):
                ch.eng = dve
                ch.link(dve.reciprocal(self_e[:], S.acc[:, :, D:XG]))
                v = S.acc[:, :, 0:D].rearrange("p t (h c) -> p t h c", h=HEADS)
                for t in range(NB):
                    ch.step(dve.tensor_tensor(v[:, t], v[:, t], bc(self_e[:, t, :], HC), ALU.mult))
                ch.sync()
                y = S.acc[:, :, 0:D]
                ch.link(dve.tensor_tensor(y, y, bc_mid(bias[:], NB), ALU.add))
                ch.link(dve.tensor_tensor(y, y, S.xn[:], ALU.add))
                norm_into(ch, dve, S, y, stats, mv, var, root, inv, var_ready, root_ready)
                ch.link(dve.tensor_tensor(y, y, bc_mid(ln_w[:], NB), ALU.mult))
                ch.link(dve.tensor_tensor(S.x[:], S.x[:], bc_mid(ln_b[:], NB), ALU.add))
                ch.link(dve.tensor_tensor(S.x[:], S.x[:], y, ALU.add))


def norm_into(ch, dve, S, y, stats, mv, var, root, inv, var_ready, root_ready):
    for t in range(NB):
        ch.step(dve.bn_stats(stats[:, t, :], y[:, t, :]))
    ch.sync()
    for t in range(NB):
        ch.step(dve.bn_aggr(mv[:, t, :], stats[:, t, :]))
    ch.sync()
    inverse_root(ch, dve, S, mv[:, :, 1], EPS, var, root, inv, var_ready, root_ready)
    for t in range(NB):
        ch.step(dve.tensor_scalar(y[:, t, :], y[:, t, :], mv[:, t, 0:1], inv[:, t:t + 1],
                                  ALU.subtract, ALU.mult))
    ch.sync()


def expert_weights(nc, S, A, name, n, rule, weights, bias, comb, comb_t, b2=None, target=None, base=None,
                   picked=None):
    with phase(nc, name) as (sb, sem):
        w = sb("w", [128, K, n])
        b_row = sb("b_row", [P, n]) if bias is not None else None
        b2_s = sb("b2", [n, D]) if b2 is not None else None
        logits, ex = sb("logits", [P, NB, n]), sb("ex", [P, NB, n])
        best, best_at, at_f = sb("best", [P, NB, 8]), sb("best_at", [P, NB, 8], mybir.dt.uint32), sb("at_f", [P, NB, 2])
        col, pair = sb("col", [P, NB]), sb("pair", [P, NB, 2])
        if picked:
            at_f, pair = picked
        dve_step, act_step = sem("dve_step"), sem("act_step")
        loaded, product, exp_ready, exp_done, combined, turned, emptied, biased, added = (
            sem(x) for x in ("loaded", "product", "exp_ready", "exp_done", "combined", "turned", "emptied",
                             "biased", "added"))
        n_loads = 1 + (bias is not None) + (b2 is not None)
        per_bank = 512 // n
        nbanks = -(-NB // per_bank)
        with nc.Block() as block:
            @block.sync
            def _(sp):
                sp.dma_start(w[:], weights.rearrange("(k p) e -> p k e", p=128)).then_inc(loaded, 16)
                if bias is not None:
                    sp.dma_start(b_row[:], row(bias)).then_inc(loaded, 16)
                if b2 is not None:
                    sp.dma_start(b2_s[:], b2).then_inc(loaded, 16)
                sp.wait_ge(loaded, 16 * n_loads)

            @block.tensor
            def _(pe):
                pe.wait_ge(loaded, 16 * n_loads)
                for t in range(NB):
                    bank, at = t // per_bank, (t % per_bank) * n
                    for k in range(K):
                        ins = pe.matmul(S.ps[0:P, bank, at:at + n], S.xT[:, k, t * P:(t + 1) * P], w[:, k, :],
                                        start=k == 0, stop=k == K - 1)
                    ins.then_inc(product, 1)
                pe.wait_ge(combined, 1)
                for t in range(NB):
                    if t >= 2:
                        pe.wait_ge(emptied, t - 1)
                    pe.transpose(S.ps[0:n, 2 + t % 2, 0:P], comb[:, t, :], S.ident[0:P, 0:P]).then_inc(turned, 1)
                    if b2 is not None:
                        pe.wait_ge(emptied, t + 1)
                        if t >= 4:
                            pe.wait_ge(added, t - 3)
                        pe.matmul(S.ps[0:P, 4 + t % 4, 0:D], comb_t[0:n, t * P:(t + 1) * P], b2_s[:],
                                  start=True, stop=True).then_inc(biased, 1)

            @block.scalar
            def _(act):
                if rule != "top1":
                    act.wait_ge(exp_ready, 1)
                    src = pair if rule == "gates" else ex
                    act.activation(src[:], src[:], ACT.Exp).then_inc(exp_done, 1)
                for t in range(NB):
                    act.wait_ge(turned, t + 1)
                    act.copy(comb_t[0:n, t * P:(t + 1) * P], S.ps[0:n, 2 + t % 2, 0:P]).then_inc(emptied, 1)

            @block.vector
            def _(dve):
                ch = Chain(dve, dve_step)
                dve.wait_ge(product, NB)
                for b in range(nbanks):
                    t0, t1 = b * per_bank, min(NB, (b + 1) * per_bank)
                    src = S.ps[0:P, b, 0:(t1 - t0) * n].rearrange("p (t e) -> p t e", e=n)
                    if bias is not None:
                        dve.wait_ge(loaded, 16 * n_loads)
                        ch.step(dve.tensor_tensor(logits[:, t0:t1, :], src, bc_mid(b_row[:], t1 - t0), ALU.add))
                    else:
                        ch.step(dve.tensor_copy(logits[:, t0:t1, :], src))
                ch.sync()
                ranked = logits
                if rule in ("top2", "soft"):
                    ch.link(dve.tensor_reduce(col[:], logits[:], AX, ALU.max))
                    ch.link(dve.tensor_tensor(ex[:], logits[:], bc(col[:], n), ALU.subtract))
                    dve.sem_inc(exp_ready, 1)
                    dve.wait_ge(exp_done, 1)
                    ch.link(dve.tensor_reduce(col[:], ex[:], AX, ALU.add))
                    ch.link(dve.reciprocal(col[:], col[:]))
                    out = comb if rule == "soft" else ex
                    ch.link(dve.tensor_tensor(out[:], ex[:], bc(col[:], n), ALU.mult))
                    ranked = ex
                if rule != "soft":
                    for t in range(NB):
                        ch.step(dve.max(best[:, t, :], ranked[:, t, :]))
                    ch.sync()
                    for t in range(NB):
                        ch.step(dve.max_index(best_at[:, t, :], best[:, t, :], ranked[:, t, :]))
                    ch.sync()
                    ch.link(dve.tensor_copy(at_f[:], best_at[:, :, 0:2]))
                    if rule == "gates":
                        ch.link(dve.tensor_tensor(pair[:], best[:, :, 0:2], bc(best[:, :, 0], 2), ALU.subtract))
                        dve.sem_inc(exp_ready, 1)
                        dve.wait_ge(exp_done, 1)
                    elif rule == "top2":
                        ch.link(dve.tensor_copy(pair[:], best[:, :, 0:2]))
                    if rule != "top1":
                        ch.link(dve.tensor_tensor(col[:], pair[:, :, 0], pair[:, :, 1], ALU.add))
                        ch.link(dve.tensor_scalar(col[:], col[:], 1e-12, None, ALU.max))
                        ch.link(dve.reciprocal(col[:], col[:]))
                        ch.link(dve.tensor_tensor(pair[:], pair[:], bc(col[:], 2), ALU.mult))
                    ids = bc_mid(S.iota[0:P, 0:n], NB)
                    ch.link(dve.tensor_tensor(comb[:], ids, bc(at_f[:, :, 0], n), ALU.is_equal))
                    if rule != "top1":
                        ch.link(dve.tensor_tensor(comb[:], comb[:], bc(pair[:, :, 0], n), ALU.mult))
                        ch.link(dve.tensor_tensor(logits[:], ids, bc(at_f[:, :, 1], n), ALU.is_equal))
                        ch.link(dve.tensor_tensor(logits[:], logits[:], bc(pair[:, :, 1], n), ALU.mult))
                        ch.link(dve.tensor_tensor(comb[:], comb[:], logits[:], ALU.add))
                dve.sem_inc(combined, 1)
                if b2 is not None:
                    if base is not None and not isinstance(base, str):
                        ch.link(dve.tensor_tensor(target, target, base, ALU.add))
                    for t in range(NB):
                        dve.wait_ge(biased, t + 1)
                        src = S.ps[0:P, 4 + t % 4, 0:D]
                        if base is not None:
                            ins = dve.tensor_tensor(target[:, t, :], target[:, t, :], src, ALU.add)
                        else:
                            ins = dve.tensor_copy(target[:, t, :], src)
                        ins.then_inc(added, 1)


def bank_before(m, banks, per):
    return m - banks if m >= banks else max(n for n in range(per) if n % banks == m % banks) - per


def experts(nc, S, name, steps, w_first, w_second, w_last, F, act_first, act_second, comb, target,
            masked=None, pool_program=None):
    KF = F // 128
    deep = w_second is not None
    BANKS = 2 if (deep or masked is not None) else 4
    with phase(nc, name) as (sb, sem):
        w1, w2 = sb("w1", [128, 2, K, F]), sb("w2", [128, 2, KF, D])
        wm = sb("wm", [128, 2, KF, F]) if deep else None
        hid = sb("hid", [128, 2, KF, CH * P])
        hid2 = sb("hid2", [128, 2, KF, CH * P]) if deep else None
        consts = sb("consts", [128, 2, len(act_first.tables) + len(act_second.tables if deep else ()), KF])
        fetched, go, pe_go = sem("constants_fetched"), sem("go"), sem("pe_go")
        loaded = [sem(f"weights_loaded{h}") for h in range(2)]
        done = [sem(f"weights_used{h}") for h in range(2)]
        first, hidden, middle, hidden2, last, added, masks, masked_sem = (
            sem(x) for x in ("first", "hidden", "middle", "hidden2", "last", "added", "masks", "masked"))
        LOADS = 2 if not deep and masked is None else 3
        PER = steps // 2
        items = [(h, c) for h in range(2) for c in range(NCHUNK)]
        NI = len(items)

        def cols(c):
            return CH * c * P, len(chunk_blocks(c)) * P

        with nc.Block() as block:
            if pool_program:
                block.gpsimd(pool_program)

            @block.sync
            def _(sp):
                for i in peeled(sp, PER):
                    for h in range(2):
                        if later(i):
                            sp.wait_ge(done[h], i)
                        e = 2 * i + h
                        if masked is not None:
                            for j in range(2):
                                sp.dma_start(w1[:, h, :, j * 64:(j + 1) * 64], w_first(e)[:, j]).then_inc(loaded[h], 16)
                        else:
                            sp.dma_start(w1[:, h], w_first(e)).then_inc(loaded[h], 16)
                        if deep:
                            sp.dma_start(wm[:, h], w_second(e)).then_inc(loaded[h], 16)
                        sp.dma_start(w2[:, h], w_last(e)).then_inc(loaded[h], 16)

            @block.tensor
            def _(pe):
                def stage_first(i, j):
                    h, c = items[j]
                    at, width = cols(c)
                    if c == 0:
                        pe.wait_ge(loaded[h], (i + 1) * 16 * LOADS)
                    for f in range(KF):
                        m = j * KF + f
                        if later(i) or m >= BANKS:
                            pe.wait_ge(hidden, i * NI * KF + m - BANKS + 1)
                        for k in range(K):
                            ins = pe.matmul(S.ps[:, m % BANKS, 0:width], w1[:, h, k, f * 128:(f + 1) * 128],
                                            S.xT[:, k, at:at + width], start=k == 0, stop=k == K - 1)
                        ins.then_inc(first, 1)
                    if masked is not None:
                        sel, comb_b = masked
                        if later(i) or j >= 2:
                            pe.wait_ge(masked_sem, i * NI + j - 1)
                            pe.sem_inc(pe_go, 1)
                        which = (2 * i + h) if later(i) else h
                        pe.matmul(S.ps[:, 2 + j % 2, 0:width],
                                  sel[:, bass.ds(which, 1), :].rearrange("e a p -> e (a p)"),
                                  comb_b[:, at:at + width], start=True, stop=True).then_inc(masks, 1)

                def stage_middle(i, j):
                    h, c = items[j]
                    at, width = cols(c)
                    pe.wait_ge(hidden, i * NI * KF + (j + 1) * KF)
                    for f in range(KF):
                        m = j * KF + f
                        if later(i) or m >= 2:
                            pe.wait_ge(hidden2, i * NI * KF + m - 1)
                        for k in range(KF):
                            ins = pe.matmul(S.ps[:, 2 + m % 2, 0:width], wm[:, h, k, f * 128:(f + 1) * 128],
                                            hid[:, j % 2, k, 0:width], start=k == 0, stop=k == KF - 1)
                        ins.then_inc(middle, 1)

                def stage_last(i, j):
                    h, c = items[j]
                    src = hid2 if deep else hid
                    if masked is not None:
                        pe.wait_ge(masked_sem, i * NI + j + 1)
                    else:
                        pe.wait_ge(hidden2 if deep else hidden, i * NI * KF + (j + 1) * KF)
                    for n, t in enumerate(chunk_blocks(c)):
                        m = h * NB + t
                        if later(i) or m >= 4:
                            pe.wait_ge(added, i * 2 * NB + bank_before(m, 4, 2 * NB) + 1)
                        for k in range(KF):
                            ins = pe.matmul(S.ps[0:P, 4 + m % 4, 0:D], src[:, j % 2, k, n * P:(n + 1) * P],
                                            w2[:, h, k, :], start=k == 0, stop=k == KF - 1)
                        ins.then_inc(last, 1)

                lag = 2 if deep else 1
                for i in peeled(pe, PER):
                    for s in range(NI + lag):
                        if s < NI:
                            stage_first(i, s)
                        if deep and 1 <= s <= NI:
                            stage_middle(i, s - 1)
                        if s >= lag:
                            stage_last(i, s - lag)

            @block.scalar
            def _(act):
                def layer(i, j, src_sem, out_sem, out, bank0, fn, n0, free_after):
                    h, c = items[j]
                    at, width = cols(c)
                    for f in range(KF):
                        m = j * KF + f
                        act.wait_ge(src_sem, i * NI * KF + m + 1)
                        if f == 0 and (later(i) or j >= 2):
                            free_after(i, j)
                        mine = [consts[:, h, n0 + n, f:f + 1] for n in range(len(fn.tables))]
                        fn.apply(act, out[:, j % 2, f, 0:width],
                                 S.ps[:, bank0 + m % (BANKS if bank0 == 0 else 2), 0:width],
                                 mine).then_inc(out_sem, 1)

                def products_over(i, j):
                    h, c = items[j - 2] if j >= 2 else items[NI - 2 + j]
                    upto = h * NB + chunk_blocks(c)[-1] + 1
                    act.wait_ge(last, (i * 2 * NB + upto) if j >= 2 else (i * 2 * NB - 2 * NB + upto))

                def middle_over(i, j):
                    act.wait_ge(middle, i * NI * KF + (j - 1) * KF)

                def fetch(i, h):
                    e = 2 * i + h
                    if later(i):
                        act.wait_ge(hidden2 if deep else hidden, i * NI * KF - NI * KF + (h + 1) * NCHUNK * KF)
                        act.sem_inc(go, 1)
                    tables = act_first.tables + (act_second.tables if deep else [])
                    for n, (table, at) in enumerate(tables):
                        src = table[:, bass.ds(e * KF + at, KF)] if later(i) else table[:, at + e * KF:at + (e + 1) * KF]
                        ins = act.copy(consts[:, h, n, :], src)
                        ins.then_inc(fetched, 1)
                    act.wait_ge(fetched, (2 * i + h + 1) * len(tables))

                for i in peeled(act, PER):
                    for s in range(NI + (1 if deep else 0)):
                        if s < NI and items[s][1] == 0:
                            fetch(i, items[s][0])
                        if s < NI:
                            layer(i, s, first, hidden, hid, 0, act_first, 0, middle_over if deep else products_over)
                        if deep and s >= 1:
                            layer(i, s - 1, middle, hidden2, hid2, 2, act_second,
                                  len(act_first.tables), products_over)

            @block.vector
            def _(dve):
                def mask(i, j):
                    at, width = cols(items[j][1])
                    dve.wait_ge(masks, i * NI + j + 1)
                    dve.wait_ge(hidden, i * NI + j + 1)
                    v = hid[:, j % 2, 0, 0:width]
                    dve.tensor_tensor(v, v, S.ps[:, 2 + j % 2, 0:width], ALU.mult).then_inc(masked_sem, 1)

                for i in peeled(dve, PER):
                    for j in range(NI + (1 if masked is not None else 0)):
                        if masked is not None and j < NI:
                            mask(i, j)
                        jj = j - 1 if masked is not None else j
                        if jj < 0:
                            continue
                        h, c = items[jj]
                        e = 2 * i + h
                        for t in chunk_blocks(c):
                            m = h * NB + t
                            dve.wait_ge(last, i * 2 * NB + m + 1)
                            src, dst = S.ps[0:P, 4 + m % 4, 0:D], target[:, t, 0:D]
                            if later(i) or m >= NB:
                                dve.wait_ge(added, i * 2 * NB + m - NB + 1)
                            if masked is not None:
                                ins = dve.tensor_tensor(dst, dst, src, ALU.add)
                            else:
                                ins = dve.scalar_tensor_tensor(
                                    dst, src, comb[:, t, bass.ds(e, 1)] if later(i) else comb[:, t, e:e + 1],
                                    dst, ALU.mult, ALU.add)
                            ins.then_inc(added, 1)
                            if t == NB - 1:
                                dve.sem_inc(done[h], 1)


class Layer:

    def __init__(self, function, bias, scale=None):
        self.function, self.tables = function, [bias] + ([scale] if scale else [])

    def apply(self, act, out, in_, mine):
        scale = {"scale": mine[1]} if len(mine) > 1 else {}
        return act.activation(out, in_, self.function, bias=mine[0], **scale)


def by_expert(w):
    return lambda e: (w[e] if isinstance(e, int) else w[bass.ds(e, 1)].rearrange("a k f -> (a k) f"))\
        .rearrange("(k p) f -> p k f", p=128)


def ffn0(nc, S, A):
    with phase(nc, "by_src") as (sb, sem):
        kept = sb("key", [P, EC]), sb("oth", [P, EC]), sb("addr", [P, EC], I32), sb("blk", [128, NT])
        sort_edges(nc, S, A, "src", kept)
        scatter = scatter_attributes(nc, S, A, sb, sem, kept)
        comb, comb_t = sb("comb", [P, NB, 8]), sb("comb_t", [8, N])
        expert_weights(nc, S, A, "route0", 8, "top2", S.turned["L0_ffn_router_w"], None, comb, comb_t,
                       b2=A["L0_ffn_b2"], target=S.x[:], base=S.xn[:])
        experts(nc, S, "experts0", 8, by_expert(A["L0_ffn_w1"]), None, by_expert(A["L0_ffn_w2"]), 256,
                Layer(ACT.Gelu, (S.pcol, S.column["L0_ffn_b1"])), None, comb, S.x, pool_program=scatter)
        read_ends(nc, S, kept)


def mpnn(nc, S, A):
    ends, local, blk = S.end["src"], S.local["src"], S.blk["src"]
    w1t = S.turned["L1_gnn_W1"]
    with phase(nc, "mpnn") as (sb, sem):
        dve_step = sem("dve_step")
        ch = Chain(None, dve_step)
        own = sb("own", [P, NB, D])
        w1c = sb("w1c", [ED, D])
        loaded, product, out_own, out_other, stored = (
            sem(x) for x in ("loaded", "product", "out_own", "out_other", "stored"))
        with nc.Block() as block, ExitStack() as ctx:
            w1 = ctx.enter_context(nc.sbuf_tensor("mpnn_w1", [128, 2, K, D], F32))
            b1 = ctx.enter_context(nc.sbuf_tensor("mpnn_b1", [P, D], F32))

            @block.sync
            def _(sp):
                for j in range(2):
                    sp.dma_start(w1[:, j], w1t[j * D:(j + 1) * D, :].rearrange("(k p) f -> p k f", p=128))\
                      .then_inc(loaded, 16)
                sp.dma_start(w1c[:], w1t[2 * D:2 * D + ED, :]).then_inc(loaded, 16)
                sp.dma_start(b1[:], row(A["L1_gnn_b1"])).then_inc(loaded, 16)
                sp.wait_ge(loaded, 64)
                sp.wait_ge(out_other, NB)
                sp.dma_start(S.rows_b.rearrange("(t p) c -> p t c", p=P), S.acc[:, :, 0:D]).then_inc(stored, 16)
                sp.wait_ge(stored, 16)

            @block.tensor
            def _(pe):
                pe.wait_ge(loaded, 64)
                for t in range(NB):
                    if t >= 4:
                        pe.wait_ge(out_own, t - 3)
                        pe.wait_ge(out_other, t - 3)
                    for j in range(2):
                        for k in range(K):
                            ins = pe.matmul(S.ps[0:P, 2 * (t % 4) + j, 0:D], S.xT[:, k, t * P:(t + 1) * P],
                                            w1[:, j, k, :], start=k == 0, stop=k == K - 1)
                    ins.then_inc(product, 1)

            @block.scalar
            def _(act):
                for t in range(NB):
                    act.wait_ge(product, t + 1)
                    act.copy(S.acc[:, t, 0:D], S.ps[0:P, 2 * (t % 4) + 1, 0:D]).then_inc(out_other, 1)

            @block.vector
            def _(dve):
                dve.wait_ge(loaded, 64)
                for t in range(NB):
                    dve.wait_ge(product, t + 1)
                    dve.tensor_tensor(own[:, t, :], S.ps[0:P, 2 * (t % 4), 0:D], b1[:], ALU.add).then_inc(out_own, 1)

        gathered = [sem(f"gathered{u}") for u in range(U)]
        attr_in = [sem(f"attributes{h}") for h in range(2)]
        (copied, go, located, selected, turned, turned_out, widened, products, messages, rectified, summed, added,
         ready) = (sem(x) for x in ("copied", "go", "located", "selected", "turned", "turned_out", "widened",
                                    "products", "messages", "rectified", "summed", "added", "ready"))
        with nc.Block() as block, ExitStack() as ctx:
            def mb(what, shape, dt=F32):
                return ctx.enter_context(nc.sbuf_tensor(f"mpnn_{what}", shape, dt))

            idx, rows = mb("idx", [128, U, G], I32), mb("rows", [128, U, G, D + 1])
            attr, attr_t = mb("attr", [128, 2, G, 2 + ED]), mb("attr_t", [ED, 2, G, 128])
            loc = mb("loc", [128, U, G])
            onehot_b, onehot = mb("onehot_b", [128, 2, G, P], BF16), mb("onehot", [128, 2, G, P])
            onehot_t = mb("onehot_t", [P, 2, G, 128])
            view = S.records["src"].rearrange("(p t) w -> p t w", p=128)
            PB = 3

            @block.sync
            def _(sp):
                def load(q):
                    if q.since(2):
                        sp.wait_ge(turned_out, 2 * (q.n - 1))
                    sp.dma_start(attr[:, q.slot % 2], view[:, q.tiles(), :]).then_inc(attr_in[q.slot % 2], 16)
                pipeline(sp, (0, load))

            @block.gpsimd
            def _(pool):
                gather_groups(pool, ends, S.rows_b, idx, rows[:, :, :, 0:D], summed, gathered, copied, go)

            @block.vector
            def _(dve):
                dve.memset(S.acc[:], 0.0).then_inc(ready, 1)
                dve.memset(rows[:, :, :, D:D + 1], 1.0).then_inc(ready, 1)
                dve.wait_ge(ready, 2)

                def select(q):
                    if q.since(2):
                        dve.wait_ge(widened, q.n - 1)
                    one_hots(dve, S, q, onehot_b, loc, local, located, selected)

                def message(t):
                    def stage(q):
                        if t == 0:
                            dve.wait_ge(gathered[q.slot], rows_in(q))
                        dve.wait_ge(products, q.n * G + t + 1)
                        v = rows[:, q.slot, t, 0:D]
                        dve.tensor_tensor(v, v, S.ps[:, 2 + t % PB, 0:D], ALU.add).then_inc(messages, 1)
                    return stage

                pipeline(dve, (0, select), *(
                    stage for t in range(G) for stage in (
                        (1, message(t)),
                        (2, lambda q, t=t: accumulate(dve, S, q, blk, D + 1, 2, summed, added, [t])))))

            @block.scalar
            def _(act):
                def turn_out(q):
                    act.wait_ge(turned, q.n + 1)
                    act.copy(onehot_t[:, q.slot % 2],
                             S.ps[:, 5, :].bitcast(BF16)[0:P, :].rearrange("p (t e) -> p t e", e=128))\
                       .then_inc(turned_out, 1)
                    act.copy(attr_t[:, q.slot % 2],
                             S.ps[0:ED, 6:8, :].rearrange("p k (t e) -> p (k t) e", e=128)).then_inc(turned_out, 1)

                def rectify(q):
                    for half in range(2):
                        t = half * (G // 2)
                        act.wait_ge(messages, q.n * G + t + G // 2)
                        v = rows[:, q.slot, t:t + G // 2, 0:D]
                        act.activation(v, v, ACT.Relu).then_inc(rectified, 1)

                def widen_one_hots(q):
                    if q.since(2):
                        act.wait_ge(summed, (q.n - 1) * G)
                    act.copy(onehot[:, q.slot % 2], onehot_b[:, q.slot % 2]).then_inc(widened, 1)

                pipeline(act, (0, turn_out), (1, rectify), (0, widen_one_hots))

            @block.tensor
            def _(pe):
                def turn_both(q):
                    pe.wait_ge(selected, (q.n + 1) * G)
                    pe.wait_ge(attr_in[q.slot % 2], even_turn(q))
                    if q.since(1):
                        pe.wait_ge(turned_out, 2 * q.n)
                    for t in range(G):
                        pe.transpose(S.ps[:, 5, :].bitcast(BF16)[0:P, t * 128:(t + 1) * 128],
                                     onehot_b[:, q.slot % 2, t, :], S.ident_b[:])
                        ins = pe.transpose(S.ps[0:ED, 6 + t // 4, (t % 4) * 128:(t % 4 + 1) * 128],
                                           attr[:, q.slot % 2, t, 2:2 + ED], S.ident[:])
                    ins.then_inc(turned, 1)

                def product_of(t):
                    def stage(q):
                        if t == 0:
                            pe.wait_ge(turned_out, 2 * q.n + 2)
                        b = block_of(pe, blk, q, t)
                        if q.tile_since(t, PB):
                            pe.wait_ge(messages, q.n * G + t + 1 - (PB if t >= PB else 2 + (t == 2) * 1))
                        o = S.ps[:, 2 + t % PB, 0:D]
                        pe.matmul(o, onehot_t[:, q.slot % 2, t, :], at_block(own, b), start=True, stop=False)
                        pe.matmul(o, attr_t[:, q.slot % 2, t, :], w1c[:], start=False, stop=True).then_inc(products, 1)
                    return stage

                def sum_of(t):
                    def stage(q):
                        if t == 0:
                            pe.wait_ge(rectified, 2 * q.n + 2)
                            pe.wait_ge(widened, q.n + 1)
                        if q.tile_since(t, 2):
                            pe.wait_ge(added, q.n * G + t - 1)
                        pe.matmul(S.ps[0:P, t % 2, 0:D + 1], onehot[:, q.slot % 2, t, :], rows[:, q.slot, t, :],
                                  start=True, stop=True).then_inc(summed, 1)
                    return stage

                pe.wait_ge(ready, 2)
                pipeline(pe, (0, turn_both), *(
                    stage for t in range(G) for stage in ((1, product_of(t)), (2, sum_of(t)))))
        gru(nc, S, A)


def gru(nc, S, A):
    with phase(nc, "gru") as (sb, sem):
        w2, wi, wh = sb("w2", [128, K, D]), sb("wi", [128, K, 3 * D]), sb("wh", [128, K, 3 * D])
        b2, bi, bh = sb("b2", [1, D]), sb("bi", [P, 3 * D]), sb("bh", [P, 3 * D])
        b_rz, b_n = sb("b_rz", [P, 2 * D]), sb("b_n", [P, 2 * D])
        sums_t, degree = sb("sums_t", [128, 2, K, P]), sb("degree", [1, 2, P])
        agg = sb("agg", [128, 2, K, P])
        rz, nn = sb("rz", [P, 3, 2 * D]), sb("nn", [P, 3, 2 * D])
        (loaded, dve_step, turned, turned_out, aggregated, agg_out, gates, gates_out, sig, cand, tanh) = (
            sem(x) for x in ("loaded", "dve_step", "turned", "turned_out", "aggregated", "agg_out", "gates",
                             "gates_out", "sigmoids", "candidates", "tanhs"))
        with nc.Block() as block:
            @block.sync
            def _(sp):
                for dst, n in ((w2, "L1_gnn_W2"), (wi, "L1_gnn_W_ih"), (wh, "L1_gnn_W_hh")):
                    sp.dma_start(dst[:], S.turned[n].rearrange("(k p) f -> p k f", p=128)).then_inc(loaded, 16)
                sp.dma_start(b2[:], A["L1_gnn_b2"].rearrange("(a d) -> a d", a=1)).then_inc(loaded, 16)
                sp.dma_start(bi[:], row(A["L1_gnn_b_ih"])).then_inc(loaded, 16)
                sp.dma_start(bh[:], row(A["L1_gnn_b_hh"])).then_inc(loaded, 16)
                sp.wait_ge(loaded, 96)

            @block.tensor
            def _(pe):
                pe.wait_ge(loaded, 96)
                for s in range(NB + 2):
                    if s < NB:
                        if s >= 2:
                            pe.wait_ge(turned_out, 2 * (s - 1))
                        for k in range(K):
                            pe.transpose(S.ps[:, s % 2, k * P:(k + 1) * P], S.acc[:, s, k * 128:(k + 1) * 128],
                                         S.ident[0:P, 0:P])
                        pe.transpose(S.ps[0:1, s % 2, K * P:(K + 1) * P], S.acc[:, s, D:D + 1],
                                     S.ident[0:P, 0:P]).then_inc(turned, 1)
                    if 1 <= s <= NB:
                        t = s - 1
                        pe.wait_ge(turned_out, 2 * (t + 1))
                        if t >= 2:
                            pe.wait_ge(agg_out, t - 1)
                        for f in range(K):
                            o = S.ps[:, 2 + t % 2, f * P:(f + 1) * P]
                            for k in range(K):
                                pe.matmul(o, w2[:, k, f * 128:(f + 1) * 128], sums_t[:, t % 2, k, :],
                                          start=k == 0, stop=False)
                            ins = pe.matmul(o, b2[0:1, f * 128:(f + 1) * 128], degree[0:1, t % 2, :],
                                            start=False, stop=True)
                        ins.then_inc(aggregated, 1)
                    if s >= 2:
                        t = s - 2
                        pe.wait_ge(agg_out, t + 1)
                        if t >= 2:
                            pe.wait_ge(gates_out, 2 * (t - 1))
                        q = 4 + 2 * (t % 2)
                        hx = S.xT[:, :, t * P:(t + 1) * P]
                        for k in range(K):
                            pe.matmul(S.ps[0:P, q, :], agg[:, t % 2, k, :], wi[:, k, 0:2 * D], start=k == 0, stop=False)
                        for k in range(K):
                            pe.matmul(S.ps[0:P, q, :], hx[:, k], wh[:, k, 0:2 * D], start=False, stop=k == K - 1)
                        for k in range(K):
                            pe.matmul(S.ps[0:P, q + 1, 0:D], agg[:, t % 2, k, :], wi[:, k, 2 * D:], start=k == 0,
                                      stop=k == K - 1)
                        for k in range(K):
                            ins = pe.matmul(S.ps[0:P, q + 1, D:2 * D], hx[:, k], wh[:, k, 2 * D:], start=k == 0,
                                            stop=k == K - 1)
                        ins.then_inc(gates, 1)

            @block.scalar
            def _(act):
                for s in range(NB + 4):
                    if s < NB:
                        act.wait_ge(turned, s + 1)
                        if s >= 2:
                            act.wait_ge(aggregated, s - 1)
                        act.copy(sums_t[:, s % 2], S.ps[:, s % 2, 0:K * P].rearrange("p (k n) -> p k n", k=K))\
                           .then_inc(turned_out, 1)
                        act.copy(degree[:, s % 2, :], S.ps[0:1, s % 2, K * P:(K + 1) * P]).then_inc(turned_out, 1)
                    if 1 <= s <= NB:
                        t = s - 1
                        act.wait_ge(aggregated, t + 1)
                        if t >= 2:
                            act.wait_ge(gates, t - 1)
                        act.copy(agg[:, t % 2], S.ps[:, 2 + t % 2, 0:K * P].rearrange("p (k n) -> p k n", k=K))\
                           .then_inc(agg_out, 1)
                    if 3 <= s < NB + 3:
                        t = s - 3
                        act.wait_ge(gates_out, 2 * (t + 1))
                        act.activation(rz[:, t % 3, :], rz[:, t % 3, :], ACT.Sigmoid).then_inc(sig, 1)
                    if s >= 4:
                        t = s - 4
                        act.wait_ge(cand, t + 1)
                        act.activation(nn[:, t % 3, 0:D], nn[:, t % 3, 0:D], ACT.Tanh).then_inc(tanh, 1)

            @block.vector
            def _(dve):
                ch = Chain(dve, dve_step)
                dve.wait_ge(loaded, 96)
                ch.step(dve.tensor_tensor(b_rz[:], bi[:, 0:2 * D], bh[:, 0:2 * D], ALU.add))
                ch.step(dve.tensor_copy(b_n[:, 0:D], bi[:, 2 * D:]))
                ch.link(dve.tensor_copy(b_n[:, D:], bh[:, 2 * D:]))
                for s in range(NB + 2):
                    if s < NB:
                        q = 4 + 2 * (s % 2)
                        dve.wait_ge(gates, s + 1)
                        dve.tensor_tensor(rz[:, s % 3, :], S.ps[0:P, q, :], b_rz[:], ALU.add).then_inc(gates_out, 1)
                        dve.tensor_tensor(nn[:, s % 3, :], S.ps[0:P, q + 1, :], b_n[:], ALU.add).then_inc(gates_out, 1)
                    if 1 <= s <= NB:
                        t = s - 1
                        a, r = nn[:, t % 3, :], rz[:, t % 3, 0:D]
                        dve.wait_ge(sig, t + 1)
                        dve.wait_ge(gates_out, 2 * (t + 1))
                        ch.link(dve.tensor_tensor(a[:, D:], a[:, D:], r, ALU.mult))
                        ch.link(dve.tensor_tensor(a[:, 0:D], a[:, 0:D], a[:, D:], ALU.add))
                        dve.sem_inc(cand, 1)
                    if s >= 2:
                        t = s - 2
                        a, z = nn[:, t % 3, :], rz[:, t % 3, D:]
                        dve.wait_ge(tanh, t + 1)
                        ch.link(dve.tensor_tensor(a[:, D:], S.xn[:, t, :], a[:, 0:D], ALU.subtract))
                        ch.link(dve.tensor_tensor(a[:, D:], a[:, D:], z, ALU.mult))
                        ch.link(dve.tensor_tensor(S.x[:, t, :], S.x[:, t, :], a[:, 0:D], ALU.add))
                        ch.link(dve.tensor_tensor(S.x[:, t, :], S.x[:, t, :], a[:, D:], ALU.add))


def ffn1(nc, S, A):
    n = 32
    with phase(nc, "ffn1") as (sb, sem):
        comb, comb_t = sb("comb", [P, NB, n]), sb("comb_t", [n, N])
        expert_weights(nc, S, A, "route1", n, "top1", S.turned["L1_ffn_router_w"], A["L1_ffn_router_b"],
                       comb, comb_t, b2=A["L1_ffn_b2"], target=S.acc[:, :, 0:D])
        with phase(nc, "ffn1m") as (sb2, sem2):
            comb_b = sb2("comb_b", [n, N], BF16)
            sel = sb2("sel", [n, n // 2, 128], BF16)
            steps, zeroed, ready = sem2("steps"), sem2("zeroed"), sem2("ready")
            with nc.Block() as block:
                @block.gpsimd
                def _(pool):
                    pool.memset(sel[:], 1.0).then_inc(zeroed, 1)
                    pool.wait_ge(zeroed, 1)
                    v = sel[:].rearrange("e q (j f) -> e q j f", j=2)
                    pool.affine_select(out=v, in_=v, compare_op=ALU.is_equal, fill=0.0, base=0,
                                       pattern=[[-2, n // 2], [-1, 2], [0, 64]], channel_multiplier=1).then_inc(zeroed, 1)
                    pool.wait_ge(zeroed, 2)

                @block.vector
                def _(dve):
                    dve.tensor_copy(comb_b[:], comb_t[:]).then_inc(ready, 1)
                    dve.wait_ge(ready, 1)

            def first(e):
                pick = A["L1_ffn_W1"][bass.ds(e * 2, 2)] if not isinstance(e, int) else A["L1_ffn_W1"][2 * e:2 * e + 2]
                return pick.rearrange("j (k p) f -> p j k f", p=128)

            def last(e):
                v = A["L1_ffn_W2"].rearrange("(q j) h d -> q (j h) d", j=2)
                pick = v[bass.ds(e, 1)] if not isinstance(e, int) else v[e:e + 1]
                return pick.rearrange("a p d -> p a d")

            experts(nc, S, "experts1", n // 2, first, None, last, 128,
                    Layer(ACT.Relu, (S.pcol, S.column["L1_ffn_b1"])), None, comb, S.acc, masked=(sel, comb_b))
            with nc.Block() as block:
                @block.vector
                def _(dve):
                    ch = Chain(dve, steps)
                    ch.link(dve.scalar_tensor_tensor(S.x[:], S.acc[:, :, 0:D], 0.0, S.x[:], ALU.max, ALU.add))


def coefficients(c, dve, b, X, Y, V, w, ask):
    tt, ts, stt = dve.tensor_tensor, dve.tensor_scalar, dve.scalar_tensor_tensor
    den, rd, A, B, s2, s2m, r1, s, p, m, r2, cw, large = (b(k) for k in range(13))
    c.step(stt(A, V, -2.0, Y, ALU.mult, ALU.add))
    c.step(ts(B, X, -1.0, 1.0, ALU.mult, ALU.add))
    c.link(tt(den, X, Y, ALU.mult))
    c.step(tt(s2, A, X, ALU.add))
    c.link(stt(den, V, -2.0, den, ALU.mult, ALU.add))
    c.step(ts(rd, den, 1.0, MIN_NORM, ALU.add, ALU.max))
    c.step(ts(s2, s2, 0.0, None, ALU.max))
    c.link(ts(den, den, 1.0, 0.0, ALU.add, ALU.max))
    c.step(ts(cw, B, MIN_NORM, None, ALU.max))
    c.link(dve.reciprocal(rd, rd))
    c.step(ts(A, A, 1.0, None, ALU.add))
    c.link(tt(den, den, rd, ALU.mult))
    c.step(tt(cw, cw, w, ALU.mult))
    c.link(tt(s2, s2, den, ALU.mult))
    c.link(tt(s2, s2, rd, ALU.mult))
    c.link(ts(s, s2, 1e-18, None, ALU.max))

    def series():
        c.link(ts(s2m, s2, 0.05, None, ALU.min))
        c.link(ts(r1, s2m, 1.0 / 11, None, ALU.mult))
        c.link(stt(r1, r1, 1.0 / 9, s2m, ALU.add, ALU.mult))

    def more_series():
        c.step(tt(cw, cw, rd, ALU.mult))
        c.link(stt(r1, r1, 1.0 / 7, s2m, ALU.add, ALU.mult))
        c.step(ts(large, s2, 0.04, None, ALU.is_gt))
        c.link(stt(r1, r1, 1.0 / 5, s2m, ALU.add, ALU.mult))

    def last_of_series():
        c.step(dve.reciprocal(m, s))
        c.link(stt(r1, r1, 1.0 / 3, s2m, ALU.add, ALU.mult))
        c.link(ts(r1, r1, 1.0, None, ALU.add))

    ask(ACT.Ln, p, s, 1.0, series)
    ask(ACT.Exp, p, p, 0.5, more_series)
    c.link(dve.reciprocal(m, p))
    c.link(stt(m, s, 0.5, m, ALU.mult, ALU.mult))
    c.link(stt(s, p, 0.5, m, ALU.mult, ALU.add))
    c.link(ts(p, s, 1.0 - 2.0 ** -23, None, ALU.min))
    c.link(ts(m, p, -1.0, 1.0, ALU.mult, ALU.add))
    c.link(dve.reciprocal(m, m))
    c.link(stt(p, p, 1.0, m, ALU.add, ALU.mult))
    ask(ACT.Ln, p, p, 1.0, last_of_series)
    c.link(stt(r2, p, 0.5, m, ALU.mult, ALU.mult))
    c.link(tt(r2, r2, r1, ALU.subtract))
    c.link(tt(r2, r2, large, ALU.mult))
    c.link(tt(r1, r1, r2, ALU.add))
    c.link(tt(cw, cw, r1, ALU.mult))
    c.step(stt(A, A, -1.0, cw, ALU.mult, ALU.mult))
    c.link(tt(B, B, cw, ALU.mult))
    return A, B


def artanh_ratio(c, dve, s2, s, s2m, r1, p, m, r2, ask):
    tt, ts, stt = dve.tensor_tensor, dve.tensor_scalar, dve.scalar_tensor_tensor
    c.link(ts(s2m, s2, 0.05, None, ALU.min))
    c.link(ts(r1, s2m, 1.0 / 11, None, ALU.mult))
    for k in (9, 7, 5, 3):
        c.link(stt(r1, r1, 1.0 / k, s2m, ALU.add, ALU.mult))
    c.link(ts(r1, r1, 1.0, None, ALU.add))
    c.link(ts(p, s, 1.0 - 2.0 ** -23, None, ALU.min))
    c.link(ts(m, p, -1.0, 1.0, ALU.mult, ALU.add))
    c.link(dve.reciprocal(m, m))
    c.link(stt(p, p, 1.0, m, ALU.add, ALU.mult))
    ask(ACT.Ln, p, p, 1.0)
    c.link(dve.reciprocal(m, s))
    c.link(stt(r2, p, 0.5, m, ALU.mult, ALU.mult))
    c.link(tt(r2, r2, r1, ALU.subtract))
    c.link(ts(m, s2, 0.04, None, ALU.is_gt))
    c.link(tt(r2, r2, m, ALU.mult))
    c.link(tt(r1, r1, r2, ALU.add))


def hyperbolic(nc, S, A):
    ends, local, blk = S.end["dst"], S.local["dst"], S.blk["dst"]
    FILL_EVERY = 2
    COEF = 41
    with phase(nc, "hyp") as (sb, sem):
        dve_step, act_ask, act_done = sem("dve_step"), sem("act_ask"), sem("act_done")
        ch = Chain(None, dve_step)
        with ExitStack() as ctx:
            nodes = ctx.enter_context(nc.sbuf_tensor("hyp_nodes", [P, NB, D + 8], F32))
            junk = ctx.enter_context(nc.sbuf_tensor("hyp_junk", [128, 2, D], F32))
            stored, filled = sem("stored"), sem("filled")
            with nc.Block() as block:
                @block.sync
                def _(sp):
                    sp.wait_ge(filled, 1)
                    sp.dma_start(S.rows.rearrange("(t p) c -> p t c", p=P), nodes[:]).then_inc(stored, 16)
                    sp.wait_ge(stored, 16)

                @block.vector
                def _(dve):
                    ch.eng = dve
                    ch.step(dve.memset(S.acc[:], 0.0))
                    ch.step(dve.tensor_copy(nodes[:, :, 0:D], S.xn[:]))
                    ch.link(dve.memset(nodes[:, :, D:], 0.0))
                    for t in range(NB):
                        ch.link(dve.tensor_tensor_reduce(junk[0:P, t % 2, :], S.xn[:, t, :], S.xn[:, t, :], 1.0, 0.0,
                                                         ALU.mult, ALU.add, nodes[:, t, D:D + 1]))
                    ch.sync()
                    dve.sem_inc(filled, 1)

            gathered = [sem(f"gathered{u}") for u in range(U)]
            (copied, go, located, selected, turned, turned_out, looked_up, dotted, ready, scaled, summed, added,
             coef_step) = (
                sem(x) for x in ("copied", "go", "located", "selected", "turned", "turned_out", "looked_up", "dotted",
                                 "coefs_ready", "scaled", "summed", "added", "coef_step"))
            jobs = []
            with nc.Block() as block, ExitStack() as ctx2:
                def mb(what, shape, dt=F32):
                    return ctx2.enter_context(nc.sbuf_tensor(f"hyp_{what}", shape, dt))

                idx, rows = mb("idx", [128, U, G], I32), mb("rows", [128, U, G, XG])
                loc = mb("loc", [128, U, G])
                onehot_b, onehot = mb("onehot_b", [128, 2, G, P], BF16), mb("onehot", [128, U, G, P])
                onehot_t = mb("onehot_t", [P, 2, G, 128])
                X, V = mb("X", [128, 2, G]), mb("V", [128, 2, G])
                Y, wts = mb("Y", [128, 2, G]), mb("wts", [128, 2, G])
                cols = mb("cols", [128, 2, 13, G])
                LB = 3

                @block.gpsimd
                def _(pool):
                    gather_groups(pool, ends, S.rows, idx, rows, summed, gathered, copied, go)

                @block.vector
                def _(dve):
                    def columns(q):
                        h = q.slot % 2
                        dve.wait_ge(gathered[q.slot], rows_in(q))
                        dve.tensor_copy(wts[:, h], S.edge_w[:, q.tiles()]).then_inc(dotted, 1)
                        dve.tensor_copy(Y[:, h], rows[:, q.slot, :, D]).then_inc(dotted, 1)

                    def dot(q, t):
                        h = q.slot % 2
                        dve.wait_ge(looked_up, q.n * G + t + 1)
                        src = S.ps[:, 5 + t % LB, 0:D + 1]
                        dve.tensor_copy(X[:, h, t:t + 1], src[:, D:D + 1]).then_inc(dotted, 1)
                        if t >= 2:
                            dve.wait_ge(dotted, 2 * (q.n * (G + 1) + t))
                        elif q.since(1):
                            dve.wait_ge(dotted, 2 * (q.n * (G + 1) + t - 1))
                        dve.tensor_tensor_reduce(junk[:, t % 2, :], src[:, 0:D], rows[:, q.slot, t, 0:D],
                                                 1.0, 0.0, ALU.mult, ALU.add, V[:, h, t:t + 1]).then_inc(dotted, 1)

                    def coefs(q):
                        h = q.slot % 2
                        add = [lambda t=t: accumulate(dve, S, q.previous(), blk, D + 1, 4, summed, added, [t])
                               for t in range(G)] if q.since(1) else []
                        more = not isinstance(q.n, int) or q.n + 1 < GROUPS
                        dots = [lambda t=t: dot(q.next(), t) for t in range(G)] if more else []
                        gaps = iter(add[:4] + dots[:LB] + add[4:] + dots[LB:])

                        def fill():
                            work = next(gaps, None)
                            if work:
                                work()

                        def fill_some():
                            if c.n % FILL_EVERY == 0:
                                fill()

                        c = Chain(dve, coef_step, q.n * COEF)
                        c.meanwhile = fill_some
                        asked = [0]

                        def ask(func, out, in_, scale, gap):
                            if isinstance(q.n, int) and q.n < 2:
                                jobs.append((func, out, in_, scale))
                            asked[0] += 1
                            dve.sem_inc(act_ask, 1)
                            gap()
                            dve.wait_ge(act_done, q.n * 3 + asked[0])

                        dve.wait_ge(dotted, 2 * (q.n + 1) * (G + 1))
                        if more:
                            columns(q.next())
                        al, be = coefficients(c, dve, lambda k: cols[:, h, k, :], X[:, h], Y[:, h], V[:, h], wts[:, h],
                                              ask)
                        c.link(dve.tensor_copy(rows[:, q.slot, :, D], al))
                        dve.sem_inc(ready, 1)
                        for work in gaps:
                            work()
                        assert c.n == COEF, c.n

                    def first_dots(q):
                        if isinstance(q.n, int) and q.n == 0:
                            columns(q)
                            for t in range(G):
                                dot(q, t)

                    pipeline(dve, (0, lambda q: one_hots(dve, S, q, onehot_b, loc, local, located, selected)),
                             (0, first_dots), (1, coefs))
                    accumulate(dve, S, Group(GROUPS - 1, (GROUPS - 1) % U, GROUPS // U, GROUPS - 1), blk, D + 1, 4,
                               summed, added)

                @block.scalar
                def _(act):
                    def answer(q):
                        h = q.slot % 2
                        for n, (func, out, in_, scale) in enumerate(jobs[3 * h:3 * h + 3]):
                            act.wait_ge(act_ask, q.n * 3 + n + 1)
                            act.activation(out, in_, func, scale=scale).then_inc(act_done, 1)
                        act.wait_ge(ready, q.n + 1)
                        for t in range(G):
                            v = rows[:, q.slot, t, 0:D]
                            act.activation(v, v, ACT.Copy, scale=cols[:, h, 3, t:t + 1]).then_inc(scaled, 1)

                    pipeline(act, (0, lambda q: widen(act, S, q, 4, onehot_b, onehot, onehot_t, turned, turned_out, 1)),
                             (1, answer))

                @block.tensor
                def _(pe):
                    def look_up(tiles):
                        def stage(q):
                            if tiles[0] == 0:
                                pe.wait_ge(turned_out, 2 * q.n + 2)
                            for t in tiles:
                                b = block_of(pe, blk, q, t)
                                if t >= LB:
                                    pe.wait_ge(dotted, 2 * (q.n * (G + 1) + t - LB + 2))
                                elif q.since(1):
                                    before = t + LB if t + 2 * LB >= G else t + 2 * LB
                                    pe.wait_ge(dotted, 2 * (q.n * (G + 1) - (G + 1) + before + 2))
                                pe.matmul(S.ps[:, 5 + t % LB, 0:D + 1], onehot_t[:, q.slot % 2, t, :],
                                          nodes[:, bass.ds(b, 1), 0:D + 1].rearrange("p a c -> p (a c)"),
                                          start=True, stop=True).then_inc(looked_up, 1)
                        return stage

                    def total(tiles):
                        def stage(q):
                            for t in tiles:
                                pe.wait_ge(scaled, q.n * G + t + 1)
                                if q.tile_since(t, 4):
                                    pe.wait_ge(added, q.n * G + t - 3)
                                pe.matmul(S.ps[0:P, t % 4, 0:D + 1], onehot[:, q.slot, t, :],
                                          rows[:, q.slot, t, 0:D + 1], start=True, stop=True).then_inc(summed, 1)
                        return stage

                    pipeline(pe, (0, lambda q: turn(pe, S, q, 4, onehot_b, selected, turned, turned_out, 1)),
                             (2, total(range(4))), (0, look_up(range(LB))),
                             (2, total(range(4, G))), (0, look_up(range(LB, G))))

    with phase(nc, "hypn") as (sb, sem):
        dve_step, act_ask, act_done = sem("dve_step"), sem("act_ask"), sem("act_done")
        w, bias = sb("w", [128, K, D]), sb("bias", [P, D])
        v, cols = sb("v", [P, NB, D]), sb("cols", [P, 18, NB])
        uT = sb("uT", [128, 2, K, P])
        junk = sb("junk", [P, D])
        tiny = sb("tiny", [P, 12])
        loaded, u_ready, turned, turned_out, product, emptied = (
            sem(x) for x in ("loaded", "u_ready", "turned", "turned_out", "product", "emptied"))
        jobs = []
        with nc.Block() as block:
            @block.sync
            def _(sp):
                sp.dma_start(w[:], S.turned["L2_gnn_weight"].rearrange("(k p) f -> p k f", p=128)).then_inc(loaded, 16)
                sp.dma_start(bias[:], row(A["L2_gnn_bias"])).then_inc(loaded, 16)
                sp.wait_ge(loaded, 32)

            @block.vector
            def _(dve):
                ch = Chain(dve, dve_step)
                tt, ts, stt = dve.tensor_tensor, dve.tensor_scalar, dve.scalar_tensor_tensor
                acc = S.acc[:, :, 0:D]
                x2, V, Y, X, n2, n1, c1, c2, rd, p, m, un, pn, at, g, s2m, r1, r2 = (cols[:, k, :] for k in range(18))

                def ask(func, out, in_, scale):
                    jobs.append((func, out, in_, scale))
                    dve.sem_inc(act_ask, 1)
                    dve.wait_ge(act_done, len(jobs))

                def dots(out, a, b):
                    for t in range(NB):
                        ch.link(dve.tensor_tensor_reduce(junk[:], a[:, t, :], b[:, t, :], 1.0, 0.0, ALU.mult, ALU.add,
                                                         out[:, t:t + 1]))

                def norm(out, sq, p, m):
                    ch.link(ts(sq, sq, MIN_NORM ** 2, None, ALU.max))
                    ask(ACT.Sqrt, p, sq, 1.0)
                    ch.link(dve.reciprocal(m, p))
                    ch.link(tt(m, m, sq, ALU.mult))
                    ch.link(tt(p, p, m, ALU.add))
                    ch.link(ts(out, p, 0.5, None, ALU.mult))

                def mobius(Xc, Yc, Vc):
                    ch.link(tt(rd, Xc, Yc, ALU.mult))
                    ch.link(stt(rd, Vc, 2.0, rd, ALU.mult, ALU.add))
                    ch.link(ts(rd, rd, 1.0, MIN_NORM, ALU.add, ALU.max))
                    ch.link(dve.reciprocal(rd, rd))
                    ch.link(stt(c1, Vc, 2.0, Yc, ALU.mult, ALU.add))
                    ch.link(stt(c1, c1, 1.0, rd, ALU.add, ALU.mult))
                    ch.link(ts(c2, Xc, -1.0, 1.0, ALU.mult, ALU.add))
                    ch.link(tt(c2, c2, rd, ALU.mult))

                def combine(out, a, b):
                    for t in range(NB):
                        ch.step(ts(out[:, t, :], a[:, t, :], c1[:, t:t + 1], None, ALU.mult))
                    ch.sync()
                    for t in range(NB):
                        bt = b[:, t, :] if b is not bias else bias[:]
                        ch.step(stt(out[:, t, :], bt, c2[:, t:t + 1], out[:, t, :], ALU.mult, ALU.add))
                    ch.sync()

                def scale(y, by):
                    for t in range(NB):
                        ch.step(ts(y[:, t, :], y[:, t, :], by[:, t:t + 1], None, ALU.mult))
                    ch.sync()

                for t in range(NB):
                    ch.step(stt(acc[:, t, :], S.xn[:, t, :], S.acc[:, t, D:D + 1], acc[:, t, :], ALU.mult, ALU.add))
                ch.sync()
                dots(n2, acc, acc)
                dots(x2, S.xn, S.xn)
                norm(un, n2, p, m)
                ch.link(ts(g, x2, -1.0, 1.0, ALU.mult, ALU.add))
                ch.link(ts(g, g, MIN_NORM, None, ALU.max))
                ch.link(dve.reciprocal(g, g))
                ch.link(ts(g, g, 2.0, MIN_NORM, ALU.mult, ALU.max))
                ch.link(tt(g, g, un, ALU.mult))
                ask(ACT.Tanh, g, g, 0.5)
                ch.link(dve.reciprocal(m, un))
                ch.link(tt(g, g, m, ALU.mult))
                scale(acc, g)
                dots(V, S.xn, acc)
                dots(Y, acc, acc)
                mobius(x2, Y, V)
                combine(v, S.xn, acc)
                dve.sem_inc(u_ready, 1)
                dots(n2, v, v)
                norm(un, n2, p, m)
                artanh_ratio(ch, dve, n2, un, s2m, r1, p, m, r2, ask)
                for t in range(NB):
                    dve.wait_ge(product, t + 1)
                    dve.tensor_copy(acc[:, t, :], S.ps[0:P, 4 + t % 4, 0:D]).then_inc(emptied, 1)
                dve.wait_ge(emptied, NB)
                dots(n2, acc, acc)
                norm(pn, n2, p, m)
                ch.link(tt(g, pn, r1, ALU.mult))
                ask(ACT.Tanh, g, g, 1.0)
                ch.link(dve.reciprocal(m, pn))
                ch.link(tt(g, g, m, ALU.mult))
                scale(acc, g)
                tc = lambda k: tiny[:, k:k + 1]
                dve.wait_ge(loaded, 32)
                ch.link(dve.tensor_tensor_reduce(junk[:], bias[:], bias[:], 1.0, 0.0, ALU.mult, ALU.add, tc(0)))
                norm(tc(1), tc(0), tc(2), tc(3))
                ask(ACT.Tanh, tc(4), tc(1), 1.0)
                ch.link(dve.reciprocal(tc(5), tc(1)))
                ch.link(tt(tc(4), tc(4), tc(5), ALU.mult))
                ch.link(ts(bias[:], bias[:], tc(4), None, ALU.mult))
                ch.link(dve.tensor_tensor_reduce(junk[:], bias[:], bias[:], 1.0, 0.0, ALU.mult, ALU.add, tc(6)))
                dots(X, acc, acc)
                for t in range(NB):
                    ch.link(dve.tensor_tensor_reduce(junk[:], acc[:, t, :], bias[:], 1.0, 0.0, ALU.mult, ALU.add,
                                                     V[:, t:t + 1]))
                mobius(X, tc(6).to_broadcast([P, NB]), V)
                combine(v, acc, bias)
                dots(n2, v, v)
                norm(un, n2, p, m)
                artanh_ratio(ch, dve, n2, un, s2m, r1, p, m, r2, ask)
                for t in range(NB):
                    ch.step(ts(v[:, t, :], v[:, t, :], 0.0, r1[:, t:t + 1], ALU.max, ALU.mult))
                ch.sync()
                dots(n2, v, v)
                norm(un, n2, p, m)
                ask(ACT.Tanh, g, un, 1.0)
                ch.link(dve.reciprocal(m, un))
                ch.link(ts(g, g, 1.0 - 1e-5, None, ALU.min))
                ch.link(tt(g, g, m, ALU.mult))
                for t in range(NB):
                    ch.step(stt(S.x[:, t, :], v[:, t, :], g[:, t:t + 1], S.x[:, t, :], ALU.mult, ALU.add))
                ch.sync()

            @block.scalar
            def _(act):
                for n, (func, out, in_, scale) in enumerate(jobs[:4]):
                    act.wait_ge(act_ask, n + 1)
                    act.activation(out, in_, func, scale=scale).then_inc(act_done, 1)
                for t in range(NB):
                    act.wait_ge(turned, t + 1)
                    if t >= 2:
                        act.wait_ge(product, t - 1)
                    act.copy(uT[:, t % 2], S.ps[:, t % 2, 0:K * P].rearrange("p (k n) -> p k n", k=K))\
                       .then_inc(turned_out, 1)
                for n, (func, out, in_, scale) in enumerate(jobs[4:]):
                    act.wait_ge(act_ask, 4 + n + 1)
                    act.activation(out, in_, func, scale=scale).then_inc(act_done, 1)

            @block.tensor
            def _(pe):
                pe.wait_ge(loaded, 32)
                pe.wait_ge(u_ready, 1)
                for s in range(NB + 1):
                    if s < NB:
                        if s >= 2:
                            pe.wait_ge(turned_out, s - 1)
                        for k in range(K):
                            ins = pe.transpose(S.ps[:, s % 2, k * P:(k + 1) * P], v[:, s, k * 128:(k + 1) * 128],
                                               S.ident[0:P, 0:P])
                        ins.then_inc(turned, 1)
                    if s >= 1:
                        t = s - 1
                        pe.wait_ge(turned_out, t + 1)
                        if t >= 4:
                            pe.wait_ge(emptied, t - 3)
                        for k in range(K):
                            ins = pe.matmul(S.ps[0:P, 4 + t % 4, 0:D], uT[:, t % 2, k, :], w[:, k, :],
                                            start=k == 0, stop=k == K - 1)
                        ins.then_inc(product, 1)


def ffn2(nc, S, A):
    n = 8
    with phase(nc, "ffn2") as (sb, sem):
        comb, comb_t = sb("comb", [P, NB, n]), sb("comb_t", [n, N])
        aff = sb("aff", [128, 2, 2, 2 * n])
        expert_weights(nc, S, A, "route2", n, "soft", A["L2_ffn_Wr"], A["L2_ffn_br"], comb, comb_t,
                       b2=A["L2_ffn_bo"], target=S.x[:], base="keep")
        with phase(nc, "ffn2a") as (sb2, sem2):
            tmp = sb2("tmp", [128, 2, 3, 2 * n])
            dve_step, ask, done = sem2("dve_step"), sem2("ask"), sem2("done")
            with nc.Block() as block:
                @block.scalar
                def _(act):
                    for l in range(2):
                        act.wait_ge(ask, l + 1)
                        act.activation(tmp[:, l, 1, :], tmp[:, l, 0, :], ACT.Sqrt).then_inc(done, 1)

                @block.vector
                def _(dve):
                    ch = Chain(dve, dve_step)
                    for l in range(2):
                        b, g, be, m, var = (S.pcol[:, S.column[f"L2_ffn_{x}{l + 1}"]:S.column[f"L2_ffn_{x}{l + 1}"] + 2 * n]
                                            for x in ("b", "g", "be", "m", "v"))
                        bias, scale = aff[:, l, 0, :], aff[:, l, 1, :]
                        a, r, t = tmp[:, l, 0, :], tmp[:, l, 1, :], tmp[:, l, 2, :]
                        ch.link(dve.tensor_scalar(a, var, 1e-3, None, ALU.add))
                        dve.sem_inc(ask, 1)
                        dve.wait_ge(done, l + 1)
                        newton(ch, dve, a, r, t)
                        ch.link(dve.reciprocal(t, r))
                        ch.link(dve.tensor_tensor(scale, g, t, ALU.mult))
                        ch.link(dve.tensor_tensor(bias, b, m, ALU.subtract))
                        ch.link(dve.tensor_tensor(bias, bias, scale, ALU.mult))
                        ch.link(dve.tensor_tensor(bias, bias, be, ALU.add))
        t = aff[:].rearrange("p l a e -> p (l a e)")
        layer = [Layer(ACT.Relu, (t, l * 4 * n), (t, l * 4 * n + 2 * n)) for l in range(2)]
        experts(nc, S, "experts2", n, by_expert(A["L2_ffn_W1"]), by_expert(A["L2_ffn_W2"]),
                by_expert(A["L2_ffn_Wo"]), 256, layer[0], layer[1], comb, S.x)


def newton(ch, dve, value, root, tmp):
    ch.link(dve.reciprocal(tmp, root))
    ch.link(dve.tensor_tensor(tmp, tmp, value, ALU.mult))
    ch.link(dve.tensor_tensor(root, root, tmp, ALU.add))
    ch.link(dve.tensor_scalar(root, root, 0.5, None, ALU.mult))


def column_norm(ch, dve, src, stats, mv, sem_ask, sem_done, count, eps, gamma, beta, tmp, affine):
    for k in range(K):
        for c in range(NCHUNK):
            at = CH * c * P
            width = len(chunk_blocks(c)) * P
            ch.step(dve.bn_stats(stats[:, k, c, :], src[:, k, at:at + width]))
    ch.sync()
    for k in range(K):
        ch.step(dve.bn_aggr(mv[:, k, :], stats[:, k, :, :]))
    ch.sync()
    var, root, inv = tmp[:, 0, :], tmp[:, 1, :], tmp[:, 2, :]
    ch.link(dve.tensor_scalar(var, mv[:, :, 1], eps, None, ALU.add))
    dve.sem_inc(sem_ask, 1)
    dve.wait_ge(sem_done, count)
    newton(ch, dve, var, root, inv)
    ch.link(dve.reciprocal(inv, root))
    ch.link(dve.tensor_tensor(affine[:, 0, :], gamma, inv, ALU.mult))
    ch.link(dve.tensor_tensor(inv, mv[:, :, 0], affine[:, 0, :], ALU.mult))
    ch.link(dve.tensor_tensor(affine[:, 1, :], beta, inv, ALU.subtract))


def hyperconv(nc, S, A, n, hT):
    ends, local, blk = S.end["dst"], S.local["dst"], S.blk["dst"]
    col = lambda v: S.pcol[:, S.column[f"L3_gnn_{v}"]:S.column[f"L3_gnn_{v}"] + K]
    source = S.xT if n == 1 else hT
    with phase(nc, f"conv{n}") as (sb, sem):
        w1, w2, b1 = sb("w1", [128, K, D]), sb("w2", [128, K, D]), sb("b1", [P, D])
        loaded, dve_step, product, out, stored = (
            sem(x) for x in ("loaded", "dve_step", "product", "out", "stored"))
        ch = Chain(None, dve_step)
        with nc.Block() as block:
            @block.sync
            def _(sp):
                for dst, v in ((w1, "w1"), (w2, "w2")):
                    sp.dma_start(dst[:], A[f"L3_gnn_c{n}_{v}"].rearrange("(k p) f -> p k f", p=128)).then_inc(loaded, 16)
                sp.dma_start(b1[:], row(A[f"L3_gnn_c{n}_b1"])).then_inc(loaded, 16)
                sp.wait_ge(loaded, 48)
                sp.wait_ge(out, NB)
                sp.dma_start(S.rows_b.rearrange("(t p) c -> p t c", p=P), S.acc[:, :, 0:D]).then_inc(stored, 16)
                sp.wait_ge(stored, 16)

            @block.tensor
            def _(pe):
                pe.wait_ge(loaded, 48)
                for t in range(NB):
                    if t >= 8:
                        pe.wait_ge(out, t - 7)
                    for k in range(K):
                        ins = pe.matmul(S.ps[0:P, t % 8, 0:D], source[:, k, t * P:(t + 1) * P], w1[:, k, :],
                                        start=k == 0, stop=k == K - 1)
                    ins.then_inc(product, 1)

            @block.vector
            def _(dve):
                ch.eng = dve
                dve.wait_ge(loaded, 48)
                for t in range(NB):
                    dve.wait_ge(product, t + 1)
                    ch.link(dve.tensor_tensor(S.acc[:, t, 0:D], S.ps[0:P, t % 8, 0:D], b1[:], ALU.add))
                    dve.tensor_scalar(S.acc[:, t, 0:D], S.acc[:, t, 0:D], 0.0, None, ALU.max).then_inc(out, 1)

        gathered = [sem(f"gathered{u}") for u in range(U)]
        copied, go, located, selected, summed, added, cleared = (
            sem(x) for x in ("copied", "go", "located", "selected", "summed", "added", "cleared"))
        with nc.Block() as block, ExitStack() as ctx:
            def mb(what, shape, dt=F32):
                return ctx.enter_context(nc.sbuf_tensor(f"conv{n}_{what}", shape, dt))

            idx, rows = mb("idx", [128, U, G], I32), mb("rows", [128, U, G, D])
            loc, wts, weight_of = mb("loc", [128, U, G]), mb("wts", [128, U, G]), mb("weight_of", [128, U, G, P])

            @block.gpsimd
            def _(pool):
                gather_groups(pool, ends, S.rows_b, idx, rows, summed, gathered, copied, go)

            @block.vector
            def _(dve):
                def select(q):
                    dve.tensor_copy(loc[:, q.slot, :], local[:, q.tiles()]).then_inc(located, 1)
                    dve.tensor_copy(wts[:, q.slot, :], S.edge_w[:, q.tiles()]).then_inc(located, 1)
                    dve.wait_ge(located, 2 * q.n + 2)
                    for t in range(G):
                        dve.tensor_scalar(weight_of[:, q.slot, t, :], S.iota[:, 0:P], loc[:, q.slot, t:t + 1],
                                          wts[:, q.slot, t:t + 1], ALU.is_equal, ALU.mult).then_inc(selected, 1)

                dve.memset(S.acc[:], 0.0).then_inc(cleared, 1)
                dve.wait_ge(cleared, 1)
                pipeline(dve, (0, select), (1, lambda q: accumulate(dve, S, q, blk, D, 8, summed, added)))

            @block.tensor
            def _(pe):
                def total(q):
                    pe.wait_ge(selected, (q.n + 1) * G)
                    pe.wait_ge(gathered[q.slot], rows_in(q))
                    for t in range(G):
                        if q.since(1):
                            pe.wait_ge(added, q.n * G + t - 7)
                        pe.matmul(S.ps[0:P, t, 0:D], weight_of[:, q.slot, t, :], rows[:, q.slot, t, :],
                                  start=True, stop=True).then_inc(summed, 1)
                pipeline(pe, (0, total))

        turned, turned_out, product2, out2, ask, root, shown, applied, last = (
            sem(x) for x in ("turned", "turned_out", "product2", "out2", "ask", "root", "shown", "applied", "last"))
        with nc.Block() as block, ExitStack() as ctx:
            def mb(what, shape, dt=F32):
                return ctx.enter_context(nc.sbuf_tensor(f"conv{n}_{what}", shape, dt))

            aggT = mb("aggT", [128, 2, K, CH * P])
            stats, mv, tmp, affine = (mb("stats", [128, K, NCHUNK, 6]), mb("mv", [128, K, 2]), mb("tmp", [128, 3, K]),
                                      mb("affine", [128, 2, 2, K]))

            @block.tensor
            def _(pe):
                for s in range(NCHUNK + 1):
                    if s < NCHUNK:
                        for m, t in enumerate(chunk_blocks(s)):
                            if t >= 4:
                                pe.wait_ge(turned_out, t - 3)
                            for k in range(K):
                                ins = pe.transpose(S.ps[:, t % 4, k * P:(k + 1) * P], S.acc[:, t, k * 128:(k + 1) * 128],
                                                   S.ident[0:P, 0:P])
                            ins.then_inc(turned, 1)
                    if s >= 1:
                        c = s - 1
                        width = len(chunk_blocks(c)) * P
                        pe.wait_ge(turned_out, chunk_blocks(c)[-1] + 1)
                        for f in range(K):
                            m = c * K + f
                            if m >= 4:
                                pe.wait_ge(out2, m - 3)
                            for k in range(K):
                                ins = pe.matmul(S.ps[:, 4 + m % 4, 0:width], w2[:, k, f * 128:(f + 1) * 128],
                                                aggT[:, c % 2, k, 0:width], start=k == 0, stop=k == K - 1)
                            ins.then_inc(product2, 1)
                if n == 2:
                    pe.wait_ge(applied, 4)
                    for t in range(NB):
                        if t >= 4:
                            pe.wait_ge(last, t - 3)
                        for k in range(K):
                            ins = pe.transpose(S.ps[0:P, t % 4, k * 128:(k + 1) * 128], hT[:, k, t * P:(t + 1) * P],
                                               S.ident[:])
                        ins.then_inc(shown, 1)

            @block.scalar
            def _(act):
                for t in range(NB):
                    c, m = t // CH, t % CH
                    act.wait_ge(turned, t + 1)
                    if c >= 2:
                        act.wait_ge(product2, (c - 1) * K)
                    act.copy(aggT[:, c % 2, :, m * P:(m + 1) * P],
                             S.ps[:, t % 4, 0:K * P].rearrange("p (k n) -> p k n", k=K)).then_inc(turned_out, 1)
                for a in range(2):
                    act.wait_ge(ask, 2 * a + 1)
                    act.activation(tmp[:, 1, :], tmp[:, 0, :], ACT.Sqrt).then_inc(root, 1)
                    act.wait_ge(ask, 2 * a + 2)
                    function = ACT.Identity if (n == 2 and a == 1) else ACT.Relu
                    for k in range(K):
                        act.activation(hT[:, k, :], hT[:, k, :], function, bias=affine[:, a, 1, k:k + 1],
                                       scale=affine[:, a, 0, k:k + 1]).then_inc(applied, 1)

            @block.vector
            def _(dve):
                ch.eng = dve
                for m in range(NCHUNK * K):
                    c, f = m // K, m % K
                    width = len(chunk_blocks(c)) * P
                    at = c * CH * P
                    dve.wait_ge(product2, m + 1)
                    dve.tensor_scalar(hT[:, f, at:at + width], S.ps[:, 4 + m % 4, 0:width],
                                      col(f"c{n}_b2")[:, f:f + 1], None, ALU.add).then_inc(out2, 1)
                dve.wait_ge(out2, NCHUNK * K)
                for a, v in enumerate((f"c{n}_", f"bn{n}_")):
                    if a:
                        dve.wait_ge(applied, 2)
                    column_norm(ch, dve, hT, stats, mv, ask, root, a + 1, EPS, col(v + "g"), col(v + "b"),
                                tmp, affine[:, a])
                    dve.sem_inc(ask, 1)
                if n == 2:
                    dve.wait_ge(applied, 4 - 0)
                    for t in range(NB):
                        dve.wait_ge(shown, t + 1)
                        ch.link(dve.tensor_tensor(S.acc[:, t, 0:D], S.xn[:, t, :], S.ps[0:P, t % 4, 0:D], ALU.add))
                        dve.sem_inc(last, 1)
                        ch.link(dve.scalar_tensor_tensor(S.x[:, t, :], S.acc[:, t, 0:D], 0.0, S.x[:, t, :],
                                                         ALU.max, ALU.add))


def hypergraph(nc, S, A):
    with phase(nc, "hgraph") as (sb, sem):
        hT = sb("hT", [128, K, N])
        hyperconv(nc, S, A, 1, hT)
        hyperconv(nc, S, A, 2, hT)


NE3 = 16
PICK_TILES = (2 * N + NE3 * 127) // 128 + 1
PICK_TILES += -PICK_TILES % U


def sort_picks(nc, S, key, expert_of, node_of, pick_of):
    PC, T = 2 * NB, PICK_TILES
    HALF = NE3 // 2
    with phase(nc, "picks") as (sb, sem):
        onehot = sb("onehot", [P, NE3, PC], BF16)
        before, ones_b = sb("before", [P, P], BF16), sb("ones_b", [P, P], BF16)
        count, ones_p, one_c = sb("count", [P, NE3]), sb("ones_p", [P, 128]), sb("one_c", [P, PC])
        tiles_i, tiles = sb("tiles_i", [128, NE3], I32), sb("tiles", [128, NE3])
        upto, start, slot0 = sb("upto", [128, NE3]), sb("start", [128, NE3]), sb("slot0", [128, NE3])
        iota_t, blk = sb("iota_t", [128, T]), sb("blk", [128, T])
        cum, pos = sb("cum", [P, NE3, PC]), sb("pos", [P, PC])
        hi_i, hi, addr = sb("hi_i", [P, PC], I32), sb("hi", [P, PC]), sb("addr", [P, PC], I32)
        ids, pad = sb("ids", [P, NB, 2], I32), sb("pad", [128, T], I32)
        half_i, half = sb("half_i", [128, T], I32), sb("half", [128, T])
        consts, padded, dve_step, counted, ranks, addressed, written, back = (
            sem(x) for x in ("consts", "padded", "dve_step", "counted", "ranks", "addressed", "written", "back"))
        table = S.picks.rearrange("(p t) w -> p (t w)", p=128)
        with nc.Block() as block:
            @block.sync
            def _(sp):
                sp.dma_start(S.rows_b.rearrange("(t p) c -> p t c", p=P), S.xn[:]).then_inc(padded, 16)
                sp.wait_ge(consts, 6)
                sp.dma_start(table, pad[:]).then_inc(padded, 16)
                sp.wait_ge(padded, 32)
                sp.wait_ge(written, 16 * PC)
                sp.dma_start(pick_of[:], table).then_inc(back, 16)
                sp.wait_ge(back, 16)

            @block.gpsimd
            def _(pool):
                pool.memset(before[:], 0.0).then_inc(consts, 1)
                pool.wait_ge(consts, 1)
                pool.affine_select(out=before[:], in_=before[:], compare_op=ALU.is_gt, fill=-1.0, base=0,
                                   pattern=[[1, P]], channel_multiplier=-1).then_inc(consts, 1)
                pool.memset(ones_b[:], 1.0).then_inc(consts, 1)
                pool.iota(iota_t[:], pattern=[[1, T]], base=0, channel_multiplier=0,
                          allow_small_or_imprecise_dtypes=True).then_inc(consts, 1)
                pool.iota(ids[:], pattern=[[2 * P, NB], [1, 2]], base=0, channel_multiplier=2).then_inc(consts, 1)
                pool.iota(pad[:], pattern=[[1, T]], base=2 * N, channel_multiplier=T).then_inc(consts, 1)
                pool.wait_ge(padded, 32)
                pool.wait_ge(addressed, 1)
                flat = ids[:].rearrange("p t j -> p (t j)")
                for c in range(PC):
                    pool.indirect_dma_start(
                        out=S.picks, out_offset=bass.IndirectOffsetOnAxis(ap=addr[:, c:c + 1], axis=0),
                        in_=flat[:, c:c + 1], in_offset=None).then_inc(written, 16)

            @block.tensor
            def _(pe):
                pe.wait_ge(counted, 1)
                pe.wait_ge(consts, 6)
                pe.matmul(S.ps[:, 4, 0:NE3], ones_p[:], count[:], start=True, stop=True).then_inc(ranks, 1)
                for a in range(2):
                    rhs = onehot[:, a * HALF:(a + 1) * HALF, :].rearrange("p e c -> p (e c)")
                    pe.matmul(S.ps[0:P, a, 0:HALF * PC], ones_b[:], rhs, start=True, stop=True)
                    pe.matmul(S.ps[0:P, 2 + a, 0:HALF * PC], before[:], rhs, start=True, stop=True).then_inc(ranks, 1)

            @block.vector
            def _(dve):
                ch = Chain(dve, dve_step)
                ch.step(dve.memset(ones_p[:], 1.0))
                ch.step(dve.memset(one_c[:], 1.0))
                for e in range(NE3):
                    ch.step(dve.tensor_scalar(onehot[:, e, :], key, float(e), None, ALU.is_equal))
                ch.sync()
                ch.link(dve.tensor_reduce(count[:], onehot[:], AX, ALU.add))
                dve.sem_inc(counted, 1)
                dve.wait_ge(ranks, 3)
                ch.link(dve.tensor_scalar(tiles_i[:], S.ps[:, 4, 0:NE3], 127.0, None, ALU.add))
                ch.link(dve.tensor_scalar(tiles_i[:], tiles_i[:], 7, None, ALU.arith_shift_right))
                ch.link(dve.tensor_copy(tiles[:], tiles_i[:]))
                ch.link(dve.tensor_tensor_scan(upto[0:P], one_c[:, 0:NE3], tiles[0:P], 0.0, ALU.mult, ALU.add))
                ch.link(dve.tensor_tensor(start[0:P], upto[0:P], tiles[0:P], ALU.subtract))
                ch.link(dve.tensor_scalar(slot0[0:P], start[0:P], 128.0, None, ALU.mult))
                ch.link(dve.tensor_scalar(blk[0:P], iota_t[0:P], start[0:P, 1:2], None, ALU.is_ge))
                for e in range(2, NE3):
                    ch.link(dve.scalar_tensor_tensor(blk[0:P], iota_t[0:P], start[0:P, e:e + 1], blk[0:P],
                                                     ALU.is_ge, ALU.add))
                ch.step(dve.tensor_copy(expert_of[:], blk[0:1, :]))
                for e in range(NE3):
                    at = (e % HALF) * PC
                    ch.step(dve.tensor_tensor_scan(cum[:, e, :], one_c[:], S.ps[0:P, e // HALF, at:at + PC],
                                                   slot0[0:P, e:e + 1], ALU.mult, ALU.add))
                ch.sync()
                for a in range(2):
                    v = cum[:, a * HALF:(a + 1) * HALF, :].rearrange("p e c -> p (e c)")
                    ch.step(dve.tensor_tensor(v, v, S.ps[0:P, 2 + a, 0:HALF * PC], ALU.add))
                ch.sync()
                ch.link(dve.tensor_tensor(cum[:], cum[:], onehot[:], ALU.mult))
                ch.link(dve.tensor_reduce(pos[:], cum[:].rearrange("p e c -> p c e"), AX, ALU.add))
                ch.link(dve.tensor_copy(hi_i[:], pos[:]))
                ch.link(dve.tensor_scalar(hi_i[:], hi_i[:], 7, None, ALU.arith_shift_right))
                ch.link(dve.tensor_copy(hi[:], hi_i[:]))
                ch.link(dve.scalar_tensor_tensor(pos[:], hi[:], -128.0, pos[:], ALU.mult, ALU.add))
                ch.link(dve.scalar_tensor_tensor(addr[:], pos[:], float(T), hi[:], ALU.mult, ALU.add))
                dve.sem_inc(addressed, 1)
                dve.wait_ge(back, 16)
                ch.link(dve.tensor_scalar(half_i[:], pick_of[:], 1, None, ALU.arith_shift_right))
                ch.link(dve.tensor_copy(half[:], half_i[:]))
                ch.link(dve.tensor_scalar(node_of[:], half[:], float(N - 1), None, ALU.min))


def picked_experts(nc, S, A, expert_of, node_of, pick_of):
    F = 512
    KF = F // 128
    first_bias = S.column["L3_ffn_b1"]
    with phase(nc, "mlp") as (sb, sem):
        gi, si = sb("gi", [128, U, 1], I32), sb("si", [128, U, 1], I32)
        rows, rows_t = sb("rows", [128, U, D]), sb("rows_t", [128, U, K, 128])
        w1, w2 = sb("w1", [128, U, K, F]), sb("w2", [128, U, KF, D])
        hid, bias, y = sb("hid", [128, U, KF, 128]), sb("bias", [128, U, KF]), sb("y", [128, U, D])
        loaded, gathered, stored = ([sem(f"{x}{u}") for u in range(U)] for x in ("loaded", "gathered", "stored"))
        to_gather, to_store, go, turned, turned_out, bias_in, first, hidden, second, evacuated = (
            sem(x) for x in ("to_gather", "to_store", "go", "turned", "turned_out", "bias_in", "first", "hidden",
                             "second", "evacuated"))

        def expert(eng, q):
            return eng.value_load(expert_of[0:1, bass.ds(q.n, 1)], min_val=0, max_val=NE3 - 1)

        def run(eng, *stages):
            pipeline(eng, *stages, groups=PICK_TILES)

        with nc.Block() as block:
            @block.sync
            def _(sp):
                def load(q):
                    e = expert(sp, q)
                    if q.since(U):
                        sp.wait_ge(second, q.n - U + 1)
                    for dst, w in ((w1, A["L3_ffn_w1"]), (w2, A["L3_ffn_w2"])):
                        sp.dma_start(dst[:, q.slot], by_expert(w)(e)).then_inc(loaded[q.slot], 16)
                run(sp, (0, load))

            @block.gpsimd
            def _(pool):
                def gather(q):
                    if q.since(U):
                        pool.wait_ge(turned, q.n - U + 1)
                    pool.tensor_copy(gi[:, q.slot], node_of[:, bass.ds(q.n, 1)]).then_inc(to_gather, 1)
                    pool.wait_ge(to_gather, q.n + 1)
                    pool.sem_inc(go, 1)
                    pool.indirect_dma_start(
                        out=rows[:, q.slot, :], out_offset=None, in_=S.rows_b,
                        in_offset=bass.IndirectOffsetOnAxis(ap=gi[:, q.slot, 0:1], axis=0)).then_inc(gathered[q.slot], 16)

                def store(q):
                    pool.wait_ge(evacuated, q.n + 1)
                    pool.tensor_copy(si[:, q.slot], pick_of[:, bass.ds(q.n, 1)]).then_inc(to_store, 1)
                    pool.wait_ge(to_store, q.n + 1)
                    pool.sem_inc(go, 1)
                    pool.indirect_dma_start(
                        out=S.choices, out_offset=bass.IndirectOffsetOnAxis(ap=si[:, q.slot, 0:1], axis=0),
                        in_=y[:, q.slot, :], in_offset=None).then_inc(stored[q.slot], 16)

                run(pool, (0, gather), (3, store))
                for u in range(U):
                    pool.wait_ge(stored[u], PICK_TILES // U * 16)

            @block.tensor
            def _(pe):
                def turn_rows(q):
                    pe.wait_ge(gathered[q.slot], (q.turn + 1) * 16)
                    if q.since(2):
                        pe.wait_ge(turned_out, q.n - 1)
                    for k in range(K):
                        ins = pe.transpose(S.ps[:, q.slot % 2, k * 128:(k + 1) * 128],
                                           rows[:, q.slot, k * 128:(k + 1) * 128], S.ident[:])
                    ins.then_inc(turned, 1)

                def product_1(q):
                    pe.wait_ge(loaded[q.slot], (q.turn + 1) * 32)
                    pe.wait_ge(turned_out, q.n + 1)
                    if q.since(2):
                        pe.wait_ge(hidden, (q.n - 1) * KF)
                    for f in range(KF):
                        for k in range(K):
                            ins = pe.matmul(S.ps[:, 2 + q.slot % 2, f * 128:(f + 1) * 128],
                                            w1[:, q.slot, k, f * 128:(f + 1) * 128], rows_t[:, q.slot, k, :],
                                            start=k == 0, stop=k == K - 1)
                    ins.then_inc(first, 1)

                def product_2(q):
                    pe.wait_ge(hidden, (q.n + 1) * KF)
                    if q.since(2):
                        pe.wait_ge(evacuated, q.n - 1)
                    for k in range(KF):
                        ins = pe.matmul(S.ps[:, 4 + q.slot % 2, 0:D], hid[:, q.slot, k, :], w2[:, q.slot, k, :],
                                        start=k == 0, stop=k == KF - 1)
                    ins.then_inc(second, 1)

                run(pe, (0, turn_rows), (1, product_1), (2, product_2))

            @block.scalar
            def _(act):
                def turn_out(q):
                    act.wait_ge(turned, q.n + 1)
                    act.copy(rows_t[:, q.slot],
                             S.ps[:, q.slot % 2, 0:K * 128].rearrange("p (k n) -> p k n", k=K)).then_inc(turned_out, 1)

                def rectify(q):
                    act.wait_ge(bias_in, q.n + 1)
                    act.wait_ge(first, q.n + 1)
                    if q.since(U):
                        act.wait_ge(second, q.n - U + 1)
                    for f in range(KF):
                        act.activation(hid[:, q.slot, f, :], S.ps[:, 2 + q.slot % 2, f * 128:(f + 1) * 128], ACT.Relu,
                                       bias=bias[:, q.slot, f:f + 1]).then_inc(hidden, 1)

                run(act, (0, turn_out), (1, rectify))

            @block.vector
            def _(dve):
                def fetch(q):
                    e = expert(dve, q)
                    if q.since(U):
                        dve.wait_ge(hidden, (q.n - U + 1) * KF)
                    dve.tensor_copy(bias[:, q.slot, :],
                                    S.pcol[:, bass.ds(e * KF + first_bias, KF)]).then_inc(bias_in, 1)

                def evacuate(q):
                    dve.wait_ge(second, q.n + 1)
                    if q.since(U):
                        dve.wait_ge(stored[q.slot], q.turn * 16)
                    dve.tensor_copy(y[:, q.slot, :], S.ps[:, 4 + q.slot % 2, 0:D]).then_inc(evacuated, 1)

                run(dve, (0, fetch), (2, evacuate))


def ffn3(nc, S, A, out):
    n = NE3
    with phase(nc, "ffn3") as (sb, sem):
        comb, comb_t = sb("comb", [P, NB, n]), sb("comb_t", [n, N])
        at_f, pair = sb("experts_of", [P, NB, 2]), sb("weights_of", [P, NB, 2])
        expert_weights(nc, S, A, "route3", n, "gates", A["L3_ffn_gate_w"], A["L3_ffn_gate_b"], comb, comb_t,
                       b2=A["L3_ffn_b2"], target=S.acc[:, :, 0:D], picked=(at_f, pair))
        expert_of = sb("expert_of", [1, PICK_TILES], I32)
        node_of, pick_of = sb("node_of", [128, PICK_TILES], I32), sb("pick_of", [128, PICK_TILES], I32)
        sort_picks(nc, S, at_f[:].rearrange("p t j -> p (t j)"), expert_of, node_of, pick_of)
        picked_experts(nc, S, A, expert_of, node_of, pick_of)
        with phase(nc, "weigh") as (sb2, sem2):
            z = sb2("z", [P, NB, 2, D])
            loaded, weighed = sem2("loaded"), sem2("weighed")
            with nc.Block() as block:
                @block.sync
                def _(sp):
                    sp.dma_start(z[:], S.choices[0:2 * N, :].rearrange("(t p j) c -> p t j c", p=P, j=2))\
                      .then_inc(loaded, 16)
                    sp.wait_ge(loaded, 16)

                @block.vector
                def _(dve):
                    dve.wait_ge(loaded, 16)
                    for j in range(2):
                        if j:
                            dve.wait_ge(weighed, NB)
                        for t in range(NB):
                            dve.scalar_tensor_tensor(S.acc[:, t, 0:D], z[:, t, j, :], pair[:, t, j:j + 1],
                                                     S.acc[:, t, 0:D], ALU.mult, ALU.add).then_inc(weighed, 1)
                    dve.wait_ge(weighed, 2 * NB)
    with phase(nc, "final") as (sb, sem):
        stats, mv = sb("stats", [P, NB, 6]), sb("mv", [P, NB, 2])
        var, root, inv = sb("var", [P, NB]), sb("root", [P, NB]), sb("inv", [P, NB])
        gamma, beta = sb("gamma", [P, D]), sb("beta", [P, D])
        loaded, dve_step, var_ready, root_ready, finished, stored = (
            sem(x) for x in ("loaded", "dve_step", "var_ready", "root_ready", "finished", "stored"))
        with nc.Block() as block:
            @block.sync
            def _(sp):
                sp.dma_start(gamma[:], row(A["L3_ffn_gamma"])).then_inc(loaded, 16)
                sp.dma_start(beta[:], row(A["L3_ffn_beta"])).then_inc(loaded, 16)
                sp.wait_ge(finished, 1)
                sp.dma_start(out.rearrange("(t p) c -> p t c", p=P), S.x[:]).then_inc(stored, 16)
                sp.wait_ge(stored, 16)

            @block.scalar
            def _(act):
                act.wait_ge(var_ready, 1)
                act.activation(root[:], var[:], ACT.Sqrt).then_inc(root_ready, 1)

            @block.vector
            def _(dve):
                ch = Chain(dve, dve_step)
                y = S.acc[:, :, 0:D]
                ch.link(dve.tensor_tensor(y, y, S.xn[:], ALU.add))
                norm_into(ch, dve, S, y, stats, mv, var, root, inv, var_ready, root_ready)
                dve.wait_ge(loaded, 32)
                ch.link(dve.tensor_tensor(y, y, bc_mid(gamma[:], NB), ALU.mult))
                ch.link(dve.tensor_tensor(S.x[:], S.x[:], bc_mid(beta[:], NB), ALU.add))
                ch.link(dve.tensor_tensor(S.x[:], S.x[:], y, ALU.add))
                dve.sem_inc(finished, 1)


def plan(nc, S, A, out):
    return [
        lambda: setup(nc, S, A),
        lambda: sort_edges(nc, S, A, "dst"),
        lambda: layer_norm(nc, S, "ln0"),
        lambda: gat(nc, S, A),
        lambda: layer_norm(nc, S, "ln1"),
        lambda: ffn0(nc, S, A),
        lambda: layer_norm(nc, S, "ln2"),
        lambda: mpnn(nc, S, A),
        lambda: layer_norm(nc, S, "ln3"),
        lambda: ffn1(nc, S, A),
        lambda: layer_norm(nc, S, "ln4"),
        lambda: hyperbolic(nc, S, A),
        lambda: layer_norm(nc, S, "ln5"),
        lambda: ffn2(nc, S, A),
        lambda: layer_norm(nc, S, "ln6"),
        lambda: hypergraph(nc, S, A),
        lambda: layer_norm(nc, S, "ln7"),
        lambda: ffn3(nc, S, A, out),
    ]


def build(nc, A, out):
    S = Shared()
    with ExitStack() as ctx:
        def sb(name, shape, dt=F32):
            return ctx.enter_context(nc.sbuf_tensor(name, shape, dt))

        def dram(name, shape, dt=F32):
            return nc.dram_tensor(name, shape, dt, kind="Internal").ap()

        S.x, S.xn = sb("x", [P, NB, D]), sb("xn", [P, NB, D])
        S.acc = sb("acc", [P, NB, XG])
        S.xT = sb("xT", [128, K, N])
        S.ident, S.iota, S.ident_b = sb("ident", [128, 128]), sb("iota", [128, 128]), sb("ident_b", [128, 128], BF16)
        S.pcol = sb("pcol", [128, place_vectors()[1] * 128])
        S.end = {k: sb(f"end_{k}", [128, NT], I32) for k in ("dst", "src")}
        S.local = {k: sb(f"local_{k}", [128, NT]) for k in ("dst", "src")}
        S.blk = {k: sb(f"blk_{k}", [1, NT], I32) for k in ("dst", "src")}
        S.edge_w = sb("edge_w", [128, NT])
        S.ps = ctx.enter_context(nc.psum_tensor("ps", [128, 8, 512], F32))
        S.turned = {n: dram(f"turned_{n}", (c, r)) for n, r, c in TURNED}
        S.records = {"dst": dram("records_dst", (SLOTS, 3)), "src": dram("records_src", (SLOTS, 2 + ED))}
        S.rows = dram("rows", (N, XG))
        S.picks = dram("picks", (PICK_TILES * 128, 1), I32)
        S.choices = dram("choices", (2 * N + PICK_TILES * 128, D))
        S.rows8 = dram("rows8", (N, HEADS))
        S.rows_b = dram("rows_b", (N, D))
        S.rows_c = dram("rows_c", (N, D + 1))
        for step in plan(nc, S, A, out):
            step()


def kernel(**inputs):
    import numpy as np
    import concourse.bacc as bacc
    from concourse.bass_utils import run_bass_kernel_spmd

    nc = bacc.Bacc("TRN2", target_bir_lowering=False, num_devices=1)
    arrays, A = {}, {}
    for name, value in inputs.items():
        a = np.ascontiguousarray(value)
        arrays[f"in_{name}"] = a
        A[name] = nc.dram_tensor(f"in_{name}", a.shape, mybir.dt.from_np(a.dtype), kind="ExternalInput").ap()
    out = nc.dram_tensor("out_x", (N, D), F32, kind="ExternalOutput").ap()
    build(nc, A, out)
    return run_bass_kernel_spmd(nc, [arrays], core_ids=[0]).results[0]["out_x"]
```
